# Optimizing a Trainium2 kernel written in Bass

```python
import numpy as np
import jax
import jax.numpy as jnp

def _softmax(x, axis=-1):
    return jax.nn.softmax(x, axis=axis)

def _gelu(x):
    return jax.nn.gelu(x, approximate=True)

def _silu(x):
    return jax.nn.silu(x)

def _sigmoid(x):
    return jax.nn.sigmoid(x)

def _layernorm(x, axis=-1, eps=1e-05):
    m = jnp.mean(x, axis=axis, keepdims=True)
    v = jnp.var(x, axis=axis, keepdims=True)
    return (x - m) / jnp.sqrt(v + eps)

def _scatter_add(tgt, idx, src, axis=0):
    return tgt.at[idx].add(src)

def _segment_sum(src, seg, n):
    return jax.ops.segment_sum(src, seg, n)
kernel_name = 'mk_seq_postln_d2_jaxref_r4_bd9245'

def setup_inputs(seed: int=0):
    np.random.seed(seed)
    _w = jnp.asarray

    def _L0_attn_setup():
        import jax, jax.numpy as jnp
        import numpy as np
        E2M1_GRID = jnp.array([0.0, 0.5, 1.0, 1.5, 2.0, 3.0, 4.0, 6.0], dtype=jnp.float32)
        E2M1_MIDS = (E2M1_GRID[1:] + E2M1_GRID[:-1]) / 2.0
        FP4_MAX = 6.0
        FP8_E4M3_MAX = 448.0

        def nvfp4_quant_dequant(w):
            O, I = w.shape
            w16 = w.reshape(O, I // 128, 8, 16)
            amax128 = jnp.max(jnp.abs(w16), axis=(-2, -1))
            outer = amax128 / (FP4_MAX * FP8_E4M3_MAX)
            outer = jnp.where(outer > 0, outer, 1.0)
            amax16 = jnp.max(jnp.abs(w16), axis=-1)
            inner = amax16 / FP4_MAX / outer[..., None]
            inner = inner.astype(jnp.float8_e4m3fn).astype(jnp.float32)
            scale = outer[..., None] * inner
            safe = jnp.where(scale > 0, scale, 1.0)[..., None]
            code = w16 / safe
            a = jnp.abs(code)
            idx = jnp.searchsorted(E2M1_MIDS, a)
            q = E2M1_GRID[idx] * jnp.sign(code)
            return (q * scale[..., None]).reshape(O, I)
        key = jax.random.key(seed)
        k0, k1, k2 = jax.random.split(key, 3)
        B, S, H = (2, 512, 512)
        hidden_states = jax.random.normal(k0, (B, S, H), dtype=jnp.float32)
        w_qkv = jax.random.normal(k1, (3 * H, H), dtype=jnp.float32) * 0.023
        w_o = jax.random.normal(k2, (H, H), dtype=jnp.float32) * 0.023
        w_qkv = nvfp4_quant_dequant(w_qkv)
        w_o = nvfp4_quant_dequant(w_o)
        return {'hidden_states': hidden_states, 'w_qkv': w_qkv, 'w_o': w_o}
    _L0_attn_in = _L0_attn_setup()

    def _L0_ffn_setup():
        import jax, jax.numpy as jnp
        import numpy as np

        def _sparsify_2to4(h):
            B, S, I = h.shape
            g = h.reshape(B, S, I // 4, 4)
            a = jnp.abs(g)
            _, idx = jax.lax.top_k(a, 2)
            pos = jnp.arange(4)
            mask = (pos == idx[..., 0:1]) | (pos == idx[..., 1:2])
            return (g * mask.astype(g.dtype)).reshape(B, S, I)
        key = jax.random.key(seed)
        k1, k2, k3, k4 = jax.random.split(key, 4)
        B, S, H, I = (4, 512, 512, 2048)
        x = jax.random.normal(k1, (B, S, H), dtype=jnp.float32)
        w_gate = jax.random.normal(k2, (H, I), dtype=jnp.float32) / np.sqrt(H)
        w_up = jax.random.normal(k3, (H, I), dtype=jnp.float32) / np.sqrt(H)
        w_down = jax.random.normal(k4, (I, H), dtype=jnp.float32) / np.sqrt(I)
        return {'x': x, 'w_gate': w_gate, 'w_up': w_up, 'w_down': w_down}
    _L0_ffn_in = _L0_ffn_setup()

    def _L1_attn_setup():
        import jax, jax.numpy as jnp
        import numpy as np
        HIDDEN = 512
        N_HEADS = 16
        HEAD_DIM = HIDDEN // N_HEADS
        ROTARY_DIM = 32
        ROPE_BASE = 10000.0
        NEG_INF = -10000.0

        def _rope_cos_sin(seqlen, dtype):
            inv_freq = 1.0 / ROPE_BASE ** (jnp.arange(0, ROTARY_DIM, 2, dtype=jnp.float32) / ROTARY_DIM)
            t = jnp.arange(seqlen, dtype=jnp.float32)
            freqs = jnp.outer(t, inv_freq)
            return (jnp.cos(freqs).astype(dtype), jnp.sin(freqs).astype(dtype))

        def _apply_rotary(u, cos, sin):
            u_rot, u_pass = (u[..., :ROTARY_DIM], u[..., ROTARY_DIM:])
            u1, u2 = (u_rot[..., :ROTARY_DIM // 2], u_rot[..., ROTARY_DIM // 2:])
            c = cos[None, :, None, :]
            s = sin[None, :, None, :]
            rot = jnp.concatenate([u1 * c - u2 * s, u1 * s + u2 * c], axis=-1)
            return jnp.concatenate([rot, u_pass], axis=-1)
        key = jax.random.key(seed)
        k1, k2, k3 = jax.random.split(key, 3)
        x = jax.random.normal(k1, (2, 512, HIDDEN), dtype=jnp.float32)
        Wqkv_w = jax.random.normal(k2, (3 * HIDDEN, HIDDEN), dtype=jnp.float32) * (1.0 / np.sqrt(HIDDEN))
        Wqkv_b = jax.random.normal(k3, (3 * HIDDEN,), dtype=jnp.float32) * 0.01
        return {'x': x, 'Wqkv_w': Wqkv_w, 'Wqkv_b': Wqkv_b}
    _L1_attn_in = _L1_attn_setup()

    def _L1_ffn_setup():
        import jax, jax.numpy as jnp
        import numpy as np
        NUM_EXPERTS = 16
        C = 1.0
        key = jax.random.key(seed)
        k1, k2, k3 = jax.random.split(key, 3)
        b, s, h = (4, 512, 512)
        return {'x': jax.random.normal(k1, (b, s, h), dtype=jnp.float32), 'router_w': jax.random.normal(k2, (h, NUM_EXPERTS), dtype=jnp.float32) * 0.02, 'router_b': jnp.zeros((NUM_EXPERTS,), dtype=jnp.float32), 'expert_w': jax.random.normal(k3, (h, h), dtype=jnp.float32) * 0.02, 'expert_b': jnp.zeros((h,), dtype=jnp.float32)}
    _L1_ffn_in = _L1_ffn_setup()
    _d = {'L0_attn_hidden_states': _L0_attn_in['hidden_states'], 'L0_attn_w_qkv': _L0_attn_in['w_qkv'], 'L0_attn_w_o': _L0_attn_in['w_o'], 'L0_ffn_w_gate': _L0_ffn_in['w_gate'], 'L0_ffn_w_up': _L0_ffn_in['w_up'], 'L0_ffn_w_down': _L0_ffn_in['w_down'], 'L1_attn_Wqkv_w': _L1_attn_in['Wqkv_w'], 'L1_attn_Wqkv_b': _L1_attn_in['Wqkv_b'], 'L1_ffn_router_w': _L1_ffn_in['router_w'], 'L1_ffn_router_b': _L1_ffn_in['router_b'], 'L1_ffn_expert_w': _L1_ffn_in['expert_w'], 'L1_ffn_expert_b': _L1_ffn_in['expert_b']}
    _x0 = _d['L0_attn_hidden_states']
    _d['L0_attn_hidden_states'] = jax.random.normal(jax.random.fold_in(jax.random.key(seed), 1), (4, 1024, 512), dtype=_x0.dtype)
    del _x0
    return _d

def reference(L0_attn_hidden_states, L0_attn_w_qkv, L0_attn_w_o, L0_ffn_w_gate, L0_ffn_w_up, L0_ffn_w_down, L1_attn_Wqkv_w, L1_attn_Wqkv_b, L1_ffn_router_w, L1_ffn_router_b, L1_ffn_expert_w, L1_ffn_expert_b):

    def _L0_attn_ref(hidden_states, w_qkv, w_o):
        import jax, jax.numpy as jnp
        import numpy as np
        E2M1_GRID = jnp.array([0.0, 0.5, 1.0, 1.5, 2.0, 3.0, 4.0, 6.0], dtype=jnp.float32)
        E2M1_MIDS = (E2M1_GRID[1:] + E2M1_GRID[:-1]) / 2.0
        FP4_MAX = 6.0
        FP8_E4M3_MAX = 448.0

        def nvfp4_quant_dequant(w):
            O, I = w.shape
            w16 = w.reshape(O, I // 128, 8, 16)
            amax128 = jnp.max(jnp.abs(w16), axis=(-2, -1))
            outer = amax128 / (FP4_MAX * FP8_E4M3_MAX)
            outer = jnp.where(outer > 0, outer, 1.0)
            amax16 = jnp.max(jnp.abs(w16), axis=-1)
            inner = amax16 / FP4_MAX / outer[..., None]
            inner = inner.astype(jnp.float8_e4m3fn).astype(jnp.float32)
            scale = outer[..., None] * inner
            safe = jnp.where(scale > 0, scale, 1.0)[..., None]
            code = w16 / safe
            a = jnp.abs(code)
            idx = jnp.searchsorted(E2M1_MIDS, a)
            q = E2M1_GRID[idx] * jnp.sign(code)
            return (q * scale[..., None]).reshape(O, I)
        B, S, H = hidden_states.shape
        num_heads = 16
        head_dim = H // num_heads
        qkv = jnp.einsum('bsh,oh->bso', hidden_states, w_qkv)
        qkv = qkv.reshape(B, S, 3, num_heads, head_dim)
        qkv = jnp.transpose(qkv, (2, 0, 3, 1, 4))
        q, k, v = (qkv[0], qkv[1], qkv[2])
        scale = 1.0 / jnp.sqrt(jnp.float32(head_dim))
        scores = jnp.einsum('bhqd,bhkd->bhqk', q, k) * scale
        causal = jnp.tril(jnp.ones((S, S), dtype=bool))
        scores = jnp.where(causal, scores, jnp.finfo(scores.dtype).min)
        probs = jax.nn.softmax(scores, axis=-1)
        attn = jnp.einsum('bhqk,bhkd->bhqd', probs, v)
        attn = jnp.transpose(attn, (0, 2, 1, 3)).reshape(B, S, H)
        return jnp.einsum('bsh,oh->bso', attn, w_o)

    def _L0_ffn_ref(x, w_gate, w_up, w_down):
        import jax, jax.numpy as jnp
        import numpy as np

        def _sparsify_2to4(h):
            B, S, I = h.shape
            g = h.reshape(B, S, I // 4, 4)
            a = jnp.abs(g)
            _, idx = jax.lax.top_k(a, 2)
            pos = jnp.arange(4)
            mask = (pos == idx[..., 0:1]) | (pos == idx[..., 1:2])
            return (g * mask.astype(g.dtype)).reshape(B, S, I)
        h = jax.nn.silu(jnp.einsum('bsh,hi->bsi', x, w_gate)) * jnp.einsum('bsh,hi->bsi', x, w_up)
        h_sparse = _sparsify_2to4(h)
        return jnp.einsum('bsi,ih->bsh', h_sparse, w_down)

    def _L1_attn_ref(x, Wqkv_w, Wqkv_b):
        import jax, jax.numpy as jnp
        import numpy as np
        HIDDEN = 512
        N_HEADS = 16
        HEAD_DIM = HIDDEN // N_HEADS
        ROTARY_DIM = 32
        ROPE_BASE = 10000.0
        NEG_INF = -10000.0

        def _rope_cos_sin(seqlen, dtype):
            inv_freq = 1.0 / ROPE_BASE ** (jnp.arange(0, ROTARY_DIM, 2, dtype=jnp.float32) / ROTARY_DIM)
            t = jnp.arange(seqlen, dtype=jnp.float32)
            freqs = jnp.outer(t, inv_freq)
            return (jnp.cos(freqs).astype(dtype), jnp.sin(freqs).astype(dtype))

        def _apply_rotary(u, cos, sin):
            u_rot, u_pass = (u[..., :ROTARY_DIM], u[..., ROTARY_DIM:])
            u1, u2 = (u_rot[..., :ROTARY_DIM // 2], u_rot[..., ROTARY_DIM // 2:])
            c = cos[None, :, None, :]
            s = sin[None, :, None, :]
            rot = jnp.concatenate([u1 * c - u2 * s, u1 * s + u2 * c], axis=-1)
            return jnp.concatenate([rot, u_pass], axis=-1)
        B, S, _ = x.shape
        qkv = jnp.einsum('bse,oe->bso', x, Wqkv_w) + Wqkv_b
        qkv = qkv.reshape(B, S, 3, N_HEADS, HEAD_DIM)
        cos, sin = _rope_cos_sin(S, x.dtype)
        q = _apply_rotary(qkv[:, :, 0], cos, sin)
        k = _apply_rotary(qkv[:, :, 1], cos, sin)
        v = qkv[:, :, 2]
        scale = 1.0 / np.sqrt(HEAD_DIM)
        scores = jnp.einsum('bthd,bshd->bhts', q, k * scale)
        causal_mask = jnp.triu(jnp.full((S, S), NEG_INF, dtype=scores.dtype), 1)
        scores = scores + causal_mask
        attn = jax.nn.softmax(scores, axis=-1)
        out = jnp.einsum('bhts,bshd->bthd', attn, v)
        return out.reshape(B, S, N_HEADS * HEAD_DIM)

    def _L1_ffn_ref(x, router_w, router_b, expert_w, expert_b):
        import jax, jax.numpy as jnp
        import numpy as np
        NUM_EXPERTS = 16
        C = 1.0
        b, s, h = x.shape
        bs = b * s
        k = min(int(bs * C / NUM_EXPERTS), bs)
        xf = x.reshape(bs, h)
        logits = xf @ router_w + router_b
        S = jax.nn.softmax(logits, axis=-1)
        G, idx = jax.lax.top_k(S.T, k)
        tokens = xf[idx]
        out = jnp.einsum('ekh,hd->ekd', tokens, expert_w) + expert_b
        weighted = G[..., None] * out
        y = jnp.zeros((bs, h), dtype=x.dtype).at[idx.reshape(-1)].add(weighted.reshape(-1, h))
        return y.reshape(b, s, h)
    x = L0_attn_hidden_states
    x = _layernorm(x + _L0_attn_ref(x, L0_attn_w_qkv, L0_attn_w_o), axis=-1)
    x = _layernorm(x + _L0_ffn_ref(x, L0_ffn_w_gate, L0_ffn_w_up, L0_ffn_w_down), axis=-1)
    x = _layernorm(x + _L1_attn_ref(x, L1_attn_Wqkv_w, L1_attn_Wqkv_b), axis=-1)
    x = _layernorm(x + _L1_ffn_ref(x, L1_ffn_router_w, L1_ffn_router_b, L1_ffn_expert_w, L1_ffn_expert_b), axis=-1)
    return x

_drawn_inputs = setup_inputs


def setup_inputs(seed=0):
    import zlib

    import numpy as np

    out = dict(_drawn_inputs(seed))
    spreads = {'L1_ffn_router_b': (0.0, 0.728), 'L1_ffn_expert_b': (0.0, 0.491)}
    factors = {'L1_attn_Wqkv_b': 5.418}
    for name, (base, spread) in spreads.items():
        noise = np.random.default_rng([zlib.crc32(name.encode()), seed]).standard_normal(out[name].shape)
        drawn = base * np.exp(spread * noise) if base else spread * noise
        out[name] = jnp.asarray(drawn.astype(out[name].dtype))
    for name, factor in factors.items():
        out[name] = (out[name] * factor).astype(out[name].dtype)
    return out
```

```python
from contextlib import ExitStack

import concourse.bass as bass
from concourse import mybir

F32 = mybir.dt.float32
F32R = mybir.dt.float32r
BF16 = mybir.dt.bfloat16
I32 = mybir.dt.int32
ALU = mybir.AluOpType
ACT = mybir.ActivationFunctionType
AX = mybir.AxisListType

P = 128
B, S, H = 4, 1024, 512
T = B * S
NH, HD = 16, 32
KT = H // P
TT = S // P
G = NH * HD // P
HG = P // HD
FFN = 2048
NE = 16
TOPK = T // NE
EPS = 1e-5
SCALE = float(HD) ** -0.5
TERMS = ((0, 0), (0, 1), (1, 0))
SWAP_HALVES = [(i + 16) % 32 for i in range(32)]


def hold(eng, sem, value, passed):
    eng.wait_ge(sem, value)
    eng.sem_inc(passed, 1)


class Tail:

    def __init__(self, nc, ctx, name, res, y, xn, xTs, psum_slots, consts, x_out, xT_out):
        def sem(n):
            return consts.semaphore(f"{name}_{n}")

        def sb(n, shape):
            return ctx.enter_context(nc.sbuf_tensor(f"{name}_{n}", shape, F32))

        self.nc, self.psT, self.c = nc, psum_slots, consts
        self.x_out = x_out.rearrange("(b t p) n -> b t p n", b=B, p=P)
        self.xT_out = xT_out.rearrange("(k p) (b t c) -> b t p k c", p=P, b=B, c=P) if xT_out is not None else None
        self.res, self.y, self.xn, self.xTs = res, y, xn, xTs
        self.stats = sb("stats", [P, 2, 6])
        self.mv = sb("mv", [P, 2, 2])
        self.vare = sb("vare", [P, 2])
        self.rstd = sb("rstd", [P, 2])
        self.res_in = [sem(f"res_in{i}") for i in (0, 1)]
        self.y_sum = sem("y_sum")
        self.y_stats = sem("y_stats")
        self.y_mv = sem("y_mv")
        self.y_vare = sem("y_vare")
        self.y_rstd = sem("y_rstd")
        self.xn_done = sem("xn_done")
        self.xT_psum = sem("xT_psum")
        self.xT_done = sem("xT_done")
        self.passed = [sem(f"passed_{e}") for e in ("sp", "pool", "dve")]
        self.out_x = [sem(f"out_x{i}") for i in (0, 1)]
        self.out_xT = [sem(f"out_xT{i}") for i in (0, 1)]

    def load_res(self, sp, b, tt, x_in):
        if tt >= 2:
            sp.wait_ge(self.y_sum, b * TT + tt - 1)
        sp.dma_start(self.res[tt % 2], x_in[b, tt]).then_inc(self.res_in[tt % 2], 16)

    def store(self, sp, b, tt):
        sp.wait_ge(self.xn_done, b * TT + tt + 1)
        sp.dma_start(self.x_out[b, tt], self.xn[tt % 2]).then_inc(self.out_x[tt % 2], 16)
        if self.xT_out is not None:
            sp.wait_ge(self.xT_done, b * TT + tt + 1)
            sp.dma_start(self.xT_out[b, tt], self.xTs[tt % 2].rearrange("p (k c) -> p k c", k=KT)).then_inc(self.out_xT[tt % 2], 16)

    @staticmethod
    def loads(b, tt):
        return (b * (TT // 2) + tt // 2 + 1) * 16

    def wait_stored(self, sp, b):
        for slot in (0, 1):
            if self.xT_out is not None:
                sp.wait_ge(self.out_xT[slot], self.loads(b, TT - 2))
            hold(sp, self.out_x[slot], self.loads(b, TT - 2), self.passed[0])

    def add_stats(self, dve, b, tt, part):
        s = tt % 2
        dve.wait_ge(self.res_in[s], self.loads(b, tt))
        dve.tensor_tensor(self.y[s], part, self.res[s], ALU.add).then_inc(self.y_sum, 1)
        dve.wait_ge(self.y_sum, b * TT + tt + 1)
        self.stats_of(dve, b, tt)

    def stats_of(self, dve, b, tt):
        s = tt % 2
        n = b * TT + tt + 1
        dve.bn_stats(self.stats[:, s, :], self.y[tt % len(self.y)]).then_inc(self.y_stats, 1)
        hold(dve, self.y_stats, n, self.passed[2])
        dve.bn_aggr(self.mv[:, s, :], self.stats[:, s, :]).then_inc(self.y_mv, 1)
        dve.wait_ge(self.y_mv, n)
        dve.tensor_scalar(self.vare[:, s:s + 1], self.mv[:, s, 1:2], EPS, None, ALU.add).then_inc(self.y_vare, 1)

    def rsqrt(self, pool, b, tt):
        s = tt % 2
        pool.wait_ge(self.y_vare, b * TT + tt + 1)
        pool.tensor_tensor(self.rstd[:, s:s + 1], self.vare[:, s:s + 1], self.c.neg_half[:, :], ALU.pow).then_inc(self.y_rstd, 1)

    def norm(self, dve, b, tt):
        s = tt % 2
        dve.wait_ge(self.y_rstd, b * TT + tt + 1)
        if tt >= 2:
            dve.wait_ge(self.out_x[s], self.loads(b, tt - 2))
            if self.xT_out is not None:
                dve.wait_ge(self.xT_psum, b * TT + tt - 1)
        dve.tensor_scalar(self.xn[s], self.y[tt % len(self.y)], self.mv[:, s, 0:1], self.rstd[:, s:s + 1],
                          ALU.subtract, ALU.mult).then_inc(self.xn_done, 1)

    def transpose(self, pe, b, tt):
        s = tt % 2
        pe.wait_ge(self.xn_done, b * TT + tt + 1)
        if tt >= 2:
            pe.wait_ge(self.xT_done, b * TT + tt - 1)
        for k in range(KT):
            last = pe.transpose(self.psT[s][:, k * P:(k + 1) * P], self.xn[s][:, k * P:(k + 1) * P], self.c.ident[:, :])
        last.then_inc(self.xT_psum, 1)

    def copy_T(self, act, b, tt):
        s = tt % 2
        act.wait_ge(self.xT_psum, b * TT + tt + 1)
        if tt >= 2:
            act.wait_ge(self.out_xT[s], self.loads(b, tt - 2))
        act.activation(self.xTs[s], self.psT[s], ACT.Copy).then_inc(self.xT_done, 1)


class Consts:

    def __init__(self, nc, ctx):
        self.nc, self.sems = nc, []
        self.semaphores = ctx.enter_context(ExitStack())
        def sb(n, shape, dt=F32):
            return ctx.enter_context(nc.sbuf_tensor(n, shape, dt))

        self.ident = sb("ident", [P, P])
        self.ident_r = sb("ident_r", [P, P], F32R)
        self.neg_half = sb("neg_half", [P, 1])
        self.ones = sb("ones", [P, HD])
        made = self.semaphore("consts_made")
        with nc.Block() as block:
            @block.gpsimd
            def _(pool):
                pool.memset(self.neg_half[:, :], -0.5)
                pool.memset(self.ones[:, :], 1.0)
                pool.memset(self.ident[:, :], 0.0).then_inc(made, 1)
                pool.wait_ge(made, 1)
                pool.affine_select(out=self.ident[:, :], in_=self.ident[:, :], compare_op=ALU.not_equal, fill=1.0,
                                   base=0, pattern=[[-1, P]], channel_multiplier=1).then_inc(made, 1)

            @block.vector
            def _(dve):
                dve.wait_ge(made, 2)
                dve.tensor_copy(self.ident_r[:, :], self.ident[:, :]).then_inc(made, 1)
        self.end_phase()

    def semaphore(self, name):
        self.sems.append(self.semaphores.enter_context(self.nc.semaphore(name)))
        return self.sems[-1]

    def end_phase(self):
        with self.nc.Block() as block:
            @block.sync
            def _(sp):
                for s in self.sems:
                    sp.sem_clear(s)
        self.semaphores.close()
        self.sems = []


def attention_phase(nc, c, L, xT_in, x_in, wqkvT, woT, bias, rope, m_scratch, x_out, xT_out):
    NEG = -1e30 if bias is None else -10000.0
    ctx = ExitStack()
    with ctx:
        def sb(n, shape, dt=F32):
            return ctx.enter_context(nc.sbuf_tensor(f"{L}_{n}", shape, dt))

        def sem(n):
            return c.semaphore(f"{L}_{n}")

        w = [sb("w_hi", [P, KT, 3 * H], F32R), sb("w_lo", [P, KT, 3 * H], F32R)]
        xs = [sb("x_hi", [P, KT, S], F32R), sb("x_lo", [P, KT, S], F32R)]
        raw = sb("raw", [P, 2, S])
        attn = sb("attn", [P, G, S])
        V = sb("V", [P, TT, H])
        q_hi, q_lo = sb("q_hi", [P, S], F32R), sb("q_lo", [P, S], F32R)
        k_hi, k_lo = raw[:, 0, :].bitcast(F32R), raw[:, 1, :].bitcast(F32R)
        QS = sb("q_stack", [97, HG, S], F32R)
        KS = sb("k_stack", [97, HG, S], F32R)
        PT = sb("PT", [P, 8, S])
        tail_buf = PT[:, 0:4, :].rearrange("p a (c n) -> p (a c) n", n=H)
        tri = sb("tri", [P, P], F32R)
        tri_f = q_lo[:, 0:P].bitcast(F32)
        nmax = sb("nmax", [P, HG * TT])
        nmax_T = sb("nmax_T", [HG * TT, P], F32R)
        if woT is not None:
            wo = sb("wo", [P, KT, H])
        if bias is not None:
            bias_qk = sb("bias_qk", [P, 2 * G])
            bias_v = sb("bias_v", [P, H])
            cosT, sinT = sb("cosT", [P, S]), sb("sinT", [P, S])
            flat, swapped = PT[:, 6, :], PT[:, 7, :]
        A = [ctx.enter_context(nc.psum_tensor(f"{L}_A{i}", [P, S], F32)) for i in range(2)]
        O = ctx.enter_context(nc.psum_tensor(f"{L}_O", [P, S], F32))
        SUM = ctx.enter_context(nc.psum_tensor(f"{L}_SUM", [P, S], F32))
        v_bank = [O[:, 0:H], O[:, H:S], SUM[:, 0:H], SUM[:, H:S]]

        w_in, w_hi_done, w_lo_done = sem("w_in"), sem("w_hi_done"), sem("w_lo_done")
        const_done, tri_made = sem("const_done"), sem("tri_made")
        x_in_raw = [sem(f"x_in_raw{i}") for i in (0, 1)]
        x_hi_done, x_lo_done = sem("x_hi_done"), sem("x_lo_done")
        v_psum, v_done = sem("v_psum"), sem("v_done")
        qk_psum, qk_hi, qk_lo = sem("qk_psum"), sem("qk_hi"), sem("qk_lo")
        r_flat, r_swap, r_cos, r_sin, r_sum = (sem(n) for n in ("r_flat", "r_swap", "r_cos", "r_sin", "r_sum"))
        stacked = sem("stacked")
        s_psum, max_done = sem("s_psum"), sem("max_done")
        mT_psum, mT_done, m_out, m_row = sem("mT_psum"), sem("mT_done"), sem("m_out"), sem("m_row")
        st_psum, exp_done, cut_done, pv_done = sem("st_psum"), sem("exp_done"), sem("cut_done"), sem("pv_done")
        inv_done, attn_done, y_psum = sem("inv_done"), sem("attn_done"), sem("y_psum")
        slots = [[tail_buf[:, 2 * i + j, :] for j in (0, 1)] for i in range(4)]
        tail = Tail(nc, ctx, f"{L}_t", *slots, [A[i][:, H:S] for i in range(2)], c, x_out, xT_out)

        x_rows = x_in.rearrange("(b t p) n -> b t p n", b=B, p=P)
        x_cols = xT_in.rearrange("(k p) (b s) -> b k p s", p=P, b=B)
        U = HG * TT
        STACKS = 6 * HG
        w_raw = PT[:, 0:6, :].rearrange("p a n -> p (a n)")
        w_flat = [t[:, :, :].rearrange("p k n -> p (k n)") for t in w]
        block = ctx.enter_context(nc.Block())

        @block.sync
        def _(sp):
            sp.dma_start(w_raw.rearrange("p (k n) -> p k n", k=KT), wqkvT.rearrange("(k p) n -> p k n", p=P)).then_inc(w_in, 16)
            if woT is not None:
                sp.dma_start(wo[:, :, :], woT.rearrange("(k p) n -> p k n", p=P)).then_inc(w_in, 16)
            if bias is not None:
                sp.dma_start(bias_qk[:, :], bias[0]).then_inc(w_in, 16)
                sp.dma_start(bias_v[:, :], bias[1].partition_broadcast(P)).then_inc(w_in, 16)
                sp.dma_start(cosT[:, :], rope[0]).then_inc(w_in, 16)
                sp.dma_start(sinT[:, :], rope[1]).then_inc(w_in, 16)
            with sp.Fori(0, B) as b:
                for k in range(KT):
                    sp.wait_ge(x_lo_done, b * KT + k + 1)
                    sp.dma_start(raw[:, k % 2, :], x_cols[b, k]).then_inc(x_in_raw[k % 2], 16)
                for g in range(G):
                    for i in range(2):
                        sp.wait_ge(qk_hi, b * 2 * G + 2 * g + i + 1)
                        sp.wait_ge(qk_lo, b * 2 * G + 2 * g + i + 1)
                        hi, lo = ((q_hi[:, :], q_lo[:, :]), (k_hi, k_lo))[i]
                        rows = ((hi, hi, lo), (hi, lo, hi))[i]
                        for n, src in enumerate(rows):
                            for j in range(HG):
                                sp.dma_start((QS, KS)[i][HD * n:HD * n + HD, j, :].bitcast(F32),
                                             src[HD * j:HD * j + HD, :].bitcast(F32)).then_inc(stacked, 16)
                    sp.wait_ge(mT_done, b * G + g + 1)
                    sp.dma_start(m_scratch, nmax_T[:, :].bitcast(F32)).then_inc(m_out, 16)
                    sp.wait_ge(m_out, (b * G + g + 1) * 16)
                    sp.dma_start(QS[96:97, :, :].bitcast(F32), m_scratch.rearrange("(o j t) c -> o j (t c)", o=1, j=HG)).then_inc(m_row, 16)
                sp.wait_ge(attn_done, b * G + G)
                for tt in range(TT + 2):
                    if tt < TT:
                        tail.load_res(sp, b, tt, x_rows)
                    if tt >= 2:
                        tail.store(sp, b, tt - 2)
                tail.wait_stored(sp, b)

        @block.gpsimd
        def _(pool):
            pool.memset(tri_f, 0.0).then_inc(tri_made, 1)
            pool.wait_ge(tri_made, 1)
            pool.memset(KS[96:97, :, :].bitcast(F32), 1.0).then_inc(const_done, 1)
            pool.wait_ge(const_done, 1)
            pool.affine_select(out=tri_f, in_=tri_f, compare_op=ALU.is_ge, fill=NEG, base=0,
                               pattern=[[-1, P]], channel_multiplier=1).then_inc(tri_made, 1)
            with pool.Fori(0, B) as b:
                for g in range(G):
                    if bias is not None:
                        for i in range(2):
                            n = b * 2 * G + 2 * g + i
                            pool.wait_ge(r_swap, n + 1)
                            pool.tensor_tensor(swapped, swapped, sinT[:, :], ALU.mult).then_inc(r_sin, 1)
                    for kt in range(TT):
                        for j in range(HG):
                            u = kt * HG + j
                            hold(pool, exp_done, b * G * U + g * U + u + 1, tail.passed[1])
                            diag = PT[:, u % 8, 0:P]
                            pool.affine_select(out=diag, in_=diag, compare_op=ALU.is_ge, fill=0.0, base=0,
                                               pattern=[[1, P]], channel_multiplier=-1).then_inc(cut_done, 1)
                for tt in range(TT):
                    tail.rsqrt(pool, b, tt)

        @block.scalar
        def _(act):
            act.wait_ge(w_in, 32 if bias is None else 80)
            act.activation(w_flat[0], w_raw, ACT.Copy).then_inc(w_hi_done, 1)
            with act.Fori(0, B) as b:
                for k in range(KT):
                    act.wait_ge(x_in_raw[k % 2], (b * (KT // 2) + k // 2 + 1) * 16)
                    act.activation(xs[0][:, k, :], raw[:, k % 2, :], ACT.Copy).then_inc(x_hi_done, 1)
                for g in range(G):
                    for i in range(2):
                        n = b * 2 * G + 2 * g + i
                        hi = (q_hi[:, :], k_hi)[i]
                        act.wait_ge(qk_psum, n + 1)
                        if bias is not None:
                            if i == 1:
                                act.wait_ge(qk_hi, n)
                                act.wait_ge(qk_lo, n)
                            act.activation(flat, A[i][:, :], ACT.Identity, bias=bias_qk[:, i * G + g:i * G + g + 1]).then_inc(r_flat, 1)
                            act.wait_ge(r_sum, n + 1)
                            act.activation(hi, flat, ACT.Copy, scale=SCALE if i == 0 else 1.0).then_inc(qk_hi, 1)
                        else:
                            act.activation(hi, A[i][:, :], ACT.Copy, scale=SCALE if i == 0 else 1.0).then_inc(qk_hi, 1)
                    act.wait_ge(mT_psum, b * G + g + 1)
                    act.activation(nmax_T[:, :], A[0][0:HG * TT, 0:P], ACT.Copy).then_inc(mT_done, 1)
                    for kt in range(TT):
                        for j in range(HG):
                            u = kt * HG + j
                            act.wait_ge(st_psum, b * G * U + g * U + u + 1)
                            if kt >= 2 and j == 0:
                                act.wait_ge(pv_done, b * G * TT + g * TT + kt - 1)
                            act.activation(PT[:, u % 8, 0:S - kt * P], A[u % 2][:, 0:S - kt * P], ACT.Exp).then_inc(exp_done, 1)
                for tt in range(TT):
                    tail.copy_T(act, b, tt)

        @block.vector
        def _(dve):
            dve.wait_ge(tri_made, 2)
            dve.tensor_copy(tri[:, :], tri_f).then_inc(const_done, 1)
            dve.wait_ge(w_hi_done, 1)
            dve.tensor_tensor(w_flat[1], w_raw, w_flat[0].bitcast(F32), ALU.subtract).then_inc(w_lo_done, 1)
            dve.memset(nmax[:, :], 0.0).then_inc(x_lo_done, 2)
            with dve.Fori(0, B) as b:
                for k in range(KT):
                    dve.wait_ge(x_hi_done, b * KT + k + 1)
                    dve.tensor_tensor(xs[1][:, k, :], raw[:, k % 2, :], xs[0][:, k, :].bitcast(F32), ALU.subtract).then_inc(x_lo_done, 1)
                for tt in range(TT):
                    dve.wait_ge(v_psum, b * TT + tt + 1)
                    if bias is None:
                        dve.tensor_copy(V[:, tt, :], v_bank[tt % 4]).then_inc(v_done, 1)
                    else:
                        dve.tensor_tensor(V[:, tt, :], v_bank[tt % 4], bias_v[:, :], ALU.add).then_inc(v_done, 1)
                for g in range(G):
                    for i in range(2):
                        n = b * 2 * G + 2 * g + i
                        hi, lo = ((q_hi[:, :], q_lo[:, :]), (k_hi, k_lo))[i]
                        if bias is not None:
                            if i == 1:
                                dve.wait_ge(r_sum, n)
                            hold(dve, r_flat, n + 1, tail.passed[2])
                            dve.stream_shuffle(swapped, flat, SWAP_HALVES).then_inc(r_swap, 1)
                            dve.wait_ge(r_swap, n + 1)
                            dve.tensor_tensor(flat, flat, cosT[:, :], ALU.mult).then_inc(r_cos, 1)
                            dve.wait_ge(r_sin, n + 1)
                            dve.wait_ge(r_cos, n + 1)
                            dve.tensor_tensor(flat, flat, swapped, ALU.add).then_inc(r_sum, 1)
                        if g and i == 0:
                            dve.wait_ge(attn_done, b * G + g)
                        dve.wait_ge(qk_hi, n + 1)
                        src = A[i][:, :] if bias is None else flat
                        dve.scalar_tensor_tensor(out=lo, in0=src, scalar=SCALE if i == 0 else 1.0, in1=hi.bitcast(F32),
                                                 op0=ALU.mult, op1=ALU.subtract).then_inc(qk_lo, 1)
                    for u in range(U):
                        width = (u % TT + 1) * P
                        dve.wait_ge(s_psum, b * G * U + g * U + u + 1)
                        dve.tensor_reduce(nmax[:, u:u + 1], A[u % 2][:, 0:width], AX.X, ALU.max, negate=True).then_inc(max_done, 1)
                    dve.wait_ge(pv_done, b * G * TT + g * TT + TT)
                    inv = q_lo[:, :].bitcast(F32)
                    dve.reciprocal(inv, SUM[:, :]).then_inc(inv_done, 1)
                    dve.wait_ge(inv_done, b * G + g + 1)
                    dve.tensor_tensor(attn[:, g, :], O[:, :], inv, ALU.mult).then_inc(attn_done, 1)
                for tt in range(TT + 1):
                    if tt < TT:
                        dve.wait_ge(y_psum, b * TT + tt + 1)
                        tail.add_stats(dve, b, tt, A[tt % 2][:, 0:H])
                    if tt:
                        tail.norm(dve, b, tt - 1)

        @block.tensor
        def _(pe):
            pe.wait_ge(w_lo_done, 1)
            pe.wait_ge(const_done, 2)
            with pe.Fori(0, B) as b:
                pe.wait_ge(x_lo_done, b * KT + KT + 2)
                for tt in range(TT):
                    if tt >= 4:
                        pe.wait_ge(v_done, b * TT + tt - 3)
                    for n, (i, j) in enumerate(TERMS):
                        for k in range(KT):
                            last = pe.matmul(v_bank[tt % 4], xs[i][:, k, tt * P:(tt + 1) * P], w[j][:, k, 2 * H:3 * H],
                                             start=(n == 0 and k == 0), stop=(n == 2 and k == KT - 1))
                    last.then_inc(v_psum, 1)
                for g in range(G):
                    if g:
                        pe.wait_ge(exp_done, b * G * U + g * U)
                    for i in range(2):
                        for h in range(S // 512):
                            for n, (a, d) in enumerate(TERMS):
                                for k in range(KT):
                                    last = pe.matmul(A[i][:, h * 512:(h + 1) * 512], w[a][:, k, i * H + g * P:i * H + (g + 1) * P],
                                                     xs[d][:, k, h * 512:(h + 1) * 512],
                                                     start=(n == 0 and k == 0), stop=(n == 2 and k == KT - 1))
                        last.then_inc(qk_psum, 1)
                    pe.wait_ge(stacked, (b * G + g + 1) * STACKS * 16)
                    for u in range(U):
                        j, qt = divmod(u, TT)
                        if u >= 2:
                            pe.wait_ge(max_done, b * G * U + g * U + u - 1)
                        width = (qt + 1) * P
                        for c0 in range(0, width, 512):
                            c1 = min(c0 + 512, width)
                            pe.matmul(A[u % 2][:, c0:c1], QS[0:96, j, qt * P:(qt + 1) * P], KS[0:96, j, c0:c1],
                                      start=True, stop=True)
                        last = pe.matmul(A[u % 2][:, width - P:width], c.ident_r[:, :], tri[:, :], start=False, stop=True,
                                         skip_group_check=True)
                        last.then_inc(s_psum, 1)
                    pe.wait_ge(max_done, b * G * U + (g + 1) * U)
                    pe.transpose(A[0][0:HG * TT, 0:P], nmax[:, :], c.ident[:, :]).then_inc(mT_psum, 1)
                    pe.wait_ge(m_row, (b * G + g + 1) * 16)
                    if g == 0:
                        pe.wait_ge(v_done, b * TT + TT)
                    else:
                        pe.wait_ge(attn_done, b * G + g)

                    def scores_T(kt):
                        width = S - kt * P
                        for j in range(HG):
                            u = kt * HG + j
                            if u >= 2:
                                pe.wait_ge(exp_done, b * G * U + g * U + u - 1)
                            for c0 in range(0, width, 512):
                                c1 = min(c0 + 512, width)
                                last = pe.matmul(A[u % 2][:, c0:c1], KS[0:97, j, kt * P:(kt + 1) * P],
                                                 QS[0:97, j, kt * P + c0:kt * P + c1], start=True, stop=True)
                            last.then_inc(st_psum, 1)

                    def values(kt):
                        pe.wait_ge(cut_done, b * G * U + g * U + (kt + 1) * HG)
                        for half in range(2):
                            q0, q1 = max(kt * P, half * 512), (half + 1) * 512
                            if q0 >= q1:
                                continue
                            for out, lhs in ((O, None), (SUM, c.ones)):
                                for j in range(HG):
                                    stat = c.ones[:, :] if lhs is not None else V[:, kt, g * P + HD * j:g * P + HD * (j + 1)]
                                    last = pe.matmul(out[HD * j:HD * (j + 1), q0:q1], stat,
                                                     PT[:, (kt * HG + j) % 8, q0 - kt * P:q1 - kt * P],
                                                     start=(kt == 0), stop=(kt == 4 * half + 3), tile_position=(0, HD * j))
                        last.then_inc(pv_done, 1)

                    scores_T(0)
                    for kt in range(1, TT):
                        scores_T(kt)
                        values(kt - 1)
                    values(TT - 1)
                pe.wait_ge(attn_done, b * G + G)
                for tt in range(TT + 1):
                    if tt < TT:
                        if tt >= 2:
                            pe.wait_ge(tail.y_sum, b * TT + tt - 1)
                        for k in range(KT):
                            col = attn[:, k, tt * P:(tt + 1) * P]
                            if woT is not None:
                                last = pe.matmul(A[tt % 2][:, 0:H], col, wo[:, k, :], start=(k == 0), stop=(k == KT - 1))
                            else:
                                last = pe.transpose(A[tt % 2][:, k * P:(k + 1) * P], col, c.ident[:, :])
                        last.then_inc(y_psum, 1)
                    if tt:
                        tail.transpose(pe, b, tt - 1)
                pe.wait_ge(tail.xT_done, b * TT + TT)


def ffn_phase(nc, c, xT_in, x_in, wg, wu, wd, x_out, xT_out):
    GT, PARTS, NB = FFN // (4 * P), 3, S // 512
    NU = GT * NB
    ctx = ExitStack()
    with ctx:
        def sb(n, shape, dt=F32):
            return ctx.enter_context(nc.sbuf_tensor(f"f_{n}", shape, dt))

        def sem(n):
            return c.semaphore(f"f_{n}")

        xs = [sb("x_hi", [P, KT, S], F32R), sb("x_lo", [P, KT, S], F32R)]
        w_raw = sb("w_raw", [P, 2, 4 * 512])
        w = [[sb(f"w_{n}{i}", [P, PARTS, 4 * 512], F32R) for n in ("hi", "lo")] for i in (0, 1)]
        y = sb("y", [P, TT, H])
        sg = sb("silu_gate", [P, 2, 512])
        h = sb("h", [P, 4, 512])
        mag = sb("mag", [P, 4, 512])
        raw = mag[:, :, :].rearrange("p (a b) n -> p a (b n)", a=2)
        cmp = sb("cmp", [P, 6, 512], BF16)
        pair = sb("pair", [P, 4, 512], BF16)
        wins = pair
        hs = [sb("h_hi", [P, 4, 512], F32R), sb("h_lo", [P, 4, 512], F32R)]
        GU = [[ctx.enter_context(nc.psum_tensor(f"f_{n}{i}", [P, 512], F32)) for n in ("gate", "up")] for i in (0, 1)]
        D = [ctx.enter_context(nc.psum_tensor(f"f_D{i}", [P, H], F32)) for i in range(4)]

        x_raw_in = [sem("x_raw_in0"), sem("x_raw_in1")]
        x_hi_done, x_lo_done, y_in = sem("x_hi_done"), sem("x_lo_done"), sem("y_in")
        w_raw_in = [sem("w_raw_in0"), sem("w_raw_in1")]
        w_hi_done, w_lo_done = sem("w_hi_done"), sem("w_lo_done")
        gu_psum, silu_done, h_done, mag_done = sem("gu_psum"), sem("silu_done"), sem("h_done"), sem("mag_done")
        cmp_done, pair_done, wins_done, keep_done = sem("cmp_done"), sem("pair_done"), sem("wins_done"), sem("keep_done")
        hs_hi_done, hs_lo_done, d_psum, sum_done = sem("hs_hi_done"), sem("hs_lo_done"), sem("d_psum"), sem("sum_done")
        tail = Tail(nc, ctx, "f_t", None, [y[:, t, :] for t in range(TT)], [mag[:, i, :] for i in (0, 1)],
                    [mag[:, i, :] for i in (2, 3)], [GU[i][0][:, :] for i in (0, 1)], c, x_out, xT_out)

        x_rows = x_in.rearrange("(b t p) n -> b p t n", b=B, p=P)
        x_cols = xT_in.rearrange("(k p) (b s) -> b k p s", p=P, b=B)
        w_dram = [wg.rearrange("g p k j m -> g p (k j m)"), wu.rearrange("g p k j m -> g p (k j m)"),
                  wd.rearrange("g p j n -> g p (j n)")]
        gate_up = [[t[:, :, :].rearrange("p a (k j m) -> p a k j m", k=KT, j=4) for t in s] for s in w]
        down = [[t[:, 2, :].rearrange("p (j n) -> p j n", j=4) for t in s] for s in w]
        block = ctx.enter_context(nc.Block())

        def first_part(b, gt):
            return 3 + b * GT * PARTS + gt * PARTS

        def raw_count(b, gt, m):
            return (b * (GT * PARTS // 2) + (3 + gt * PARTS + m) // 2 + 1) * 16

        @block.sync
        def _(sp):
            for m in range(PARTS):
                if m == 2:
                    sp.wait_ge(w_lo_done, 1)
                sp.dma_start(w_raw[:, m % 2, :], w_dram[m][0]).then_inc(w_raw_in[m % 2], 16)
            with sp.Fori(0, B) as b:
                sp.dma_start(y[:, :, :], x_rows[b]).then_inc(y_in, 16)
                for k in range(KT):
                    sp.wait_ge(x_lo_done, b * KT + k + 1)
                    sp.dma_start(raw[:, k % 2, :], x_cols[b, k]).then_inc(x_raw_in[k % 2], 16)
                for gt in range(GT):
                    for m in range(PARTS):
                        sp.wait_ge(w_lo_done, first_part(b, gt) + m - 1)
                        sp.dma_start(w_raw[:, (1 + gt + m) % 2, :], w_dram[m][(gt + 1) % GT]).then_inc(w_raw_in[(1 + gt + m) % 2], 16)
                for tt in range(TT):
                    tail.store(sp, b, tt)
                tail.wait_stored(sp, b)

        @block.gpsimd
        def _(pool):
            def split_lo(gt_to, m, slot, count):
                pool.wait_ge(w_hi_done, count)
                pool.tensor_tensor(w[gt_to % 2][1][:, m, :], w_raw[:, slot, :], w[gt_to % 2][0][:, m, :].bitcast(F32),
                                   ALU.subtract).then_inc(w_lo_done, 1)

            for m in range(PARTS):
                split_lo(0, m, m % 2, m + 1)
            with pool.Fori(0, B) as b:
                for gt in range(GT):
                    for m in range(PARTS):
                        split_lo(gt + 1, m, (1 + gt + m) % 2, first_part(b, gt) + m + 1)
                for tt in range(TT):
                    tail.rsqrt(pool, b, tt)

        @block.scalar
        def _(act):
            for m in range(PARTS):
                act.wait_ge(w_raw_in[m % 2], 16 * (m // 2 + 1))
                act.activation(w[0][0][:, m, :], w_raw[:, m % 2, :], ACT.Copy).then_inc(w_hi_done, 1)

            def split_h(b, u):
                act.wait_ge(keep_done, (b * NU + u + 1) * 4)
                if u:
                    act.wait_ge(d_psum, (b * NU + u) * 4)
                act.activation(hs[0][:, :, :], h[:, :, :], ACT.Copy).then_inc(hs_hi_done, 1)

            with act.Fori(0, B) as b:
                for k in range(KT):
                    act.wait_ge(x_raw_in[k % 2], (b * (KT // 2) + k // 2 + 1) * 16)
                    act.activation(xs[0][:, k, :], raw[:, k % 2, :], ACT.Copy).then_inc(x_hi_done, 1)
                for u in range(NU):
                    for j in range(4):
                        n = (b * NU + u) * 4 + j
                        act.wait_ge(gu_psum, n + 1)
                        if u or j >= 2:
                            act.wait_ge(h_done, n - 1)
                        act.activation(sg[:, j % 2, :], GU[j % 2][0][:, :], ACT.Silu).then_inc(silu_done, 1)
                        act.wait_ge(h_done, n + 1)
                        if u:
                            act.wait_ge(cmp_done, (b * NU + u) * 3)
                        elif j == 0:
                            act.wait_ge(x_lo_done, b * KT + KT + 2)
                        act.activation(mag[:, j, :], h[:, j, :], ACT.Abs).then_inc(mag_done, 1)
                    if u % NB == 0:
                        gt = u // NB
                        for m in range(PARTS):
                            act.wait_ge(w_raw_in[(1 + gt + m) % 2], raw_count(b, gt, m))
                            if u >= NB:
                                act.wait_ge(d_psum, (b * NU + u) * 4)
                            act.activation(w[(gt + 1) % 2][0][:, m, :], w_raw[:, (1 + gt + m) % 2, :], ACT.Copy).then_inc(w_hi_done, 1)
                    split_h(b, u)
                for tt in range(TT):
                    tail.copy_T(act, b, tt)

        @block.vector
        def _(dve):
            dve.memset(pair[:, :, :], 0.0).then_inc(x_lo_done, 2)

            def mul(b, u, j):
                n = (b * NU + u) * 4 + j
                dve.wait_ge(silu_done, n + 1)
                dve.tensor_tensor(h[:, j, :], sg[:, j % 2, :], GU[j % 2][1][:, :], ALU.mult).then_inc(h_done, 1)

            def add(b, u):
                for t in range(4):
                    n = (b * NU + u) * 4 + t
                    tile = y[:, (u % NB) * 4 + t, :]
                    if u < NB:
                        dve.wait_ge(y_in, (b + 1) * 16)
                    else:
                        dve.wait_ge(sum_done, n + 1 - NB * 4)
                    dve.wait_ge(d_psum, n + 1)
                    dve.tensor_tensor(tile, D[t][:, :], tile, ALU.add).then_inc(sum_done, 1)

            def choose(b, u):
                n = b * NU + u
                dve.wait_ge(mag_done, (n + 1) * 4)
                dve.tensor_tensor(cmp[:, 0:2, :], mag[:, 0::2, :], mag[:, 1::2, :], ALU.is_ge).then_inc(cmp_done, 1)
                dve.tensor_tensor(cmp[:, 2:4, :], mag[:, 0:2, :], mag[:, 2:4, :], ALU.is_ge).then_inc(cmp_done, 1)
                dve.tensor_tensor(cmp[:, 4:6, :], mag[:, 0:2, :], mag[:, 3:1:-1, :], ALU.is_ge).then_inc(cmp_done, 1)
                dve.wait_ge(cmp_done, (n + 1) * 3)
                dve.tensor_tensor(pair[:, 0:2, :], cmp[:, 2:4, :], cmp[:, 4:6, :], ALU.add).then_inc(pair_done, 1)
                dve.tensor_tensor(pair[:, 2:4, :], cmp[:, 2:5:2, :], cmp[:, 5:2:-2, :], ALU.add).then_inc(pair_done, 1)
                dve.wait_ge(pair_done, (n + 1) * 2)
                dve.tensor_tensor(wins[:, 0, :], pair[:, 0, :], cmp[:, 0, :], ALU.add).then_inc(wins_done, 1)
                dve.tensor_tensor(wins[:, 1, :], pair[:, 1, :], cmp[:, 0, :], ALU.subtract).then_inc(wins_done, 1)
                dve.tensor_tensor(wins[:, 2, :], cmp[:, 1, :], pair[:, 2, :], ALU.subtract).then_inc(wins_done, 1)
                dve.tensor_tensor(wins[:, 3, :], cmp[:, 1, :], pair[:, 3, :], ALU.add).then_inc(wins_done, 1)
                dve.wait_ge(wins_done, (n + 1) * 4)
                for j, (op, bound) in enumerate(((ALU.is_ge, 2.0), (ALU.is_ge, 1.0), (ALU.is_ge, 0.0), (ALU.is_le, 1.0))):
                    dve.scalar_tensor_tensor(out=h[:, j, :], in0=wins[:, j, :], scalar=bound, in1=h[:, j, :],
                                             op0=op, op1=ALU.mult).then_inc(keep_done, 1)
                dve.wait_ge(hs_hi_done, n + 1)
                dve.tensor_tensor(hs[1][:, :, :], h[:, :, :], hs[0][:, :, :].bitcast(F32), ALU.subtract).then_inc(hs_lo_done, 1)

            with dve.Fori(0, B) as b:
                for k in range(KT):
                    dve.wait_ge(x_hi_done, b * KT + k + 1)
                    dve.tensor_tensor(xs[1][:, k, :], raw[:, k % 2, :], xs[0][:, k, :].bitcast(F32), ALU.subtract).then_inc(x_lo_done, 1)
                for u in range(NU):
                    if u:
                        dve.wait_ge(hs_lo_done, b * NU + u)
                    mul(b, u, 0)
                    mul(b, u, 1)
                    if u:
                        add(b, u - 1)
                    mul(b, u, 2)
                    mul(b, u, 3)
                    choose(b, u)
                add(b, NU - 1)
                dve.wait_ge(sum_done, (b + 1) * NU * 4)
                for tt in range(TT + 1):
                    if tt < TT:
                        tail.stats_of(dve, b, tt)
                    if tt:
                        tail.norm(dve, b, tt - 1)

        @block.tensor
        def _(pe):
            def gate_up_products(b, u, j):
                n = (b * NU + u) * 4 + j
                s, blk = (u // NB) % 2, u % NB
                if u or j >= 2:
                    pe.wait_ge(h_done, n - 1)
                for a in (0, 1):
                    for t, (i, d) in enumerate(TERMS):
                        for k in range(KT):
                            last = pe.matmul(GU[j % 2][a][:, :], gate_up[s][i][:, a, k, j, :], xs[d][:, k, blk * 512:(blk + 1) * 512],
                                             start=(t == 0 and k == 0), stop=(t == 2 and k == KT - 1))
                last.then_inc(gu_psum, 1)

            def down_products(b, u):
                s = (u // NB) % 2
                pe.wait_ge(hs_lo_done, b * NU + u + 1)
                for tt in range(4):
                    if u:
                        pe.wait_ge(sum_done, (b * NU + u) * 4 - 3 + tt)
                    for t, (i, d) in enumerate(TERMS):
                        for j in range(4):
                            last = pe.matmul(D[tt][:, :], hs[i][:, j, tt * P:(tt + 1) * P], down[s][d][:, j, :],
                                             start=(t == 0 and j == 0), stop=(t == 2 and j == 3))
                    last.then_inc(d_psum, 1)

            with pe.Fori(0, B) as b:
                pe.wait_ge(x_lo_done, b * KT + KT + 2)
                for u in range(NU):
                    if u % NB == 0:
                        pe.wait_ge(w_lo_done, first_part(b, u // NB))
                    gate_up_products(b, u, 0)
                    gate_up_products(b, u, 1)
                    if u:
                        down_products(b, u - 1)
                    gate_up_products(b, u, 2)
                    gate_up_products(b, u, 3)
                down_products(b, NU - 1)
                for tt in range(TT):
                    tail.transpose(pe, b, tt)
                pe.wait_ge(tail.xT_done, b * TT + TT)


def moe_phase(nc, c, xT_in, x_in, ew, rw, eb, rb, same_expert, earlier_chunk, chunk_of, out):
    NT, NC = T // P, P // NE
    R = NT // NC
    W = R * P
    HALVES = [1 << n for n in range(W.bit_length() - 1)]
    ctx = ExitStack()
    with ctx:
        def sb(n, shape, dt=F32):
            return ctx.enter_context(nc.sbuf_tensor(f"m_{n}", shape, dt))

        def sem(n):
            return c.semaphore(f"m_{n}")

        w_raw, w = sb("w_raw", [P, KT, H]), [sb("w_hi", [P, KT, H], F32R), sb("w_lo", [P, KT, H], F32R)]
        rw_sb, rb_sb, eb_sb = sb("rw", [P, KT, NE]), sb("rb", [P, NE]), sb("eb", [P, H])
        same_sb, earlier_sb, chunk_sb = sb("same", [P, P]), sb("earlier", [P, P]), sb("chunk", [P, NC])
        raw = sb("raw", [P, 2, KT, W])
        xs = [sb("x_hi", [P, KT, W * 2], F32R), sb("x_lo", [P, KT, W * 2], F32R)]
        z = sb("z", [P, NT, H])
        logits, e = sb("logits", [P, NT, NE]), sb("e", [P, NT, NE])
        row = sb("row", [P, 2, NT])
        probs = sb("probs", [P, R, NC, NE])
        ST = sb("ST", [P, W])
        junk, eq = sb("junk", [P, W]), sb("eq", [P, W])
        pre = [sb("pre0", [P, W]), sb("pre1", [P, W])]
        thr, cand, taken = sb("thr", [P, 1], I32), sb("cand", [P, 1], I32), sb("taken", [P, 1])
        bit = sb("bit", [P, 1], I32)
        cnt, need = sb("cnt", [P, 3]), sb("need", [P, 2])
        gates = sb("gates", [P, NT])
        tail_slots = [[w_raw[:, 2 * i + j, :] for j in (0, 1)] for i in (0, 1)] + [[raw[:, 0, j, :] for j in (0, 1)], None]
        psL = [ctx.enter_context(nc.psum_tensor(f"m_psL{i}", [P, R, NE], F32)) for i in (0, 1)]
        psZ = [ctx.enter_context(nc.psum_tensor(f"m_psZ{i}", [P, H], F32)) for i in (0, 1)]
        psT = ctx.enter_context(nc.psum_tensor("m_psT", [P, W], F32))
        psC = ctx.enter_context(nc.psum_tensor("m_psC", [P, 4], F32))
        psG = ctx.enter_context(nc.psum_tensor("m_psG", [P, R, NC], F32))

        small_in, w_in, w_hi_done, w_lo_done = sem("small_in"), sem("w_in"), sem("w_hi_done"), sem("w_lo_done")
        raw_in = [sem("raw_in0"), sem("raw_in1")]
        l_psum, l_done = sem("l_psum"), sem("l_done")
        step = sem("softmax_step")
        exp_done, t_psum, st_done = sem("exp_done"), sem("t_psum"), sem("st_done")
        x_hi_done, x_lo_done, z_psum, z_done = sem("x_hi_done"), sem("x_lo_done"), sem("z_psum"), sem("z_done")
        cand_done, cnt_done, cnt_psum, taken_done, thr_done = (sem(n) for n in ("cand_done", "cnt_done", "cnt_psum", "taken_done", "thr_done"))
        bit_done = sem("bit_done")
        tie_cnt, tie_psum, tie = sem("tie_cnt"), sem("tie_psum"), sem("tie_step")
        g_in, g_psum, g_done = sem("g_in"), sem("g_psum"), sem("g_done")
        tail = Tail(nc, ctx, "m_t", *tail_slots, None, c, out, None)

        x_rows = x_in.rearrange("(b t p) n -> b t p n", b=B, p=P)
        x_cols = xT_in.rearrange("(k p) (c s) -> c p k s", p=P, c=NC)
        w_flat = [t[:, :, :].rearrange("p k n -> p (k n)") for t in w]
        BC = NC // B
        block = ctx.enter_context(nc.Block())

        @block.sync
        def _(sp):
            sp.dma_start(rw_sb[:, :, :], rw.rearrange("(k p) n -> p k n", p=P)).then_inc(small_in, 16)
            sp.dma_start(rb_sb[:, :], rb.partition_broadcast(P)).then_inc(small_in, 16)
            sp.dma_start(eb_sb[:, :], eb.partition_broadcast(P)).then_inc(small_in, 16)
            sp.dma_start(same_sb[:, :], same_expert).then_inc(small_in, 16)
            sp.dma_start(earlier_sb[:, :], earlier_chunk).then_inc(small_in, 16)
            sp.dma_start(chunk_sb[:, :], chunk_of).then_inc(small_in, 16)
            sp.dma_start(w_raw[:, :, :], ew.rearrange("(k p) n -> p k n", p=P)).then_inc(w_in, 16)
            with sp.Fori(0, B) as b:
                for i in range(BC):
                    sp.wait_ge(l_psum, b * BC + i + 1)
                    sp.dma_start(raw[:, i, :, :], x_cols[b * BC + i]).then_inc(raw_in[i], 16)
            with sp.Fori(0, B) as b:
                for i in range(BC):
                    if i == 0:
                        sp.wait_ge(l_psum, NC + 2)
                    sp.wait_ge(x_lo_done, b * BC + i + 1)
                    sp.dma_start(raw[:, i, :, :], x_cols[b * BC + i]).then_inc(raw_in[i], 16)
            sp.wait_ge(g_done, 1)
            with sp.Fori(0, B) as b:
                for tt in range(TT + 2):
                    if tt < TT:
                        tail.load_res(sp, b, tt, x_rows)
                    if tt >= 2:
                        tail.store(sp, b, tt - 2)
                tail.wait_stored(sp, b)

        @block.gpsimd
        def _(pool):
            with pool.Fori(0, B) as b:
                for tt in range(TT):
                    tail.rsqrt(pool, b, tt)

        @block.scalar
        def _(act):
            act.wait_ge(w_in, 16)
            act.activation(w_flat[0], w_raw[:, :, :].rearrange("p k n -> p (k n)"), ACT.Copy).then_inc(w_hi_done, 1)
            act.wait_ge(step, 2)
            act.activation(e[:, :, :], logits[:, :, :], ACT.Exp).then_inc(exp_done, 1)
            act.wait_ge(t_psum, 1)
            act.activation(ST[:, :], psT[:, :], ACT.Copy).then_inc(st_done, 1)
            with act.Fori(0, B) as b:
                for i in range(BC):
                    act.wait_ge(raw_in[i], (B + b + 1) * 16)
                    if i == 0:
                        act.wait_ge(z_psum, b * TT + 1)
                    act.activation(xs[0][:, :, i * W:(i + 1) * W], raw[:, i, :, :], ACT.Copy).then_inc(x_hi_done, 1)

        @block.vector
        def _(dve):
            dve.wait_ge(w_hi_done, 1)
            dve.tensor_tensor(w_flat[1], w_raw[:, :, :].rearrange("p k n -> p (k n)"), w_flat[0].bitcast(F32),
                              ALU.subtract).then_inc(w_lo_done, 1)
            dve.memset(thr[:, :], 0).then_inc(thr_done, 1)
            dve.memset(bit[:, :], 1 << 30).then_inc(bit_done, 1)
            dve.memset(junk[:, 0:1], 0.0).then_inc(l_psum, 2)
            dve.memset(junk[:, 1:2], 0.0).then_inc(x_lo_done, 2)
            dve.memset(junk[:, 2:3], 0.0).then_inc(l_done, 2)
            dve.wait_ge(small_in, 6 * 16)
            with dve.Fori(0, B) as b:
                for i in range(BC):
                    dve.wait_ge(l_psum, b * BC + i + 3)
                    dve.tensor_tensor(logits[:, bass.ds(b * BC * R + i * R, R), :], psL[i][:, :, :],
                                      rb_sb[:, :].unsqueeze(1).to_broadcast([P, R, NE]), ALU.add).then_inc(l_done, 1)
            dve.wait_ge(l_done, NC + 2)
            dve.tensor_reduce(row[:, 0, :], logits[:, :, :], AX.X, ALU.max).then_inc(step, 1)
            dve.wait_ge(step, 1)
            dve.tensor_tensor(logits[:, :, :], logits[:, :, :], row[:, 0, :].unsqueeze(2).to_broadcast([P, NT, NE]),
                              ALU.subtract).then_inc(step, 1)
            dve.wait_ge(exp_done, 1)
            dve.tensor_reduce(row[:, 1, :], e[:, :, :], AX.X, ALU.add).then_inc(step, 1)
            dve.wait_ge(step, 3)
            dve.reciprocal(row[:, 0, :], row[:, 1, :]).then_inc(step, 1)
            dve.wait_ge(step, 4)
            dve.tensor_tensor(probs[:, :, :, :].rearrange("p r c e -> p c r e"),
                              e[:, :, :].rearrange("p (c r) e -> p c r e", c=NC),
                              row[:, 0, :].rearrange("p (c r) -> p c r", c=NC).unsqueeze(3).to_broadcast([P, NC, R, NE]),
                              ALU.mult).then_inc(step, 1)
            dve.wait_ge(st_done, 1)
            with dve.Fori(0, B) as b:
                for i in range(BC):
                    dve.wait_ge(x_hi_done, b * BC + i + 1)
                    dve.tensor_tensor(xs[1][:, :, i * W:(i + 1) * W], raw[:, i, :, :],
                                      xs[0][:, :, i * W:(i + 1) * W].bitcast(F32), ALU.subtract).then_inc(x_lo_done, 1)
                for tt in range(TT):
                    n = b * TT + tt
                    dve.wait_ge(thr_done, n + 1)
                    dve.wait_ge(bit_done, n + 1)
                    dve.tensor_tensor(cand[:, :], thr[:, :], bit[:, :], ALU.bitwise_or).then_inc(cand_done, 1)
                    dve.wait_ge(cand_done, n + 1)
                    dve.tensor_scalar(bit[:, :], bit[:, :], 1, None, ALU.logical_shift_right).then_inc(bit_done, 1)
                    dve.tensor_scalar(junk[:, :], ST[:, :], cand[:, :].bitcast(F32), None, ALU.is_ge, ALU.add,
                                      accum_out=cnt[:, 0:1]).then_inc(cnt_done, 1)
                    dve.wait_ge(z_psum, n + 2)
                    dve.tensor_tensor(z[:, bass.ds(b * TT + tt, 1), :].rearrange("p a n -> p (a n)"), psZ[tt % 2][:, :], eb_sb[:, :],
                                      ALU.add).then_inc(z_done, 1)
                    dve.wait_ge(cnt_psum, n + 1)
                    dve.scalar_tensor_tensor(out=taken[:, :], in0=psC[:, 0:1], scalar=TOPK - 0.5, in1=cand[:, :].bitcast(F32),
                                             op0=ALU.is_ge, op1=ALU.mult).then_inc(taken_done, 1)
                    dve.wait_ge(taken_done, n + 1)
                    dve.tensor_tensor(thr[:, :].bitcast(F32), thr[:, :].bitcast(F32), taken[:, :], ALU.max).then_inc(thr_done, 1)
            dve.wait_ge(thr_done, NT + 1)
            t = thr[:, :].bitcast(F32)
            dve.tensor_scalar(junk[:, :], ST[:, :], t, None, ALU.is_gt, ALU.add, accum_out=cnt[:, 1:2]).then_inc(tie_cnt, 1)
            dve.tensor_scalar(eq[:, :], ST[:, :], t, None, ALU.is_equal, ALU.add, accum_out=cnt[:, 2:3]).then_inc(tie_cnt, 1)
            dve.wait_ge(tie_cnt, 2)
            src = eq
            for s, d in enumerate(HALVES):
                dst = pre[s % 2]
                dve.tensor_tensor(dst[:, d:W], src[:, d:W], src[:, 0:W - d], ALU.add).then_inc(tie, 1)
                dve.tensor_copy(dst[:, 0:d], src[:, 0:d]).then_inc(tie, 1)
                dve.wait_ge(tie, 2 * (s + 1))
                src = dst
            n = 2 * len(HALVES)
            dve.wait_ge(tie_psum, 1)
            dve.tensor_copy(need[:, 1:2], psC[:, 2:3]).then_inc(tie, 1)
            dve.wait_ge(tie, n + 1)
            dve.scalar_tensor_tensor(out=need[:, 0:1], in0=psC[:, 1:2], scalar=-1.0, in1=need[:, 1:2],
                                     op0=ALU.mult, op1=ALU.subtract).then_inc(tie, 1)
            dve.wait_ge(tie, n + 2)
            dve.tensor_scalar(need[:, 1:2], need[:, 0:1], float(TOPK), None, ALU.add).then_inc(tie, 1)
            dve.wait_ge(tie, n + 3)
            dve.scalar_tensor_tensor(out=eq[:, :], in0=src[:, :], scalar=need[:, 1:2], in1=eq[:, :],
                                     op0=ALU.is_le, op1=ALU.mult).then_inc(tie, 1)
            dve.wait_ge(tie, n + 4)
            dve.scalar_tensor_tensor(out=eq[:, :], in0=ST[:, :], scalar=t, in1=eq[:, :],
                                     op0=ALU.is_gt, op1=ALU.add).then_inc(tie, 1)
            dve.wait_ge(tie, n + 5)
            dve.tensor_tensor(junk[:, :], eq[:, :], ST[:, :], ALU.mult).then_inc(g_in, 1)
            dve.wait_ge(g_psum, 1)
            dve.tensor_copy(gates[:, :].rearrange("p (c r) -> p r c", c=NC), psG[:, :, :]).then_inc(g_done, 1)
            dve.wait_ge(g_done, 1)
            dve.wait_ge(z_done, NT)
            with dve.Fori(0, B) as b:
                for tt in range(TT + 1):
                    if tt < TT:
                        s = tt % 2
                        if tt >= 2:
                            dve.wait_ge(tail.xn_done, b * TT + tt - 1)
                        dve.wait_ge(tail.res_in[s], tail.loads(b, tt))
                        dve.scalar_tensor_tensor(out=tail.y[s], in0=z[:, bass.ds(b * TT + tt, 1), :].rearrange("p a n -> p (a n)"),
                                                 scalar=gates[:, bass.ds(b * TT + tt, 1)], in1=tail.res[s],
                                                 op0=ALU.mult, op1=ALU.add).then_inc(tail.y_sum, 1)
                        dve.wait_ge(tail.y_sum, b * TT + tt + 1)
                        tail.stats_of(dve, b, tt)
                    if tt:
                        tail.norm(dve, b, tt - 1)

        @block.tensor
        def _(pe):
            pe.wait_ge(small_in, 6 * 16)
            with pe.Fori(0, B) as b:
                for i in range(BC):
                    pe.wait_ge(l_done, b * BC + i + 1)
                    pe.wait_ge(raw_in[i], (b + 1) * 16)
                    for r in range(R):
                        for k in range(KT):
                            last = pe.matmul(psL[i][:, r, :], raw[:, i, k, r * P:(r + 1) * P], rw_sb[:, k, :],
                                             start=(k == 0), stop=(k == KT - 1))
                    last.then_inc(l_psum, 1)
            pe.wait_ge(step, 5)
            for r in range(R):
                last = pe.transpose(psT[:, r * P:(r + 1) * P], probs[:, r, :, :].rearrange("p c e -> p (c e)"), c.ident[:, :])
            last.then_inc(t_psum, 1)
            pe.wait_ge(w_lo_done, 1)
            pe.matmul(psC[:, 3:4], c.ident[:, :], c.ident[:, 0:1], start=True, stop=True).then_inc(z_psum, 1)
            with pe.Fori(0, B) as b:
                pe.wait_ge(x_lo_done, b * BC + BC + 2)
                for tt in range(TT):
                    n = b * TT + tt
                    if tt >= 2:
                        pe.wait_ge(z_done, n - 1)
                    for a, (i, d) in enumerate(TERMS):
                        for k in range(KT):
                            last = pe.matmul(psZ[tt % 2][:, :], xs[i][:, k, tt * P:(tt + 1) * P], w[d][:, k, :],
                                             start=(a == 0 and k == 0), stop=(a == 2 and k == KT - 1))
                    last.then_inc(z_psum, 1)
                    pe.wait_ge(cnt_done, n + 1)
                    pe.matmul(psC[:, 0:1], same_sb[:, :], cnt[:, 0:1], start=True, stop=True).then_inc(cnt_psum, 1)
            pe.wait_ge(tie_cnt, 2)
            pe.matmul(psC[:, 1:2], same_sb[:, :], cnt[:, 1:2], start=True, stop=True)
            pe.matmul(psC[:, 2:3], earlier_sb[:, :], cnt[:, 2:3], start=True, stop=True).then_inc(tie_psum, 1)
            pe.wait_ge(g_in, 1)
            for r in range(R):
                last = pe.matmul(psG[:, r, :], junk[:, r * P:(r + 1) * P], chunk_sb[:, :], start=True, stop=True)
            last.then_inc(g_psum, 1)


def build(nc, xT, x, wqkvT0, wo0T, wg, wu, wd, wqkvT1, bqkT1, bv1, cosT, sinT, rw, rb, ew, eb,
          same_expert, earlier_chunk, chunk_of, out, stages=4):
    def scratch(name, shape):
        return nc.dram_tensor(name, shape, F32, kind="Internal").ap()

    x1, x1T, x2, x2T, x3, x3T = (scratch(f"s_{n}", s) for n, s in
                                 (("x1", [T, H]), ("x1T", [H, T]), ("x2", [T, H]), ("x2T", [H, T]), ("x3", [T, H]), ("x3T", [H, T])))
    m_scratch = scratch("s_m", [HG * TT, P])
    with ExitStack() as ctx:
        c = Consts(nc, ctx)
        if stages == 1:
            x1 = out
        attention_phase(nc, c, "a0", xT, x, wqkvT0, wo0T, None, None, m_scratch, x1, x1T)
        c.end_phase()
        if stages == 1:
            return
        ffn_phase(nc, c, x1T, x1, wg, wu, wd, out if stages == 2 else x2, x2T)
        c.end_phase()
        if stages == 2:
            return
        attention_phase(nc, c, "a1", x2T, x2, wqkvT1, None, (bqkT1, bv1), (cosT, sinT), m_scratch, out if stages == 3 else x3, x3T)
        c.end_phase()
        if stages == 3:
            return
        moe_phase(nc, c, x3T, x3, ew, rw, eb, rb, same_expert, earlier_chunk, chunk_of, out)


def kernel(**inputs):
    import numpy as np
    import concourse.bacc as bacc
    from concourse.bass_utils import run_bass_kernel_spmd

    arrays, order = layout(inputs, np)
    nc = bacc.Bacc("TRN2", target_bir_lowering=False, num_devices=1)
    args = [nc.dram_tensor(f"in_{n}", arrays[n].shape, mybir.dt.from_np(arrays[n].dtype), kind="ExternalInput").ap() for n in order]
    out = nc.dram_tensor("out_y", (T, H), F32, kind="ExternalOutput").ap()
    build(nc, *args, out)
    r = run_bass_kernel_spmd(nc, [{f"in_{n}": arrays[n] for n in order}], core_ids=[0])
    return r.results[0]["out_y"].reshape(B, S, H)


def layout(inputs, np):
    a = {k: np.asarray(v) for k, v in inputs.items()}
    x = a["L0_attn_hidden_states"].reshape(T, H)
    inv_freq = (1.0 / np.float32(10000.0) ** (np.arange(0, HD, 2, dtype=np.float32) / np.float32(HD))).astype(np.float32)
    freqs = np.outer(np.arange(S, dtype=np.float32), inv_freq).astype(np.float32).T
    cos, sin = np.cos(freqs), np.sin(freqs)
    chunk, expert = np.arange(P) // NE, np.arange(P) % NE
    arrays = {
        "xT": np.ascontiguousarray(x.T),
        "x": x,
        "wqkvT0": np.ascontiguousarray(a["L0_attn_w_qkv"].T),
        "wo0T": np.ascontiguousarray(a["L0_attn_w_o"].T),
        "wg": np.ascontiguousarray(a["L0_ffn_w_gate"].reshape(KT, P, 4, P, 4).transpose(2, 1, 0, 4, 3)),
        "wu": np.ascontiguousarray(a["L0_ffn_w_up"].reshape(KT, P, 4, P, 4).transpose(2, 1, 0, 4, 3)),
        "wd": a["L0_ffn_w_down"].reshape(4, P, 4, H),
        "wqkvT1": np.ascontiguousarray(a["L1_attn_Wqkv_w"].T),
        "bqkT1": np.ascontiguousarray(a["L1_attn_Wqkv_b"][0:2 * H].reshape(2 * G, P).T),
        "bv1": a["L1_attn_Wqkv_b"][2 * H:3 * H],
        "cosT": np.ascontiguousarray(np.tile(np.concatenate([cos, cos]), (HG, 1)).astype(np.float32)),
        "sinT": np.ascontiguousarray(np.tile(np.concatenate([-sin, sin]), (HG, 1)).astype(np.float32)),
        "rw": a["L1_ffn_router_w"],
        "rb": a["L1_ffn_router_b"],
        "ew": a["L1_ffn_expert_w"],
        "eb": a["L1_ffn_expert_b"],
        "same_expert": (expert[:, None] == expert[None, :]).astype(np.float32),
        "earlier_chunk": ((expert[:, None] == expert[None, :]) & (chunk[:, None] < chunk[None, :])).astype(np.float32),
        "chunk_of": (chunk[:, None] == np.arange(P // NE)[None, :]).astype(np.float32),
    }
    return arrays, list(arrays)
```

```python
from contextlib import ExitStack

import concourse.bass as bass
from concourse import mybir

F32 = mybir.dt.float32
F32R = mybir.dt.float32r
BF16 = mybir.dt.bfloat16
I32 = mybir.dt.int32
ALU = mybir.AluOpType
ACT = mybir.ActivationFunctionType
AX = mybir.AxisListType

P = 128
B, S, H = 4, 1024, 512
T = B * S
NH, HD = 16, 32
KT = H // P
TT = S // P
G = NH * HD // P
HG = P // HD
FFN = 2048
NE = 16
TOPK = T // NE
EPS = 1e-5
SCALE = float(HD) ** -0.5
TERMS = ((0, 0), (0, 1), (1, 0))
SWAP_HALVES = [(i + 16) % 32 for i in range(32)]


def hold(eng, sem, value, passed):
    eng.wait_ge(sem, value)
    eng.sem_inc(passed, 1)


class Tail:

    def __init__(self, nc, ctx, name, res, y, xn, xTs, psum_slots, consts, x_out, xT_out):
        def sem(n):
            return consts.semaphore(f"{name}_{n}")

        def sb(n, shape):
            return ctx.enter_context(nc.sbuf_tensor(f"{name}_{n}", shape, F32))

        self.nc, self.psT, self.c = nc, psum_slots, consts
        self.x_out = x_out.rearrange("(b t p) n -> b t p n", b=B, p=P)
        self.xT_out = xT_out.rearrange("(k p) (b t c) -> b t p k c", p=P, b=B, c=P) if xT_out is not None else None
        self.res, self.y, self.xn, self.xTs = res, y, xn, xTs
        self.stats = sb("stats", [P, 4, 6])
        self.mv = sb("mv", [P, 4, 2])
        self.vare = sb("vare", [P, 4])
        self.rstd = sb("rstd", [P, 4])
        self.res_in = [sem(f"res_in{i}") for i in (0, 1)]
        self.y_sum = sem("y_sum")
        self.y_stats = sem("y_stats")
        self.y_mv = sem("y_mv")
        self.y_vare = sem("y_vare")
        self.y_rstd = sem("y_rstd")
        self.xn_done = sem("xn_done")
        self.xT_psum = sem("xT_psum")
        self.xT_done = sem("xT_done")
        self.passed = [sem(f"passed_{e}") for e in ("sp", "pool", "dve")]
        self.out_x = [sem(f"out_x{i}") for i in (0, 1)]
        self.out_xT = [sem(f"out_xT{i}") for i in (0, 1)]

    def load_res(self, sp, b, tt, x_in):
        if tt >= 2:
            sp.wait_ge(self.xn_done if self.y is self.res else self.y_sum, b * TT + tt - 1)
        sp.dma_start(self.res[tt % 2], x_in[b, tt]).then_inc(self.res_in[tt % 2], 16)

    def store(self, sp, b, tt):
        sp.wait_ge(self.xn_done, b * TT + tt + 1)
        sp.dma_start(self.x_out[b, tt], self.xn[tt % len(self.xn)]).then_inc(self.out_x[tt % 2], 16)
        if self.xT_out is not None:
            sp.wait_ge(self.xT_done, b * TT + tt + 1)
            sp.dma_start(self.xT_out[b, tt], self.xTs[tt % 2].rearrange("p (k c) -> p k c", k=KT)).then_inc(self.out_xT[tt % 2], 16)

    @staticmethod
    def loads(b, tt):
        return (b * (TT // 2) + tt // 2 + 1) * 16

    def wait_stored(self, sp, b):
        for slot in (0, 1):
            if self.xT_out is not None:
                sp.wait_ge(self.out_xT[slot], self.loads(b, TT - 2))
            hold(sp, self.out_x[slot], self.loads(b, TT - 2), self.passed[0])

    def add_stats(self, dve, b, tt, part):
        s = tt % 2
        dve.wait_ge(self.res_in[s], self.loads(b, tt))
        dve.tensor_tensor(self.y[s], part, self.res[s], ALU.add).then_inc(self.y_sum, 1)
        dve.wait_ge(self.y_sum, b * TT + tt + 1)
        self.stats_of(dve, b, tt)

    def stats_of(self, dve, b, tt):
        s = tt % 4
        n = b * TT + tt + 1
        dve.bn_stats(self.stats[:, s, :], self.y[tt % len(self.y)]).then_inc(self.y_stats, 1)
        hold(dve, self.y_stats, n, self.passed[2])
        dve.bn_aggr(self.mv[:, s, :], self.stats[:, s, :]).then_inc(self.y_mv, 1)
        dve.wait_ge(self.y_mv, n)
        dve.tensor_scalar(self.vare[:, s:s + 1], self.mv[:, s, 1:2], EPS, None, ALU.add).then_inc(self.y_vare, 1)

    def rsqrt(self, pool, b, tt):
        s = tt % 4
        pool.wait_ge(self.y_vare, b * TT + tt + 1)
        pool.tensor_tensor(self.rstd[:, s:s + 1], self.vare[:, s:s + 1], self.c.neg_half[:, :], ALU.pow).then_inc(self.y_rstd, 1)

    def norm(self, dve, b, tt):
        s = tt % 4
        dve.wait_ge(self.y_rstd, b * TT + tt + 1)
        if tt >= 2 and self.xn is not self.y:
            dve.wait_ge(self.out_x[tt % 2], self.loads(b, tt - 2))
            if self.xT_out is not None:
                dve.wait_ge(self.xT_psum, b * TT + tt - 1)
        dve.tensor_scalar(self.xn[tt % len(self.xn)], self.y[tt % len(self.y)], self.mv[:, s, 0:1], self.rstd[:, s:s + 1],
                          ALU.subtract, ALU.mult).then_inc(self.xn_done, 1)

    def transpose(self, pe, b, tt):
        s = tt % 2
        pe.wait_ge(self.xn_done, b * TT + tt + 1)
        slots = len(self.psT)
        if tt >= slots:
            pe.wait_ge(self.xT_done, b * TT + tt + 1 - slots)
        for k in range(KT):
            last = pe.transpose(self.psT[tt % slots][:, k * P:(k + 1) * P], self.xn[tt % len(self.xn)][:, k * P:(k + 1) * P], self.c.ident[:, :])
        last.then_inc(self.xT_psum, 1)

    def copy_T(self, act, b, tt):
        s = tt % 2
        act.wait_ge(self.xT_psum, b * TT + tt + 1)
        if tt >= 2:
            act.wait_ge(self.out_xT[s], self.loads(b, tt - 2))
        act.activation(self.xTs[s], self.psT[tt % len(self.psT)], ACT.Copy).then_inc(self.xT_done, 1)


class Consts:

    def __init__(self, nc, ctx):
        self.nc, self.sems = nc, []
        self.semaphores = ctx.enter_context(ExitStack())
        def sb(n, shape, dt=F32):
            return ctx.enter_context(nc.sbuf_tensor(n, shape, dt))

        self.ident = sb("ident", [P, P])
        self.ident_b = sb("ident_b", [P, P], BF16)
        self.tri = sb("tri", [P, P], BF16)
        self.neg_half = sb("neg_half", [P, 1])
        self.ones = sb("ones", [P, HD])
        made, tri_made = self.semaphore("consts_made"), self.semaphore("tri_made")
        with nc.Block() as block:
            @block.gpsimd
            def _(pool):
                pool.memset(self.neg_half[:, :], -0.5)
                pool.memset(self.ones[:, :], 1.0)
                pool.memset(self.tri[:, :], 0.0).then_inc(tri_made, 1)
                pool.wait_ge(tri_made, 1)
                pool.affine_select(out=self.tri[:, :], in_=self.tri[:, :], compare_op=ALU.is_ge, fill=-1e30, base=0,
                                   pattern=[[-1, P]], channel_multiplier=1)
                pool.memset(self.ident[:, :], 0.0).then_inc(made, 1)
                pool.wait_ge(made, 1)
                pool.affine_select(out=self.ident[:, :], in_=self.ident[:, :], compare_op=ALU.not_equal, fill=1.0,
                                   base=0, pattern=[[-1, P]], channel_multiplier=1).then_inc(made, 1)

            @block.vector
            def _(dve):
                dve.wait_ge(made, 2)
                dve.tensor_copy(self.ident_b[:, :], self.ident[:, :]).then_inc(made, 1)
        self.end_phase()

    def semaphore(self, name):
        self.sems.append(self.semaphores.enter_context(self.nc.semaphore(name)))
        return self.sems[-1]

    def end_phase(self):
        with self.nc.Block() as block:
            @block.sync
            def _(sp):
                for s in self.sems:
                    sp.sem_clear(s)
        self.semaphores.close()
        self.sems = []


ORD = dict(proj=(0.0, 0.0363, 0.1, 0.15), s=(0.2097, 0.93), sc=0, rows=0.9351, w=0.5782, v=(0.26, 0.36, 0.46, 0.56),
     x=0.7363, halves=((0.0, 0.34), (0.34, 0.96)), norm=(0.035, 0.0106), stc=0)
ORD_T = dict(proj=(0.0, 0.04, 0.1, 0.15), s=(0.2, 0.93), sc=60, rows=0.9302, w=0.5, v=(0.18, 0.2, 0.22, 0.25), x=0.7075,
     halves=((0.0885, 0.55), (0.55, 0.96)), norm=(0.03, 0.01), stc=60, y=(0.4021, 0.8305), yn=0.9386)


def attention_order(tail, x_next, y_next):
    at = []
    C = ORD_T if tail else ORD
    if y_next:
        chunks = [(i, h) for h in range(2) for i in range(2)]
        at += [(C["proj"][n], ("proj", i, h)) for n, (i, h) in enumerate(chunks)]
        s = [("s", j, qt, 0) for j in range(HG) for qt in range(4)]
        s += [("s", j, qt, 0) for j in range(HG) for qt in range(4, TT)]
        s += [("s", j, qt, 1) for j in range(HG) for qt in range(4, TT)]
        cost = [min(S // 2, (qt + 1) * P - c * S // 2) + C["sc"] for _, _, qt, c in s]
        at += [(C["s"][0] + (C["s"][1] - C["s"][0]) * sum(cost[:n]) / sum(cost), e) for n, e in enumerate(s)]
        at += [(C["rows"], ("rows",)), (C["w"], ("w",))]
        at += [(x, e) for x, e in zip(C["v"], (("vt", 0), ("vb", 0), ("vt", 1), ("vb", 1)))]
    if x_next:
        at += [(C["x"] + 0.05 * k, ("x", k)) for k in range(KT)]
    if tail:
        a, z = C["y"]
        step = (z - a) / TT
        for tt in range(TT):
            p = a + step * tt
            at += [(p, ("y", tt)), (p + C["yn"] * step, ("yn", tt)), (p + (C["yn"] + 0.1) * step, ("xT", tt)), (p + (C["yn"] + 1) * step, ("store", tt))]
        at += [(C["rows"] - 0.001, ("stored",))]
    for h, (a, z) in enumerate(C["halves"]):
        tiles = 4 * (h + 1)
        cost = [sum(min(S // 2, (h + 1) * S // 2 - t * P) + C["stc"] for t in range(kt)) for kt in range(tiles + 1)]
        place = [a + (z - a) * x / cost[-1] for x in cost]
        for kt in range(tiles):
            at += [(place[kt] + (place[kt + 1] - place[kt]) * j / HG, ("st", h, kt, j)) for j in range(HG)]
            at += [(place[min(kt + 2, tiles)] - 1e-4 + 1e-5 * kt, ("pv", h, kt))]
        at += [(z + 1e-3 + C["norm"][h] * p, ("norm", h, p)) for p in range(4)]
    return [e for _, e in sorted(at, key=lambda x: x[0])]


def attention_phase(nc, c, L, xT_in, x_in, wqkv, woT, bias, rope, m_scratch, x_out, xT_out):
    ctx = ExitStack()
    with ctx:
        def sb(n, shape, dt=F32):
            return ctx.enter_context(nc.sbuf_tensor(f"{L}_{n}", shape, dt))

        def sem(n):
            return c.semaphore(f"{L}_{n}")

        HS = S // 2
        NS = HG * (4 + 4 + 4)
        NCUT = HG * TT
        EXP = 2
        NPV = 12

        w_raw = sb("w_raw", [P, KT * 3 * P])
        w = [[sb(f"w_{n}{i}", [P, KT, 3, P], F32R) for n in ("hi", "lo")] for i in (0, 1)]
        xs = [sb("x_hi", [P, KT, S], F32R), sb("x_lo", [P, KT, S], F32R)]
        x_raw = sb("x_raw", [P, 2, S])
        VT = [x_raw[:, 0, h * HS:(h + 1) * HS] for h in range(2)]
        parts = [[sb(f"{n}{i}", [P, HS], F32R) for n in ("hi", "lo")] for i in (0, 1)]
        QS = [sb(f"q_stack{i}", [97, HG, S], F32R) for i in (0, 1)]
        KS = [sb(f"k_stack{i}", [97, HG, S], F32R) for i in (0, 1)]
        V = [sb(f"V{i}", [P, TT, P]) for i in (0, 1)]
        PT = sb("PT", [P, 8, HS])
        inv = sb("inv", [P, P])
        attn = sb("attn", [P, G, S])
        tail_buf = sb("tail", [P, 6, H])
        nmax, nmax_1 = sb("nmax", [P, HG, TT]), sb("nmax_1", [P, HG, TT // 2])
        nmax_T = sb("nmax_T", [HG * TT, P], F32R)
        if woT is not None:
            wo = sb("wo", [P, KT, H])
        if bias is not None:
            bias_sb = sb("bias", [P, 3 * G])
            cosT, sinT = sb("cosT", [P, S]), sb("sinT", [P, S])

        def bank(n):
            return ctx.enter_context(nc.psum_tensor(f"{L}_{n}", [P, HS], F32))

        O, SUM = bank("O"), bank("SUM")
        st_bank = [bank("st0"), bank("st1")]
        s_bank = [bank("s0"), bank("s1")]
        p_bank = [bank("p0"), bank("p1")]

        w_in, w_hi_done, w_lo_done = sem("w_in"), sem("w_hi_done"), sem("w_lo_done")
        const_in, const_done = sem("const_in"), sem("const_done")
        x_raw_in = [sem("x_raw_in0"), sem("x_raw_in1")]
        x_hi_done, x_lo_done = sem("x_hi_done"), sem("x_lo_done")
        qk_psum, qk_hi, qk_lo = sem("qk_psum"), sem("qk_hi"), sem("qk_lo")
        r_flat, r_swap, r_cos, r_sin, r_sum = (sem(n) for n in ("r_flat", "r_swap", "r_cos", "r_sin", "r_sum"))
        stacked = [sem(f"stacked{i}") for i in range(4)]
        vt_psum, vt_done, v_psum, v_done = sem("vt_psum"), sem("vt_done"), sem("v_psum"), sem("v_done")
        s_psum, max_done, row_max = sem("s_psum"), sem("max_done"), sem("row_max")
        mT_psum, mT_done, m_out, m_row = sem("mT_psum"), sem("mT_done"), sem("m_out"), sem("m_row")
        st_psum, exp_done, cut_done, pv_done = sem("st_psum"), sem("exp_done"), sem("cut_done"), sem("pv_done")
        inv_done, attn_done, y_psum = sem("inv_done"), sem("attn_done"), sem("y_psum")
        y_slots = [tail_buf[:, i, :] for i in (0, 1)]
        tail = Tail(nc, ctx, f"{L}_t", y_slots, y_slots, [tail_buf[:, i, :] for i in (2, 3)], [tail_buf[:, i, :] for i in (4, 5)],
                    [p_bank[1][:, :]], c, x_out, xT_out)

        x_rows = x_in.rearrange("(b t p) n -> b t p n", b=B, p=P)
        x_cols = xT_in.rearrange("(k p) (b s) -> b k p s", p=P, b=B)
        w_set = [[t[:, :, :, :].rearrange("p k i n -> p (k i n)") for t in s] for s in w]
        STACK_DMAS = 3 * 16

        def st_index(h, kt, j):
            return (4 * h + kt) * HG + j

        def cut_count(h, kt):
            return (kt + 1) * HG

        def s_index(j, qt, ch):
            return (qt // 4 + ch) * 4 * HG + j * 4 + qt % 4

        def each_step(eng, step):
            step(0, -1, PROLOGUE)
            for first, last in ((True, False), (False, False), (False, True)):
                def batch(b):
                    for g in range(G):
                        step(b, g, attention_order(g == 0 and not first, g == G - 2 and not last, not (last and g == G - 1)))
                if first:
                    batch(0)
                elif last:
                    batch(B - 1)
                else:
                    with eng.Fori(1, B - 1) as b:
                        batch(b)
            step(B - 1, G, EPILOGUE)

        PROLOGUE = [("w",)] + [("x", k) for k in range(KT)] + [e for e in attention_order(False, False, True) if e[0] in ("proj", "s", "rows", "vt", "vb", "w")]
        EPILOGUE = [e for e in attention_order(True, False, False) if e[0] in ("y", "yn", "xT", "store", "stored")]
        block = ctx.enter_context(nc.Block())


        @block.sync
        def _(sp):
            if woT is not None:
                sp.dma_start(wo[:, :, :], woT.rearrange("(k p) n -> p k n", p=P)).then_inc(const_in, 16)
            if bias is not None:
                sp.dma_start(bias_sb[:, :], bias).then_inc(const_in, 16)
                sp.dma_start(cosT[:, :], rope[0]).then_inc(const_in, 16)
                sp.dma_start(sinT[:, :], rope[1]).then_inc(const_in, 16)
            loaded_w = [0]

            def step(b, g, order):
                m = b * G + g + 1
                for e in order:
                    if e[0] == "w":
                        nw = loaded_w[0] if g < 0 else m + 1
                        if g < 0:
                            loaded_w[0] += 1
                        if g < 0 and nw == 0:
                            pass
                        elif isinstance(b, int) and b == B - 1 and g >= G - 2:
                            continue
                        else:
                            sp.wait_ge(w_lo_done, nw)
                        sp.dma_start(w_raw[:, :], wqkv[(g + 2) % G if g >= 0 else nw].rearrange("p k i n -> p (k i n)")).then_inc(w_in, 16)
                    elif e[0] == "x":
                        k, q = e[1], b + 1 if g >= 0 else 0
                        if k >= 2:
                            sp.wait_ge(x_lo_done, q * KT + k - 1)
                        elif g >= 0:
                            sp.wait_ge(v_psum, (m + 1) * 2)
                        sp.dma_start(x_raw[:, k % 2, :], x_cols[q, k]).then_inc(x_raw_in[k % 2], 16)
                    elif e[0] == "proj":
                        i, h = e[1:]
                        hi, lo = parts[i]
                        stack = (QS, KS)[i][(g + 1) % 2]
                        for part, done, rows in ((hi, qk_hi, ((0, 1), (0, 2))[i]), (lo, qk_lo, ((2,), (1,))[i])):
                            sp.wait_ge(done, m * 4 + 2 * h + i + 1)
                            for r in rows:
                                sp.dma_start(stack[HD * r:HD * (r + 1), :, h * HS:(h + 1) * HS].bitcast(F32),
                                             part[:, :].bitcast(F32)).then_inc(stacked[2 * h + i], 16)
                    elif e[0] == "rows":
                        sp.wait_ge(mT_done, m + 1)
                        sp.dma_start(m_scratch, nmax_T[:, :].bitcast(F32)).then_inc(m_out, 16)
                        sp.wait_ge(m_out, (m + 1) * 16)
                        sp.dma_start(QS[(g + 1) % 2][96:97, :, :].bitcast(F32),
                                     m_scratch.rearrange("(o j t) c -> o j (t c)", o=1, j=HG)).then_inc(m_row, 16)
                    elif e[0] == "y":
                        tail.load_res(sp, b - 1 + g // G, e[1], x_rows)
                    elif e[0] == "store":
                        tail.store(sp, b - 1 + g // G, e[1])
                    elif e[0] == "stored":
                        tail.wait_stored(sp, b - 1 + g // G)

            each_step(sp, step)

        @block.gpsimd
        def _(pool):
            for s in KS:
                pool.memset(s[96:97, :, :].bitcast(F32), 1.0).then_inc(const_done, 1)
            pool.wait_ge(const_done, 2)
            if bias is not None:
                pool.wait_ge(const_in, 3 * 16)
            wn = [0]

            def step(b, g, order):
                n, m = b * G + g, b * G + g + 1
                for e in order:
                    if e[0] == "w":
                        nw, s = (wn[0], wn[0] % 2) if g < 0 else (m + 1, g % 2)
                        wn[0] += 1
                        if isinstance(b, int) and b == B - 1 and g >= G - 2:
                            continue
                        pool.wait_ge(w_hi_done, nw + 1)
                        pool.tensor_tensor(w_set[s][1], w_raw[:, :], w_set[s][0].bitcast(F32), ALU.subtract).then_inc(w_lo_done, 1)
                    elif e[0] == "proj" and bias is not None:
                        i, h = e[1:]
                        swapped = x_raw[:, i, HS:S]
                        pool.wait_ge(r_swap, m * 4 + 2 * h + i + 1)
                        pool.tensor_tensor(swapped, swapped, sinT[:, h * HS:(h + 1) * HS], ALU.mult).then_inc(r_sin, 1)
                    elif e[0] == "st" and e[2] >= 4 * e[1]:
                        u = st_index(*e[1:])
                        hold(pool, exp_done, n * (EXP * NS) + EXP * (u + 1), tail.passed[1])
                        diag = PT[:, u % 8, 0:P]
                        pool.affine_select(out=diag, in_=diag, compare_op=ALU.is_ge, fill=0.0, base=0,
                                           pattern=[[1, P]], channel_multiplier=-1).then_inc(cut_done, 1)
                    elif e[0] == "y":
                        tail.rsqrt(pool, b - 1 + g // G, e[1])

            each_step(pool, step)

        @block.scalar
        def _(act):
            act.wait_ge(const_in, 16 if bias is None else 3 * 16)
            wn = [0]

            def step(b, g, order):
                n, m = b * G + g, b * G + g + 1
                for e in order:
                    if e[0] == "w":
                        nw, s = (wn[0], wn[0] % 2) if g < 0 else (m + 1, g % 2)
                        wn[0] += 1
                        if isinstance(b, int) and b == B - 1 and g >= G - 2:
                            continue
                        act.wait_ge(w_in, (nw + 1) * 16)
                        act.activation(w_set[s][0], w_raw[:, :], ACT.Copy).then_inc(w_hi_done, 1)
                    elif e[0] == "x":
                        k, q = e[1], b + 1 if g >= 0 else 0
                        act.wait_ge(x_raw_in[k % 2], (q * (KT // 2) + k // 2 + 1) * 16)
                        act.activation(xs[0][:, k, :], x_raw[:, k % 2, :], ACT.Copy).then_inc(x_hi_done, 1)
                    elif e[0] == "proj":
                        i, h = e[1:]
                        u = m * 4 + 2 * h + i
                        src = p_bank[i][:, :]
                        act.wait_ge(qk_psum, u + 1)
                        if h:
                            act.wait_ge(stacked[i], (m + 1) * STACK_DMAS)
                        if bias is not None:
                            flat = x_raw[:, i, 0:HS]
                            if h:
                                act.wait_ge(qk_lo, u - 1)
                            act.activation(flat, src, ACT.Identity, bias=bias_sb[:, i * G + (g + 1) % G:i * G + (g + 1) % G + 1]).then_inc(r_flat, 1)
                            act.wait_ge(r_sum, u + 1)
                            src = flat
                        act.activation(parts[i][0][:, :], src, ACT.Copy, scale=SCALE if i == 0 else 1.0).then_inc(qk_hi, 1)
                    elif e[0] == "vt":
                        act.wait_ge(vt_psum, m * 2 + e[1] + 1)
                        gv = 2 * G + (g + 1) % G
                        if bias is None:
                            act.activation(VT[e[1]], p_bank[1 - e[1]][:, :], ACT.Copy).then_inc(vt_done, 1)
                        else:
                            act.activation(VT[e[1]], p_bank[1 - e[1]][:, :], ACT.Identity, bias=bias_sb[:, gv:gv + 1]).then_inc(vt_done, 1)
                    elif e[0] == "rows":
                        act.wait_ge(mT_psum, m + 1)
                        act.activation(nmax_T[:, :], p_bank[0][0:HG * TT, 0:P], ACT.Copy).then_inc(mT_done, 1)
                    elif e[0] == "st":
                        u = st_index(*e[1:])
                        act.wait_ge(st_psum, n * NS + u + 1)
                        if u >= 8 and e[3] == 0:
                            act.wait_ge(pv_done, n * NPV + u // HG - 1)
                        width = min(HS, (e[1] + 1) * HS - e[2] * P)
                        act.activation(PT[:, u % 8, 0:width], st_bank[u % 2][:, 0:width], ACT.Exp).then_inc(exp_done, EXP)
                    elif e[0] == "xT":
                        tail.copy_T(act, b - 1 + g // G, e[1])

            each_step(act, step)

        @block.vector
        def _(dve):
            if bias is not None:
                dve.wait_ge(const_in, 3 * 16)

            def step(b, g, order):
                n, m = b * G + g, b * G + g + 1
                for e in order:
                    if e[0] == "x":
                        k, q = e[1], b + 1 if g >= 0 else 0
                        dve.wait_ge(x_hi_done, q * KT + k + 1)
                        dve.tensor_tensor(xs[1][:, k, :], x_raw[:, k % 2, :], xs[0][:, k, :].bitcast(F32), ALU.subtract).then_inc(x_lo_done, 1)
                    elif e[0] == "proj":
                        i, h = e[1:]
                        u = m * 4 + 2 * h + i
                        src = p_bank[i][:, :]
                        if bias is not None:
                            flat, swapped = x_raw[:, i, 0:HS], x_raw[:, i, HS:S]
                            hold(dve, r_flat, u + 1, tail.passed[2])
                            dve.stream_shuffle(swapped, flat, SWAP_HALVES).then_inc(r_swap, 1)
                            dve.wait_ge(r_swap, u + 1)
                            dve.tensor_tensor(flat, flat, cosT[:, h * HS:(h + 1) * HS], ALU.mult).then_inc(r_cos, 1)
                            dve.wait_ge(r_sin, u + 1)
                            dve.wait_ge(r_cos, u + 1)
                            dve.tensor_tensor(flat, flat, swapped, ALU.add).then_inc(r_sum, 1)
                            src = flat
                        hi, lo = parts[i]
                        dve.wait_ge(qk_hi, u + 1)
                        dve.scalar_tensor_tensor(out=lo[:, :], in0=src, scalar=SCALE if i == 0 else 1.0, in1=hi[:, :].bitcast(F32),
                                                 op0=ALU.mult, op1=ALU.subtract).then_inc(qk_lo, 1)
                    elif e[0] == "s":
                        _, j, qt, ch = e
                        u = s_index(j, qt, ch)
                        width = min(HS, (qt + 1) * P - ch * HS)
                        dst = nmax[:, j, qt:qt + 1] if ch == 0 else nmax_1[:, j, qt - 4:qt - 3]
                        dve.wait_ge(s_psum, m * NS + u + 1)
                        dve.tensor_reduce(dst, s_bank[u % 2][:, 0:width], AX.X, ALU.max, negate=True).then_inc(max_done, 1)
                    elif e[0] == "rows":
                        dve.wait_ge(max_done, (m + 1) * NS)
                        dve.tensor_tensor(nmax[:, :, 4:TT], nmax[:, :, 4:TT], nmax_1[:, :, :], ALU.min).then_inc(row_max, 1)
                    elif e[0] == "vb":
                        dve.wait_ge(v_psum, m * 2 + e[1] + 1)
                        dve.tensor_copy(V[(g + 1) % 2][:, 4 * e[1]:4 * e[1] + 4, :],
                                        p_bank[1 - e[1]][:, :].rearrange("p (t n) -> p t n", n=P)).then_inc(v_done, 1)
                    elif e[0] == "norm":
                        _, h, p = e
                        u = (n * 2 + h) * 4 + p
                        cols = slice(p * P, (p + 1) * P)
                        dve.wait_ge(pv_done, n * NPV + 4 + 8 * h)
                        if p:
                            dve.wait_ge(attn_done, u)
                        if ("y", 0) in order:
                            dve.wait_ge(y_psum, (b - 1) * TT + 4 * h + p + 1)
                        dve.reciprocal(inv[:, :], SUM[:, cols]).then_inc(inv_done, 1)
                        dve.wait_ge(inv_done, u + 1)
                        dve.tensor_tensor(attn[:, g, h * HS + p * P:h * HS + (p + 1) * P], O[:, cols], inv[:, :], ALU.mult).then_inc(attn_done, 1)
                    elif e[0] == "y":
                        dve.wait_ge(y_psum, (b - 1 + g // G) * TT + e[1] + 1)
                        tail.add_stats(dve, b - 1 + g // G, e[1], p_bank[0][:, :])
                    elif e[0] == "yn":
                        tail.norm(dve, b - 1 + g // G, e[1])

            each_step(dve, step)

        @block.tensor
        def _(pe):
            pe.wait_ge(const_done, 2)
            pe.wait_ge(const_in, 16 if bias is None else 3 * 16)

            def step(b, g, order):
                n, m = b * G + g, b * G + g + 1
                has_tail = ("y", 0) in order
                bt = b - 1 + g // G
                set_y, set_x = (g + 1) % 2, g % 2

                def project(out, i, h):
                    for t, (a, d) in enumerate(TERMS):
                        for k in range(KT):
                            last = pe.matmul(out[:, :], w[set_y][a][:, k, i, :], xs[d][:, k, h * HS:(h + 1) * HS],
                                             start=(t == 0 and k == 0), stop=(t == 2 and k == KT - 1))
                    return last

                for e in order:
                    if e[0] == "proj":
                        i, h = e[1:]
                        if h == 0 and i == 0:
                            pe.wait_ge(w_lo_done, m + 1)
                            pe.wait_ge(x_lo_done, (b + (g + 1) // G + 1) * KT)
                        if h:
                            pe.wait_ge(qk_lo, m * 4 + i + 1)
                        elif g >= 0 and i == 0:
                            pe.wait_ge(mT_done, m)
                        elif g >= 0:
                            pe.wait_ge(v_done, m * 2)
                            if g == 1 and not (isinstance(b, int) and b == 0):
                                pe.wait_ge(tail.xT_done, b * TT)
                        project(p_bank[i], i, h).then_inc(qk_psum, 1)
                    elif e[0] == "vt":
                        pe.wait_ge(qk_lo, m * 4 + 4 - e[1])
                        project(p_bank[1 - e[1]], 2, e[1]).then_inc(vt_psum, 1)
                    elif e[0] == "vb":
                        pe.wait_ge(vt_done, m * 2 + e[1] + 1)
                        for t in range(4):
                            last = pe.transpose(p_bank[1 - e[1]][:, t * P:(t + 1) * P], VT[e[1]][:, t * P:(t + 1) * P], c.ident[:, :])
                        last.then_inc(v_psum, 1)
                    elif e[0] == "s":
                        _, j, qt, ch = e
                        u = s_index(j, qt, ch)
                        width = min(HS, (qt + 1) * P - ch * HS)
                        if j == 0 and qt % 4 == 0:
                            for r in ((0, 1), (2,), (3,))[qt // 4 + ch]:
                                pe.wait_ge(stacked[r], (m + 1) * STACK_DMAS)
                        if u >= 2:
                            pe.wait_ge(max_done, m * NS + u - 1)
                        last = pe.matmul(s_bank[u % 2][:, 0:width], QS[set_y][0:96, j, qt * P:(qt + 1) * P],
                                         KS[set_y][0:96, j, ch * HS:ch * HS + width], start=True, stop=True)
                        if qt // 4 == ch:
                            last = pe.matmul(s_bank[u % 2][:, width - P:width], c.ident_b[:, :], c.tri[:, :], start=False, stop=True,
                                             skip_group_check=True)
                        last.then_inc(s_psum, 1)
                    elif e[0] == "rows":
                        pe.wait_ge(row_max, m + 1)
                        if has_tail:
                            pe.wait_ge(tail.y_sum, (bt + 1) * TT)
                        else:
                            pe.wait_ge(v_done, m * 2 + 2)
                        pe.transpose(p_bank[0][0:HG * TT, 0:P], nmax[:, :, :].rearrange("p j t -> p (j t)"), c.ident[:, :]).then_inc(mT_psum, 1)
                    elif e[0] == "st":
                        _, h, kt, j = e
                        u = st_index(h, kt, j)
                        if u == 0:
                            pe.wait_ge(m_row, (n + 1) * 16)
                        if u >= 2:
                            pe.wait_ge(exp_done, n * (EXP * NS) + EXP * (u - 1))
                        q0 = max(h * HS, kt * P)
                        pe.matmul(st_bank[u % 2][:, 0:(h + 1) * HS - q0], KS[set_x][0:97, j, kt * P:(kt + 1) * P],
                                  QS[set_x][0:97, j, q0:(h + 1) * HS], start=True, stop=True).then_inc(st_psum, 1)
                    elif e[0] == "pv":
                        _, h, kt = e
                        if kt == 0:
                            if h:
                                pe.wait_ge(attn_done, n * 8 + 4)
                            else:
                                pe.wait_ge(v_done, (n + 1) * 2)
                                if not (isinstance(b, int) and b * G + g == 0):
                                    pe.wait_ge(attn_done, n * 8)
                        if kt >= 4 * h:
                            pe.wait_ge(cut_done, n * NCUT + cut_count(h, kt))
                        else:
                            pe.wait_ge(exp_done, n * (EXP * NS) + EXP * (st_index(h, kt, HG - 1) + 1))
                        q0 = max(0, kt * P - h * HS)
                        for out in (O, SUM):
                            for j in range(HG):
                                stat = V[set_x][:, kt, HD * j:HD * (j + 1)] if out is O else c.ones[:, :]
                                last = pe.matmul(out[HD * j:HD * (j + 1), q0:HS], stat, PT[:, st_index(h, kt, j) % 8, 0:HS - q0],
                                                 start=(kt == 0), stop=(kt == 4 * h + 3), tile_position=(0, HD * j))
                        last.then_inc(pv_done, 1)
                    elif e[0] == "y":
                        tt = e[1]
                        if tt == 0:
                            if g < G:
                                pe.wait_ge(v_done, m * 2 + 2)
                            pe.wait_ge(attn_done, (bt + 1) * G * 8)
                        else:
                            pe.wait_ge(tail.y_sum, bt * TT + tt)
                        for k in range(KT):
                            col = attn[:, k, tt * P:(tt + 1) * P]
                            if woT is not None:
                                last = pe.matmul(p_bank[0][:, :], col, wo[:, k, :], start=(k == 0), stop=(k == KT - 1))
                            else:
                                last = pe.transpose(p_bank[0][:, k * P:(k + 1) * P], col, c.ident[:, :])
                        last.then_inc(y_psum, 1)
                    elif e[0] == "xT":
                        if e[1] == 0 and g < G:
                            pe.wait_ge(v_done, m * 2 + 1)
                        tail.transpose(pe, bt, e[1])

            each_step(pe, step)


def ffn_phase(nc, c, xT_in, x_in, wg, wu, wd, x_out, xT_out):
    GT, NB = FFN // (4 * P), S // 512
    NU = GT * NB
    HALF = (slice(0, 256), slice(256, 512))
    NCMP = 3 + 2 * 3
    ctx = ExitStack()
    with ctx:
        def sb(n, shape, dt=F32):
            return ctx.enter_context(nc.sbuf_tensor(f"f_{n}", shape, dt))

        def sem(n):
            return c.semaphore(f"f_{n}")

        part_raw = sb("part_raw", [P, 2, KT * 512])
        xs = [[sb(f"x_{n}{i}", [P, KT, 512], F32R) for n in ("hi", "lo")] for i in range(NB)]
        gate = [[sb(f"gate_{n}{i}", [P, KT, 4, P], F32R) for n in ("hi", "lo")] for i in (0, 1)]
        up = [[sb(f"up_{n}{i}", [P, KT, 4, P], F32R) for n in ("hi", "lo")] for i in (0, 1)]
        down = [sb(f"down_{n}", [P, 4, H], F32R) for n in ("hi", "lo")]
        y = sb("y", [P, TT, H])
        sg = sb("silu_gate", [P, 4, 512])
        h = [sb(f"h{i}", [P, 4, 512]) for i in (0, 1)]
        h_parts = [sb(f"h_{n}", [P, 4, 512], F32R) for n in ("hi", "lo")]
        mag = sb("mag", [P, 4, 512])
        cmp = sb("cmp", [P, 6, 512], BF16)
        pair = sb("pair", [P, 4, 512], BF16)
        wins = pair
        xT_buf = sb("xT_buf", [P, 2, H])
        GU = [[ctx.enter_context(nc.psum_tensor(f"f_{n}{i}", [P, 512], F32)) for n in ("gate", "up")] for i in (0, 1)]
        D = [ctx.enter_context(nc.psum_tensor(f"f_D{i}", [P, H], F32)) for i in range(4)]

        part_in = [sem("part_in0"), sem("part_in1")]
        hi_done, lo_done = sem("hi_done"), sem("lo_done")
        y_in = [sem(f"y_in{i}") for i in range(NB)]
        gu_psum, silu_done, h_done, mag_done = sem("gu_psum"), sem("silu_done"), sem("h_done"), sem("mag_done")
        cmp_done, pair_done, wins_done, keep_done = sem("cmp_done"), sem("pair_done"), sem("wins_done"), sem("keep_done")
        h_hi_done, h_lo_done, d_psum, sum_done = sem("h_hi_done"), sem("h_lo_done"), sem("d_psum"), sem("sum_done")
        y_tiles = [y[:, t, :] for t in range(TT)]
        tail = Tail(nc, ctx, "f_t", None, y_tiles, y_tiles, [xT_buf[:, i, :] for i in (0, 1)],
                    [D[i][:, :] for i in range(4)], c, x_out, xT_out)

        x_rows = x_in.rearrange("(b i t p) n -> b i p t n", b=B, i=NB, p=P)
        x_cols = xT_in.rearrange("(k p) (b i s) -> b i p k s", p=P, b=B, i=NB)

        FIRST_PARTS = [(0, "x", 0), (0, "gate", 0), (0, "up", 0)]

        def parts(last):
            p = [(0, "x", 1), (0, "gate", 1), (0, "down", 0), (1, "up", 1)]
            for gt in range(1, GT):
                if gt + 1 < GT or not last:
                    p.append((2 * gt, "gate", (gt + 1) % GT))
                p.append((2 * gt, "down", gt))
                if gt + 1 < GT or not last:
                    p.append((2 * gt + 1, "up", (gt + 1) % GT))
            return p if last else p + [(NU - 1, "x", 0)]

        NP = len(parts(False))

        def part_number(b, q, last):
            return b * NP + len(FIRST_PARTS) + parts(last).index(q)

        def slot_of(i):
            return (len(FIRST_PARTS) + i) % 2

        def slot_count(b, i):
            return b * (NP // 2 * 16) + ((len(FIRST_PARTS) + i) // 2 + 1) * 16

        def split_to(q):
            _, kind, i = q
            if kind == "x":
                return [t[:, :, :].rearrange("p k s -> p (k s)") for t in xs[i]]
            if kind == "down":
                return [t[:, :, :].rearrange("p j n -> p (j n)") for t in down]
            return [t[:, :, :, :].rearrange("p k j m -> p (k j m)") for t in (gate if kind == "gate" else up)[i % 2]]

        def part_dram(b, q):
            _, kind, i = q
            if kind == "x":
                return x_cols[b if i else b + 1, i]
            return wd[i] if kind == "down" else (wg if kind == "gate" else wu)[i].rearrange("p k j m -> p k (j m)")

        def raw(slot):
            return part_raw[:, slot, :].rearrange("p (k n) -> p k n", k=KT)

        def count(b, u, per, more=0):
            return b * (NU * per) + (u * per + more)

        def each_step(eng, step):
            def batch(b, first, last):
                for u in range(NU):
                    step(b, u, True, not first or u > 0, first, last)

            batch(0, True, False)
            with eng.Fori(1, B - 1) as b:
                batch(b, False, False)
            batch(B - 1, False, True)
            step(B, 0, False, True, False, False)
            step(B, 1, False, False, False, False)

        def is_at(n, b, u, first):
            return not first or u >= n

        block = ctx.enter_context(nc.Block())


        @block.sync
        def _(sp):
            def load_first(i):
                _, kind, _ = FIRST_PARTS[i]
                if i >= 2:
                    sp.wait_ge(lo_done, i - 1)
                src = x_cols[0, 0] if kind == "x" else (wg if kind == "gate" else wu)[0].rearrange("p k j m -> p k (j m)")
                sp.dma_start(raw(i % 2), src).then_inc(part_in[i % 2], 16)

            def load(b, i, last):
                ps = parts(last)
                if i < len(ps):
                    sp.wait_ge(lo_done, b * NP + len(FIRST_PARTS) + i - 1)
                    sp.dma_start(raw(slot_of(i)), part_dram(b, ps[i])).then_inc(part_in[slot_of(i)], 16)

            def load_y(b, blk):
                sp.dma_start(y[:, 4 * blk:4 * blk + 4, :], x_rows[b, blk]).then_inc(y_in[blk], 16)

            for i in range(len(FIRST_PARTS)):
                load_first(i)
            load_y(0, 0)
            load_y(0, 1)
            load(0, 0, False)
            load(0, 1, False)

            def step(b, u, new, old, first, last):
                if u < NB and not first:
                    for tt in range(4 * u, 4 * u + 4):
                        tail.store(sp, b - 1, tt)
                    if new:
                        for s in (0, 1):
                            sp.wait_ge(tail.out_x[s], tail.loads(b - 1, 4 * u + 2))
                        load_y(b, u)
                    if u == NB - 1:
                        tail.wait_stored(sp, b - 1)
                if new:
                    for i, q in enumerate(parts(last)):
                        if q[0] == u:
                            if i + 2 < len(parts(last)):
                                load(b, i + 2, last)
                            elif not last:
                                load(b + 1, i + 2 - NP, False)

            each_step(sp, step)

        @block.gpsimd
        def _(pool):
            def split_lo(q, slot, n):
                pool.wait_ge(hi_done, n + 1)
                hi, lo = split_to(q)
                pool.tensor_tensor(lo, part_raw[:, slot, :], hi.bitcast(F32), ALU.subtract).then_inc(lo_done, 1)

            for n, q in enumerate(FIRST_PARTS):
                split_lo(q, n % 2, n)

            def step(b, u, new, old, first, last):
                mine = [(i, q) for i, q in enumerate(parts(last)) if q[0] == u] if new else []
                for i, q in mine:
                    if q[1] != "down":
                        split_lo(q, slot_of(i), part_number(b, q, last))
                if u == NU - 1:
                    for tt in range(4):
                        tail.rsqrt(pool, b, tt)
                if u == 0 and not first:
                    for tt in range(4, TT):
                        tail.rsqrt(pool, b - 1, tt)
                for i, q in mine:
                    if q[1] == "down":
                        split_lo(q, slot_of(i), part_number(b, q, last))

            each_step(pool, step)

        @block.scalar
        def _(act):
            for n, q in enumerate(FIRST_PARTS):
                act.wait_ge(part_in[n % 2], 16 * (n // 2 + 1))
                act.activation(split_to(q)[0], part_raw[:, n % 2, :], ACT.Copy).then_inc(hi_done, 1)

            def split_hi(b, u, kinds, first, last):
                for i, q in enumerate(parts(last)):
                    if q[0] == u and q[1] in kinds:
                        act.wait_ge(part_in[slot_of(i)], slot_count(b, i))
                        act.activation(split_to(q)[0], part_raw[:, slot_of(i), :], ACT.Copy).then_inc(hi_done, 1)

            def silu(b, u, j, first):
                act.wait_ge(gu_psum, count(b, u, 4, j + 1))
                if is_at(1, b, u, first):
                    act.wait_ge(h_done, count(b, u - 1, 4, j + 1))
                act.activation(sg[:, j, :], GU[j % 2][0][:, :], ACT.Silu).then_inc(silu_done, 1)

            def magnitude(b, u, j, first):
                act.wait_ge(h_done, count(b, u, 4, j + 1))
                if j == 0 and is_at(1, b, u, first):
                    act.wait_ge(cmp_done, count(b, u, NCMP))
                act.activation(mag[:, j, :], h[u % 2][:, j, :], ACT.Abs).then_inc(mag_done, 1)

            def split_h(b, u, half, first):
                at = HALF[half]
                act.wait_ge(keep_done, count(b, u - 1, 8, 4 * (half + 1)))
                if is_at(2, b, u, first):
                    act.wait_ge(d_psum, count(b, u - 1, 4))
                act.activation(h_parts[0][:, :, at], h[(u - 1) % 2][:, :, at], ACT.Copy).then_inc(h_hi_done, 1)

            def step(b, u, new, old, first, last):
                blk_done = u < NB and not first
                if u == 0 and new:
                    if not first:
                        act.wait_ge(gu_psum, count(b, 0, 4))
                    split_hi(b, u, ("x",), first, last)
                if new:
                    silu(b, u, 0, first)
                if old:
                    split_h(b, u, 0, first)
                for tt in range(4 * u, 4 * u + 2) if blk_done else ():
                    tail.copy_T(act, b - 1, tt)
                if new:
                    silu(b, u, 1, first)
                if old:
                    split_h(b, u, 1, first)
                for tt in range(4 * u + 2, 4 * u + 4) if blk_done else ():
                    tail.copy_T(act, b - 1, tt)
                if new:
                    magnitude(b, u, 0, first)
                    magnitude(b, u, 1, first)
                    if u:
                        act.wait_ge(gu_psum, count(b, u, 4))
                    split_hi(b, u, ("gate", "up") if u == 0 else ("gate", "up", "x"), first, last)
                    silu(b, u, 2, first)
                    magnitude(b, u, 2, first)
                    if u % NB == 0:
                        if old:
                            act.wait_ge(d_psum, count(b, u, 4))
                        split_hi(b, u, ("down",), first, last)
                    silu(b, u, 3, first)
                    magnitude(b, u, 3, first)

            each_step(act, step)

        @block.vector
        def _(dve):
            def mul(b, u, j, first):
                if j == 0 and is_at(2, b, u, first):
                    dve.wait_ge(h_lo_done, count(b, u - 1, 2))
                dve.wait_ge(silu_done, count(b, u, 4, j + 1))
                dve.tensor_tensor(h[u % 2][:, j, :], sg[:, j, :], GU[j % 2][1][:, :], ALU.mult).then_inc(h_done, 1)

            def add(b, u, first):
                blk = (u - 1) % NB
                for t in range(4):
                    tt = blk * 4 + t
                    if u == 1 or u == 2:
                        dve.wait_ge(y_in[blk], b * 16 + 16)
                    else:
                        dve.wait_ge(sum_done, count(b, u - 1 - NB, 4, t + 1))
                    dve.wait_ge(d_psum, count(b, u - 1, 4, t + 1))
                    dve.tensor_tensor(y[:, tt, :], D[t][:, :], y[:, tt, :], ALU.add).then_inc(sum_done, 1)
                    if u == NU - 1 or u == 0:
                        dve.wait_ge(sum_done, count(b, u - 1, 4, t + 1))
                        tail.stats_of(dve, b if u else b - 1, tt)

            def compare(b, u, i, j, at, slot):
                dve.wait_ge(mag_done, count(b, u, 4, j + 1))
                dve.tensor_tensor(cmp[:, slot, at], mag[:, i, at], mag[:, j, at], ALU.is_ge).then_inc(cmp_done, 1)

            def choose(b, u, half):
                at, hu = HALF[half], h[u % 2]
                compare(b, u, 0, 3, at, 4)
                compare(b, u, 1, 3, at, 3)
                compare(b, u, 2, 3, at, 1)
                dve.wait_ge(cmp_done, count(b, u, NCMP, 3 + 3 * (half + 1)))
                dve.tensor_tensor(pair[:, 0:2, at], cmp[:, 2:4, at], cmp[:, 4:6, at], ALU.add).then_inc(pair_done, 1)
                dve.tensor_tensor(pair[:, 2:4, at], cmp[:, 2:5:2, at], cmp[:, 5:2:-2, at], ALU.add).then_inc(pair_done, 1)
                dve.wait_ge(pair_done, count(b, u, 4, 2 * (half + 1)))
                dve.tensor_tensor(wins[:, 0, at], pair[:, 0, at], cmp[:, 0, at], ALU.add).then_inc(wins_done, 1)
                dve.tensor_tensor(wins[:, 1, at], pair[:, 1, at], cmp[:, 0, at], ALU.subtract).then_inc(wins_done, 1)
                dve.tensor_tensor(wins[:, 2, at], cmp[:, 1, at], pair[:, 2, at], ALU.subtract).then_inc(wins_done, 1)
                dve.tensor_tensor(wins[:, 3, at], cmp[:, 1, at], pair[:, 3, at], ALU.add).then_inc(wins_done, 1)
                dve.wait_ge(wins_done, count(b, u, 8, 4 * (half + 1)))
                for j, (op, bound) in enumerate(((ALU.is_ge, 2.0), (ALU.is_ge, 1.0), (ALU.is_ge, 0.0), (ALU.is_le, 1.0))):
                    dve.scalar_tensor_tensor(out=hu[:, j, at], in0=wins[:, j, at], scalar=bound, in1=hu[:, j, at],
                                             op0=op, op1=ALU.mult).then_inc(keep_done, 1)

            def split_lo(b, u, half):
                at, hu = HALF[half], h[u % 2]
                dve.wait_ge(h_hi_done, count(b, u, 2, half + 1))
                dve.tensor_tensor(h_parts[1][:, :, at], hu[:, :, at], h_parts[0][:, :, at].bitcast(F32),
                                  ALU.subtract).then_inc(h_lo_done, 1)

            def step(b, u, new, old, first, last):
                if old:
                    choose(b, u - 1, 0)
                if new:
                    mul(b, u, 0, first)
                if old:
                    choose(b, u - 1, 1)
                    split_lo(b, u - 1, 0)
                if new:
                    mul(b, u, 1, first)
                if old:
                    split_lo(b, u - 1, 1)
                if new:
                    mul(b, u, 2, first)
                    compare(b, u, 0, 1, slice(0, 512), 0)
                    compare(b, u, 0, 2, slice(0, 512), 2)
                    compare(b, u, 1, 2, slice(0, 512), 5)
                if old:
                    add(b, u, first)
                done = (b, range(4)) if u == NU - 1 else (b - 1, range(4, TT)) if u == 0 and not first else None
                for tt in done[1][:2] if done else ():
                    tail.norm(dve, done[0], tt)
                if new:
                    mul(b, u, 3, first)
                for tt in done[1][2:] if done else ():
                    tail.norm(dve, done[0], tt)

            each_step(dve, step)

        @block.tensor
        def _(pe):
            def gate_up_products(b, u, j, first, last):
                s, blk = (u // NB) % 2, u % NB
                if j >= 2:
                    pe.wait_ge(h_done, count(b, u, 4, j - 1))
                elif is_at(1, b, u, first):
                    pe.wait_ge(h_done, count(b, u - 1, 4, j + 3))
                for a, weights in enumerate((gate, up)):
                    if j == 0:
                        if first and u == 0:
                            pe.wait_ge(lo_done, 2 + a)
                        elif u == 0 and a == 0:
                            pe.wait_ge(lo_done, b * NP + len(FIRST_PARTS))
                        elif u == 1 and a == 0:
                            pe.wait_ge(lo_done, part_number(b, (0, "x", 1), last) + 1)
                        elif u % NB == 0 and u:
                            q = (u - 2 + a, ("gate", "up")[a], u // NB)
                            pe.wait_ge(lo_done, part_number(b, q, last) + 1)
                    for t, (i, d) in enumerate(TERMS):
                        for k in range(KT):
                            last_mm = pe.matmul(GU[j % 2][a][:, :], weights[s][i][:, k, j, :], xs[blk][d][:, k, :],
                                                start=(t == 0 and k == 0), stop=(t == 2 and k == KT - 1))
                last_mm.then_inc(gu_psum, 1)

            def down_products(b, u, first, last):
                if u % NB == 1:
                    pe.wait_ge(lo_done, part_number(b, (u - 1, "down", u // NB), last) + 1)
                for tt in range(4):
                    pe.wait_ge(h_lo_done, count(b, u - 1, 2, tt // 2 + 1))
                    if u < NB and not first:
                        pe.wait_ge(tail.xT_done, b * TT + (u * 4 - TT + tt + 1))
                    elif is_at(2, b, u, first):
                        pe.wait_ge(sum_done, count(b, u - 2, 4, tt + 1))
                    for t, (i, d) in enumerate(TERMS):
                        for j in range(4):
                            last_mm = pe.matmul(D[tt][:, :], h_parts[i][:, j, tt * P:(tt + 1) * P], down[d][:, j, :],
                                                start=(t == 0 and j == 0), stop=(t == 2 and j == 3))
                    last_mm.then_inc(d_psum, 1)

            def step(b, u, new, old, first, last):
                blk_done = u < NB and not first
                if new:
                    gate_up_products(b, u, 0, first, last)
                for tt in range(4 * u, 4 * u + 2) if blk_done else ():
                    tail.transpose(pe, b - 1, tt)
                if new:
                    gate_up_products(b, u, 1, first, last)
                for tt in range(4 * u + 2, 4 * u + 4) if blk_done else ():
                    tail.transpose(pe, b - 1, tt)
                if new:
                    gate_up_products(b, u, 2, first, last)
                if old:
                    down_products(b, u, first, last)
                if new:
                    gate_up_products(b, u, 3, first, last)

            each_step(pe, step)


def moe_phase(nc, c, xT_in, x_in, ew, rw, eb, rb, same_expert, earlier_chunk, chunk_of, out):
    NT, NC = T // P, P // NE
    R = NT // NC
    W = R * P
    HALVES = [1 << n for n in range(W.bit_length() - 1)]
    ctx = ExitStack()
    with ctx:
        def sb(n, shape, dt=F32):
            return ctx.enter_context(nc.sbuf_tensor(f"m_{n}", shape, dt))

        def sem(n):
            return c.semaphore(f"m_{n}")

        w_raw, w = sb("w_raw", [P, KT, H]), [sb("w_hi", [P, KT, H], F32R), sb("w_lo", [P, KT, H], F32R)]
        rw_sb, rb_sb, eb_sb = sb("rw", [P, KT, NE]), sb("rb", [P, NE]), sb("eb", [P, H])
        same_sb, earlier_sb, chunk_sb = sb("same", [P, P]), sb("earlier", [P, P]), sb("chunk", [P, NC])
        raw = sb("raw", [P, 2, KT, W])
        xs = [sb("x_hi", [P, KT, W * 2], F32R), sb("x_lo", [P, KT, W * 2], F32R)]
        z = sb("z", [P, NT, H])
        logits, e = sb("logits", [P, NT, NE]), sb("e", [P, NT, NE])
        row = sb("row", [P, 2, NT])
        probs = sb("probs", [P, R, NC, NE])
        ST = sb("ST", [P, W])
        junk, eq = sb("junk", [P, W]), sb("eq", [P, W])
        pre = [sb("pre0", [P, W]), sb("pre1", [P, W])]
        thr, cand, taken = sb("thr", [P, 1], I32), sb("cand", [P, 1], I32), sb("taken", [P, 1])
        bit = sb("bit", [P, 1], I32)
        cnt, need = sb("cnt", [P, 3]), sb("need", [P, 2])
        gates = sb("gates", [P, NT])
        tail_slots = [[w_raw[:, 2 * i + j, :] for j in (0, 1)] for i in (0, 1)] + [[raw[:, 0, j, :] for j in (0, 1)], None]
        psL = [ctx.enter_context(nc.psum_tensor(f"m_psL{i}", [P, R, NE], F32)) for i in (0, 1)]
        psZ = [ctx.enter_context(nc.psum_tensor(f"m_psZ{i}", [P, H], F32)) for i in (0, 1)]
        psT = ctx.enter_context(nc.psum_tensor("m_psT", [P, W], F32))
        psC = ctx.enter_context(nc.psum_tensor("m_psC", [P, 4], F32))
        psG = ctx.enter_context(nc.psum_tensor("m_psG", [P, R, NC], F32))

        small_in, w_in, w_hi_done, w_lo_done = sem("small_in"), sem("w_in"), sem("w_hi_done"), sem("w_lo_done")
        raw_in = [sem("raw_in0"), sem("raw_in1")]
        l_psum, l_done = sem("l_psum"), sem("l_done")
        step = sem("softmax_step")
        exp_done, t_psum, st_done = sem("exp_done"), sem("t_psum"), sem("st_done")
        x_hi_done, x_lo_done, z_psum, z_done = sem("x_hi_done"), sem("x_lo_done"), sem("z_psum"), sem("z_done")
        cand_done, cnt_done, cnt_psum, taken_done, thr_done = (sem(n) for n in ("cand_done", "cnt_done", "cnt_psum", "taken_done", "thr_done"))
        bit_done = sem("bit_done")
        tie_cnt, tie_psum, tie = sem("tie_cnt"), sem("tie_psum"), sem("tie_step")
        g_in, g_psum, g_done = sem("g_in"), sem("g_psum"), sem("g_done")
        tail = Tail(nc, ctx, "m_t", *tail_slots, None, c, out, None)

        x_rows = x_in.rearrange("(b t p) n -> b t p n", b=B, p=P)
        x_cols = xT_in.rearrange("(k p) (c s) -> c p k s", p=P, c=NC)
        w_flat = [t[:, :, :].rearrange("p k n -> p (k n)") for t in w]
        BC = NC // B
        block = ctx.enter_context(nc.Block())

        @block.sync
        def _(sp):
            sp.dma_start(rw_sb[:, :, :], rw.rearrange("(k p) n -> p k n", p=P)).then_inc(small_in, 16)
            sp.dma_start(rb_sb[:, :], rb.partition_broadcast(P)).then_inc(small_in, 16)
            sp.dma_start(eb_sb[:, :], eb.partition_broadcast(P)).then_inc(small_in, 16)
            sp.dma_start(same_sb[:, :], same_expert).then_inc(small_in, 16)
            sp.dma_start(earlier_sb[:, :], earlier_chunk).then_inc(small_in, 16)
            sp.dma_start(chunk_sb[:, :], chunk_of).then_inc(small_in, 16)
            sp.dma_start(w_raw[:, :, :], ew.rearrange("(k p) n -> p k n", p=P)).then_inc(w_in, 16)
            with sp.Fori(0, B) as b:
                for i in range(BC):
                    sp.wait_ge(l_psum, b * BC + i + 1)
                    sp.dma_start(raw[:, i, :, :], x_cols[b * BC + i]).then_inc(raw_in[i], 16)
            with sp.Fori(0, B) as b:
                for i in range(BC):
                    if i == 0:
                        sp.wait_ge(l_psum, NC + 2)
                    sp.wait_ge(x_lo_done, b * BC + i + 1)
                    sp.dma_start(raw[:, i, :, :], x_cols[b * BC + i]).then_inc(raw_in[i], 16)
            sp.wait_ge(g_done, 1)
            with sp.Fori(0, B) as b:
                for tt in range(TT + 2):
                    if tt < TT:
                        tail.load_res(sp, b, tt, x_rows)
                    if tt >= 2:
                        tail.store(sp, b, tt - 2)
                tail.wait_stored(sp, b)

        @block.gpsimd
        def _(pool):
            with pool.Fori(0, B) as b:
                for tt in range(TT):
                    tail.rsqrt(pool, b, tt)

        @block.scalar
        def _(act):
            act.wait_ge(w_in, 16)
            act.activation(w_flat[0], w_raw[:, :, :].rearrange("p k n -> p (k n)"), ACT.Copy).then_inc(w_hi_done, 1)
            act.wait_ge(step, 2)
            act.activation(e[:, :, :], logits[:, :, :], ACT.Exp).then_inc(exp_done, 1)
            act.wait_ge(t_psum, 1)
            act.activation(ST[:, :], psT[:, :], ACT.Copy).then_inc(st_done, 1)
            with act.Fori(0, B) as b:
                for i in range(BC):
                    act.wait_ge(raw_in[i], (B + b + 1) * 16)
                    if i == 0:
                        act.wait_ge(z_psum, b * TT + 1)
                    act.activation(xs[0][:, :, i * W:(i + 1) * W], raw[:, i, :, :], ACT.Copy).then_inc(x_hi_done, 1)

        @block.vector
        def _(dve):
            dve.wait_ge(w_hi_done, 1)
            dve.tensor_tensor(w_flat[1], w_raw[:, :, :].rearrange("p k n -> p (k n)"), w_flat[0].bitcast(F32),
                              ALU.subtract).then_inc(w_lo_done, 1)
            dve.memset(thr[:, :], 0).then_inc(thr_done, 1)
            dve.memset(bit[:, :], 1 << 30).then_inc(bit_done, 1)
            dve.memset(junk[:, 0:1], 0.0).then_inc(l_psum, 2)
            dve.memset(junk[:, 1:2], 0.0).then_inc(x_lo_done, 2)
            dve.memset(junk[:, 2:3], 0.0).then_inc(l_done, 2)
            dve.wait_ge(small_in, 6 * 16)
            with dve.Fori(0, B) as b:
                for i in range(BC):
                    dve.wait_ge(l_psum, b * BC + i + 3)
                    dve.tensor_tensor(logits[:, bass.ds(b * BC * R + i * R, R), :], psL[i][:, :, :],
                                      rb_sb[:, :].unsqueeze(1).to_broadcast([P, R, NE]), ALU.add).then_inc(l_done, 1)
            dve.wait_ge(l_done, NC + 2)
            dve.tensor_reduce(row[:, 0, :], logits[:, :, :], AX.X, ALU.max).then_inc(step, 1)
            dve.wait_ge(step, 1)
            dve.tensor_tensor(logits[:, :, :], logits[:, :, :], row[:, 0, :].unsqueeze(2).to_broadcast([P, NT, NE]),
                              ALU.subtract).then_inc(step, 1)
            dve.wait_ge(exp_done, 1)
            dve.tensor_reduce(row[:, 1, :], e[:, :, :], AX.X, ALU.add).then_inc(step, 1)
            dve.wait_ge(step, 3)
            dve.reciprocal(row[:, 0, :], row[:, 1, :]).then_inc(step, 1)
            dve.wait_ge(step, 4)
            dve.tensor_tensor(probs[:, :, :, :].rearrange("p r c e -> p c r e"),
                              e[:, :, :].rearrange("p (c r) e -> p c r e", c=NC),
                              row[:, 0, :].rearrange("p (c r) -> p c r", c=NC).unsqueeze(3).to_broadcast([P, NC, R, NE]),
                              ALU.mult).then_inc(step, 1)
            dve.wait_ge(st_done, 1)
            with dve.Fori(0, B) as b:
                for i in range(BC):
                    dve.wait_ge(x_hi_done, b * BC + i + 1)
                    dve.tensor_tensor(xs[1][:, :, i * W:(i + 1) * W], raw[:, i, :, :],
                                      xs[0][:, :, i * W:(i + 1) * W].bitcast(F32), ALU.subtract).then_inc(x_lo_done, 1)
                for tt in range(TT):
                    n = b * TT + tt
                    dve.wait_ge(thr_done, n + 1)
                    dve.wait_ge(bit_done, n + 1)
                    dve.tensor_tensor(cand[:, :], thr[:, :], bit[:, :], ALU.bitwise_or).then_inc(cand_done, 1)
                    dve.wait_ge(cand_done, n + 1)
                    dve.tensor_scalar(bit[:, :], bit[:, :], 1, None, ALU.logical_shift_right).then_inc(bit_done, 1)
                    dve.tensor_scalar(junk[:, :], ST[:, :], cand[:, :].bitcast(F32), None, ALU.is_ge, ALU.add,
                                      accum_out=cnt[:, 0:1]).then_inc(cnt_done, 1)
                    dve.wait_ge(z_psum, n + 2)
                    dve.tensor_tensor(z[:, bass.ds(b * TT + tt, 1), :].rearrange("p a n -> p (a n)"), psZ[tt % 2][:, :], eb_sb[:, :],
                                      ALU.add).then_inc(z_done, 1)
                    dve.wait_ge(cnt_psum, n + 1)
                    dve.scalar_tensor_tensor(out=taken[:, :], in0=psC[:, 0:1], scalar=TOPK - 0.5, in1=cand[:, :].bitcast(F32),
                                             op0=ALU.is_ge, op1=ALU.mult).then_inc(taken_done, 1)
                    dve.wait_ge(taken_done, n + 1)
                    dve.tensor_tensor(thr[:, :].bitcast(F32), thr[:, :].bitcast(F32), taken[:, :], ALU.max).then_inc(thr_done, 1)
            dve.wait_ge(thr_done, NT + 1)
            t = thr[:, :].bitcast(F32)
            dve.tensor_scalar(junk[:, :], ST[:, :], t, None, ALU.is_gt, ALU.add, accum_out=cnt[:, 1:2]).then_inc(tie_cnt, 1)
            dve.tensor_scalar(eq[:, :], ST[:, :], t, None, ALU.is_equal, ALU.add, accum_out=cnt[:, 2:3]).then_inc(tie_cnt, 1)
            dve.wait_ge(tie_cnt, 2)
            src = eq
            for s, d in enumerate(HALVES):
                dst = pre[s % 2]
                dve.tensor_tensor(dst[:, d:W], src[:, d:W], src[:, 0:W - d], ALU.add).then_inc(tie, 1)
                dve.tensor_copy(dst[:, 0:d], src[:, 0:d]).then_inc(tie, 1)
                dve.wait_ge(tie, 2 * (s + 1))
                src = dst
            n = 2 * len(HALVES)
            dve.wait_ge(tie_psum, 1)
            dve.tensor_copy(need[:, 1:2], psC[:, 2:3]).then_inc(tie, 1)
            dve.wait_ge(tie, n + 1)
            dve.scalar_tensor_tensor(out=need[:, 0:1], in0=psC[:, 1:2], scalar=-1.0, in1=need[:, 1:2],
                                     op0=ALU.mult, op1=ALU.subtract).then_inc(tie, 1)
            dve.wait_ge(tie, n + 2)
            dve.tensor_scalar(need[:, 1:2], need[:, 0:1], float(TOPK), None, ALU.add).then_inc(tie, 1)
            dve.wait_ge(tie, n + 3)
            dve.scalar_tensor_tensor(out=eq[:, :], in0=src[:, :], scalar=need[:, 1:2], in1=eq[:, :],
                                     op0=ALU.is_le, op1=ALU.mult).then_inc(tie, 1)
            dve.wait_ge(tie, n + 4)
            dve.scalar_tensor_tensor(out=eq[:, :], in0=ST[:, :], scalar=t, in1=eq[:, :],
                                     op0=ALU.is_gt, op1=ALU.add).then_inc(tie, 1)
            dve.wait_ge(tie, n + 5)
            dve.tensor_tensor(junk[:, :], eq[:, :], ST[:, :], ALU.mult).then_inc(g_in, 1)
            dve.wait_ge(g_psum, 1)
            dve.tensor_copy(gates[:, :].rearrange("p (c r) -> p r c", c=NC), psG[:, :, :]).then_inc(g_done, 1)
            dve.wait_ge(g_done, 1)
            dve.wait_ge(z_done, NT)
            with dve.Fori(0, B) as b:
                for tt in range(TT + 1):
                    if tt < TT:
                        s = tt % 2
                        if tt >= 2:
                            dve.wait_ge(tail.xn_done, b * TT + tt - 1)
                        dve.wait_ge(tail.res_in[s], tail.loads(b, tt))
                        dve.scalar_tensor_tensor(out=tail.y[s], in0=z[:, bass.ds(b * TT + tt, 1), :].rearrange("p a n -> p (a n)"),
                                                 scalar=gates[:, bass.ds(b * TT + tt, 1)], in1=tail.res[s],
                                                 op0=ALU.mult, op1=ALU.add).then_inc(tail.y_sum, 1)
                        dve.wait_ge(tail.y_sum, b * TT + tt + 1)
                        tail.stats_of(dve, b, tt)
                    if tt:
                        tail.norm(dve, b, tt - 1)

        @block.tensor
        def _(pe):
            pe.wait_ge(small_in, 6 * 16)
            with pe.Fori(0, B) as b:
                for i in range(BC):
                    pe.wait_ge(l_done, b * BC + i + 1)
                    pe.wait_ge(raw_in[i], (b + 1) * 16)
                    for r in range(R):
                        for k in range(KT):
                            last = pe.matmul(psL[i][:, r, :], raw[:, i, k, r * P:(r + 1) * P], rw_sb[:, k, :],
                                             start=(k == 0), stop=(k == KT - 1))
                    last.then_inc(l_psum, 1)
            pe.wait_ge(step, 5)
            for r in range(R):
                last = pe.transpose(psT[:, r * P:(r + 1) * P], probs[:, r, :, :].rearrange("p c e -> p (c e)"), c.ident[:, :])
            last.then_inc(t_psum, 1)
            pe.wait_ge(w_lo_done, 1)
            pe.matmul(psC[:, 3:4], c.ident[:, :], c.ident[:, 0:1], start=True, stop=True).then_inc(z_psum, 1)
            with pe.Fori(0, B) as b:
                pe.wait_ge(x_lo_done, b * BC + BC + 2)
                for tt in range(TT):
                    n = b * TT + tt
                    if tt >= 2:
                        pe.wait_ge(z_done, n - 1)
                    for a, (i, d) in enumerate(TERMS):
                        for k in range(KT):
                            last = pe.matmul(psZ[tt % 2][:, :], xs[i][:, k, tt * P:(tt + 1) * P], w[d][:, k, :],
                                             start=(a == 0 and k == 0), stop=(a == 2 and k == KT - 1))
                    last.then_inc(z_psum, 1)
                    pe.wait_ge(cnt_done, n + 1)
                    pe.matmul(psC[:, 0:1], same_sb[:, :], cnt[:, 0:1], start=True, stop=True).then_inc(cnt_psum, 1)
            pe.wait_ge(tie_cnt, 2)
            pe.matmul(psC[:, 1:2], same_sb[:, :], cnt[:, 1:2], start=True, stop=True)
            pe.matmul(psC[:, 2:3], earlier_sb[:, :], cnt[:, 2:3], start=True, stop=True).then_inc(tie_psum, 1)
            pe.wait_ge(g_in, 1)
            for r in range(R):
                last = pe.matmul(psG[:, r, :], junk[:, r * P:(r + 1) * P], chunk_sb[:, :], start=True, stop=True)
            last.then_inc(g_psum, 1)


def build(nc, xT, x, wqkv0, wo0T, wg, wu, wd, wqkv1, bqkv1, cosT, sinT, rw, rb, ew, eb,
          same_expert, earlier_chunk, chunk_of, out, stages=4):
    def scratch(name, shape):
        return nc.dram_tensor(name, shape, F32, kind="Internal").ap()

    x1, x1T, x2, x2T, x3, x3T = (scratch(f"s_{n}", s) for n, s in
                                 (("x1", [T, H]), ("x1T", [H, T]), ("x2", [T, H]), ("x2T", [H, T]), ("x3", [T, H]), ("x3T", [H, T])))
    m_scratch = scratch("s_m", [HG * TT, P])
    with ExitStack() as ctx:
        c = Consts(nc, ctx)
        if stages == 1:
            x1 = out
        attention_phase(nc, c, "a0", xT, x, wqkv0, wo0T, None, None, m_scratch, x1, x1T)
        c.end_phase()
        if stages == 1:
            return
        ffn_phase(nc, c, x1T, x1, wg, wu, wd, out if stages == 2 else x2, x2T)
        c.end_phase()
        if stages == 2:
            return
        attention_phase(nc, c, "a1", x2T, x2, wqkv1, None, bqkv1, (cosT, sinT), m_scratch, out if stages == 3 else x3, x3T)
        c.end_phase()
        if stages == 3:
            return
        moe_phase(nc, c, x3T, x3, ew, rw, eb, rb, same_expert, earlier_chunk, chunk_of, out)


def kernel(**inputs):
    import numpy as np
    import concourse.bacc as bacc
    from concourse.bass_utils import run_bass_kernel_spmd

    arrays, order = layout(inputs, np)
    nc = bacc.Bacc("TRN2", target_bir_lowering=False, num_devices=1)
    args = [nc.dram_tensor(f"in_{n}", arrays[n].shape, mybir.dt.from_np(arrays[n].dtype), kind="ExternalInput").ap() for n in order]
    out = nc.dram_tensor("out_y", (T, H), F32, kind="ExternalOutput").ap()
    build(nc, *args, out)
    r = run_bass_kernel_spmd(nc, [{f"in_{n}": arrays[n] for n in order}], core_ids=[0])
    return r.results[0]["out_y"].reshape(B, S, H)


def layout(inputs, np):
    a = {k: np.asarray(v) for k, v in inputs.items()}
    x = a["L0_attn_hidden_states"].reshape(T, H)
    inv_freq = (1.0 / np.float32(10000.0) ** (np.arange(0, HD, 2, dtype=np.float32) / np.float32(HD))).astype(np.float32)
    freqs = np.outer(np.arange(S, dtype=np.float32), inv_freq).astype(np.float32).T
    cos, sin = np.cos(freqs), np.sin(freqs)
    chunk, expert = np.arange(P) // NE, np.arange(P) % NE
    place = np.arange(P)
    within, head = place // HG, place % HG
    feature = within % 8 % 4 + within // 8 * 4 + within % 8 // 4 * (HD // 2)
    qk_order = head * HD + feature

    def qkv(w):
        w = w.T.reshape(KT, P, 3, G, P).transpose(3, 1, 0, 2, 4)
        return np.ascontiguousarray(np.stack([w[:, :, :, 0][..., qk_order], w[:, :, :, 1][..., qk_order], w[:, :, :, 2]], axis=3))

    b1 = a["L1_attn_Wqkv_b"].reshape(3, G, P)
    b1 = np.stack([b1[0][:, qk_order], b1[1][:, qk_order], b1[2]])
    arrays = {
        "xT": np.ascontiguousarray(x.T),
        "x": x,
        "wqkv0": qkv(a["L0_attn_w_qkv"]),
        "wo0T": np.ascontiguousarray(a["L0_attn_w_o"].T),
        "wg": np.ascontiguousarray(a["L0_ffn_w_gate"].reshape(KT, P, 4, P, 4).transpose(2, 1, 0, 4, 3)),
        "wu": np.ascontiguousarray(a["L0_ffn_w_up"].reshape(KT, P, 4, P, 4).transpose(2, 1, 0, 4, 3)),
        "wd": a["L0_ffn_w_down"].reshape(4, P, 4, H),
        "wqkv1": qkv(a["L1_attn_Wqkv_w"]),
        "bqkv1": np.ascontiguousarray(b1.reshape(3 * G, P).T),
        "cosT": np.ascontiguousarray(np.concatenate([cos, cos])[feature]),
        "sinT": np.ascontiguousarray(np.concatenate([-sin, sin])[feature]),
        "rw": a["L1_ffn_router_w"],
        "rb": a["L1_ffn_router_b"],
        "ew": a["L1_ffn_expert_w"],
        "eb": a["L1_ffn_expert_b"],
        "same_expert": (expert[:, None] == expert[None, :]).astype(np.float32),
        "earlier_chunk": ((expert[:, None] == expert[None, :]) & (chunk[:, None] < chunk[None, :])).astype(np.float32),
        "chunk_of": (chunk[:, None] == np.arange(P // NE)[None, :]).astype(np.float32),
    }
    return arrays, list(arrays)
```

```python
from contextlib import ExitStack

import concourse.bass as bass
from concourse import mybir

F32 = mybir.dt.float32
F32R = mybir.dt.float32r
BF16 = mybir.dt.bfloat16
I32 = mybir.dt.int32
ALU = mybir.AluOpType
ACT = mybir.ActivationFunctionType
AX = mybir.AxisListType

P = 128
B, S, H = 4, 1024, 512
T = B * S
NH, HD = 16, 32
KT = H // P
TT = S // P
G = NH * HD // P
HG = P // HD
FFN = 2048
NE = 16
TOPK = T // NE
EPS = 1e-5
SCALE = float(HD) ** -0.5
TERMS = ((0, 0), (0, 1), (1, 0))
SWAP_HALVES = [(i + 16) % 32 for i in range(32)]


def hold(eng, sem, value, passed):
    eng.wait_ge(sem, value)
    eng.sem_inc(passed, 1)


class Tail:

    def __init__(self, nc, ctx, name, res, y, xn, xTs, psum_slots, consts, x_out, xT_out):
        def sem(n):
            return consts.semaphore(f"{name}_{n}")

        def sb(n, shape):
            return ctx.enter_context(nc.sbuf_tensor(f"{name}_{n}", shape, F32))

        self.nc, self.psT, self.c = nc, psum_slots, consts
        self.x_out = x_out.rearrange("(b t p) n -> b t p n", b=B, p=P)
        self.xT_out = xT_out.rearrange("(k p) (b t c) -> b t p k c", p=P, b=B, c=P) if xT_out is not None else None
        self.res, self.y, self.xn, self.xTs = res, y, xn, xTs
        self.stats = sb("stats", [P, 4, 6])
        self.mv = sb("mv", [P, 4, 2])
        self.vare = sb("vare", [P, 4])
        self.rstd = sb("rstd", [P, 4])
        self.res_in = [sem(f"res_in{i}") for i in (0, 1)]
        self.y_sum = sem("y_sum")
        self.y_stats = sem("y_stats")
        self.y_mv = sem("y_mv")
        self.y_vare = sem("y_vare")
        self.y_rstd = sem("y_rstd")
        self.xn_done = sem("xn_done")
        self.xT_psum = sem("xT_psum")
        self.xT_done = sem("xT_done")
        self.passed = [sem(f"passed_{e}") for e in ("sp", "pool", "dve")]
        self.out_x = [sem(f"out_x{i}") for i in (0, 1)]
        self.out_xT = [sem(f"out_xT{i}") for i in (0, 1)]

    def load_res(self, sp, b, tt, x_in):
        if tt >= 2:
            sp.wait_ge(self.xn_done if self.y is self.res else self.y_sum, b * TT + tt - 1)
        sp.dma_start(self.res[tt % 2], x_in[b, tt]).then_inc(self.res_in[tt % 2], 16)

    def store(self, sp, b, tt):
        sp.wait_ge(self.xn_done, b * TT + tt + 1)
        sp.dma_start(self.x_out[b, tt], self.xn[tt % len(self.xn)]).then_inc(self.out_x[tt % 2], 16)
        if self.xT_out is not None:
            sp.wait_ge(self.xT_done, b * TT + tt + 1)
            sp.dma_start(self.xT_out[b, tt], self.xTs[tt % 2].rearrange("p (k c) -> p k c", k=KT)).then_inc(self.out_xT[tt % 2], 16)

    @staticmethod
    def loads(b, tt):
        return (b * (TT // 2) + tt // 2 + 1) * 16

    def wait_stored(self, sp, b):
        for slot in (0, 1):
            if self.xT_out is not None:
                sp.wait_ge(self.out_xT[slot], self.loads(b, TT - 2))
            hold(sp, self.out_x[slot], self.loads(b, TT - 2), self.passed[0])

    def add_stats(self, dve, b, tt, part):
        s = tt % 2
        dve.wait_ge(self.res_in[s], self.loads(b, tt))
        dve.tensor_tensor(self.y[s], part, self.res[s], ALU.add).then_inc(self.y_sum, 1)
        dve.wait_ge(self.y_sum, b * TT + tt + 1)
        self.stats_of(dve, b, tt)

    def stats_of(self, dve, b, tt):
        s = tt % 4
        n = b * TT + tt + 1
        dve.bn_stats(self.stats[:, s, :], self.y[tt % len(self.y)]).then_inc(self.y_stats, 1)
        hold(dve, self.y_stats, n, self.passed[2])
        dve.bn_aggr(self.mv[:, s, :], self.stats[:, s, :]).then_inc(self.y_mv, 1)
        dve.wait_ge(self.y_mv, n)
        dve.tensor_scalar(self.vare[:, s:s + 1], self.mv[:, s, 1:2], EPS, None, ALU.add).then_inc(self.y_vare, 1)

    def rsqrt(self, pool, b, tt):
        s = tt % 4
        pool.wait_ge(self.y_vare, b * TT + tt + 1)
        pool.tensor_tensor(self.rstd[:, s:s + 1], self.vare[:, s:s + 1], self.c.neg_half[:, :], ALU.pow).then_inc(self.y_rstd, 1)

    def norm(self, dve, b, tt):
        s = tt % 4
        dve.wait_ge(self.y_rstd, b * TT + tt + 1)
        if tt >= 2 and self.xn is not self.y:
            dve.wait_ge(self.out_x[tt % 2], self.loads(b, tt - 2))
            if self.xT_out is not None:
                dve.wait_ge(self.xT_psum, b * TT + tt - 1)
        dve.tensor_scalar(self.xn[tt % len(self.xn)], self.y[tt % len(self.y)], self.mv[:, s, 0:1], self.rstd[:, s:s + 1],
                          ALU.subtract, ALU.mult).then_inc(self.xn_done, 1)

    def transpose(self, pe, b, tt):
        s = tt % 2
        pe.wait_ge(self.xn_done, b * TT + tt + 1)
        slots = len(self.psT)
        if tt >= slots:
            pe.wait_ge(self.xT_done, b * TT + tt + 1 - slots)
        for k in range(KT):
            last = pe.transpose(self.psT[tt % slots][:, k * P:(k + 1) * P], self.xn[tt % len(self.xn)][:, k * P:(k + 1) * P], self.c.ident[:, :])
        last.then_inc(self.xT_psum, 1)

    def copy_T(self, act, b, tt):
        s = tt % 2
        act.wait_ge(self.xT_psum, b * TT + tt + 1)
        if tt >= 2:
            act.wait_ge(self.out_xT[s], self.loads(b, tt - 2))
        act.activation(self.xTs[s], self.psT[tt % len(self.psT)], ACT.Copy).then_inc(self.xT_done, 1)


class Consts:

    def __init__(self, nc, ctx):
        self.nc, self.sems = nc, []
        self.semaphores = ctx.enter_context(ExitStack())
        def sb(n, shape, dt=F32):
            return ctx.enter_context(nc.sbuf_tensor(n, shape, dt))

        self.ident = sb("ident", [P, P])
        self.ident_b = sb("ident_b", [P, P], BF16)
        self.tri = sb("tri", [P, P], BF16)
        self.neg_half = sb("neg_half", [P, 1])
        self.ones = sb("ones", [P, HD])
        made, tri_made = self.semaphore("consts_made"), self.semaphore("tri_made")
        with nc.Block() as block:
            @block.gpsimd
            def _(pool):
                pool.memset(self.neg_half[:, :], -0.5)
                pool.memset(self.ones[:, :], 1.0)
                pool.memset(self.tri[:, :], 0.0).then_inc(tri_made, 1)
                pool.wait_ge(tri_made, 1)
                pool.affine_select(out=self.tri[:, :], in_=self.tri[:, :], compare_op=ALU.is_ge, fill=-1e30, base=0,
                                   pattern=[[-1, P]], channel_multiplier=1)
                pool.memset(self.ident[:, :], 0.0).then_inc(made, 1)
                pool.wait_ge(made, 1)
                pool.affine_select(out=self.ident[:, :], in_=self.ident[:, :], compare_op=ALU.not_equal, fill=1.0,
                                   base=0, pattern=[[-1, P]], channel_multiplier=1).then_inc(made, 1)

            @block.vector
            def _(dve):
                dve.wait_ge(made, 2)
                dve.tensor_copy(self.ident_b[:, :], self.ident[:, :]).then_inc(made, 1)
        self.end_phase()

    def semaphore(self, name):
        self.sems.append(self.semaphores.enter_context(self.nc.semaphore(name)))
        return self.sems[-1]

    def end_phase(self):
        with self.nc.Block() as block:
            @block.sync
            def _(sp):
                for s in self.sems:
                    sp.sem_clear(s)
        self.semaphores.close()
        self.sems = []


ORDERS = {
    "a0": (dict(flat=0.035, hi=0.0455, lo=0.07, act_vt=0.0526, dve_vb=0.01, dve_rows=0.0055, act_rows=-0.0015,
            dve_s=-0.0139, dve_y=-0.02, proj=(0.0, 0.0363, 0.1, 0.15), s=(0.2097, 0.93), sc=0, rows=0.9351, w=0.614,
            v=(0.26, 0.4253, 0.46, 0.56), x=0.7363, halves=((0.0, 0.34), (0.34, 0.96)), norm=(0.035, 0.0106),
            stc=47.5891),
           dict(flat=0.035, hi=0.06, lo=0.07, act_vt=0.0072, dve_vb=0.0356, dve_rows=0.025, act_rows=-0.02, act_xT=0.017,
            dve_y=0.0091, dve_norm=-0.0077, pool_st=-0.0092, dve_yn=-0.02, proj=(0, 0.0338, 0.0938, 0.1438),
            s=(0.2314, 0.93), sc=96.7085, rows=0.9302, w=0.5, v=(0.25, 0.2531, 0.28, 0.3), x=0.7075,
            halves=((0.0885, 0.55), (0.55, 0.99)), norm=(0.0217, 0.01), stc=155.3498, y=(0.4021, 0.8305), yn=0.9386)),
    "a1": (dict(flat=0.0241, hi=0.06, lo=0.07, act_vt=0.0446, dve_vb=0.0147, dve_rows=0.0067, act_rows=-0.02, dve_s=-0.02,
            dve_y=0.0327, sp_lo=0.0406, pool_st=0.0079, proj=(0.0376, 0.0673, 0.13, 0.19), s=(0.22, 0.93), sc=46.0309,
            rows=0.9351, w=0.5782, v=(0.3, 0.37, 0.44, 0.5), x=0.7422, halves=((0.0874, 0.34), (0.34, 0.96)),
            norm=(0.035, 0.0106), stc=0),
           dict(flat=0.0225, hi=0.06, lo=0.07, act_vt=0.005, dve_vb=0.0296, act_rows=0.005, act_st=0.0149, dve_s=0.0049,
            act_xT=0.0362, dve_y=0.0376, dve_norm=-0.0027, pool_st=-0.0185, dve_yn=-0.02, proj=(0.0, 0.04, 0.1, 0.15),
            s=(0.28, 0.92), sc=60, rows=0.9276, w=0.4746, v=(0.25, 0.3, 0.33, 0.3311), x=0.7075,
            halves=((0.0587, 0.55), (0.55, 0.96)), norm=(0.0217, 0.01), stc=97.1951, y=(0.4021, 0.8019), yn=1.6395)),
}


def attention_order(eng, orders, tail, x_next, y_next):
    at = []
    C = orders[1 if tail else 0]
    if y_next:
        chunks = [(i, h) for h in range(2) for i in range(2)]
        for kind in ("proj", "flat", "hi", "lo"):
            at += [(C["proj"][n] + (0 if kind == "proj" else C[kind]), (kind, i, h)) for n, (i, h) in enumerate(chunks)]
        s = [("s", j, qt, 0) for j in range(HG) for qt in range(4)]
        s += [("s", j, qt, 0) for j in range(HG) for qt in range(4, TT)]
        s += [("s", j, qt, 1) for j in range(HG) for qt in range(4, TT)]
        cost = [min(S // 2, (qt + 1) * P - c * S // 2) + C["sc"] for _, _, qt, c in s]
        at += [(C["s"][0] + (C["s"][1] - C["s"][0]) * sum(cost[:n]) / sum(cost), e) for n, e in enumerate(s)]
        at += [(C["rows"], ("rows",)), (C["w"], ("w",))]
        at += [(x, e) for x, e in zip(C["v"], (("vt", 0), ("vb", 0), ("vt", 1), ("vb", 1)))]
    if x_next:
        at += [(C["x"] + 0.05 * k, ("x", k)) for k in range(KT)]
    if tail:
        a, z = C["y"]
        step = (z - a) / TT
        for tt in range(TT):
            p = a + step * tt
            at += [(p, ("y", tt)), (p + C["yn"] * step, ("yn", tt)), (p + (C["yn"] + 0.1) * step, ("xT", tt)), (p + (C["yn"] + 1) * step, ("store", tt))]
        at += [(C["rows"] - 0.001, ("stored",))]
    for h, (a, z) in enumerate(C["halves"]):
        tiles = 4 * (h + 1)
        cost = [sum(min(S // 2, (h + 1) * S // 2 - t * P) + C["stc"] for t in range(kt)) for kt in range(tiles + 1)]
        place = [a + (z - a) * x / cost[-1] for x in cost]
        for kt in range(tiles):
            at += [(place[kt] + (place[kt + 1] - place[kt]) * j / HG, ("st", h, kt, j)) for j in range(HG)]
            at += [(place[min(kt + 2, tiles)] - 1e-4 + 1e-5 * kt, ("pv", h, kt))]
        at += [(z + 1e-3 + C["norm"][h] * p, ("norm", h, p)) for p in range(4)]
    return [e for _, e in sorted(((p + C.get(f"{eng}_{e[0]}", 0), e) for p, e in at), key=lambda x: x[0])]


def attention_phase(nc, c, L, xT_in, x_in, wqkv, woT, bias, rope, m_scratch, x_out, xT_out):
    ctx = ExitStack()
    with ctx:
        def sb(n, shape, dt=F32):
            return ctx.enter_context(nc.sbuf_tensor(f"{L}_{n}", shape, dt))

        def sem(n):
            return c.semaphore(f"{L}_{n}")

        HS = S // 2
        NS = HG * (4 + 4 + 4)
        NCUT = HG * TT
        EXP = 2
        NPV = 12

        w_raw = sb("w_raw", [P, KT * 3 * P])
        w = [[sb(f"w_{n}{i}", [P, KT, 3, P], F32R) for n in ("hi", "lo")] for i in (0, 1)]
        xs = [sb("x_hi", [P, KT, S], F32R), sb("x_lo", [P, KT, S], F32R)]
        x_raw = sb("x_raw", [P, 2, S])
        VT = [x_raw[:, 0, h * HS:(h + 1) * HS] for h in range(2)]
        parts = [[sb(f"{n}{i}", [P, HS], F32R) for n in ("hi", "lo")] for i in (0, 1)]
        QS = [sb(f"q_stack{i}", [97, HG, S], F32R) for i in (0, 1)]
        KS = [sb(f"k_stack{i}", [97, HG, S], F32R) for i in (0, 1)]
        V = [sb(f"V{i}", [P, TT, P]) for i in (0, 1)]
        PT = sb("PT", [P, 8, HS])
        inv = sb("inv", [P, P])
        attn = sb("attn", [P, G, S])
        tail_buf = sb("tail", [P, 6, H])
        nmax, nmax_1 = sb("nmax", [P, HG, TT]), sb("nmax_1", [P, HG, TT // 2])
        nmax_T = sb("nmax_T", [HG * TT, P], F32R)
        if woT is not None:
            wo = sb("wo", [P, KT, H])
        if bias is not None:
            bias_sb = sb("bias", [P, 3 * G])
            cosT, sinT = sb("cosT", [P, S]), sb("sinT", [P, S])

        def bank(n):
            return ctx.enter_context(nc.psum_tensor(f"{L}_{n}", [P, HS], F32))

        O, SUM = bank("O"), bank("SUM")
        st_bank = [bank("st0"), bank("st1")]
        s_bank = [bank("s0"), bank("s1")]
        p_bank = [bank("p0"), bank("p1")]

        w_in, w_hi_done, w_lo_done = sem("w_in"), sem("w_hi_done"), sem("w_lo_done")
        const_in, const_done = sem("const_in"), sem("const_done")
        x_raw_in = [sem("x_raw_in0"), sem("x_raw_in1")]
        x_hi_done, x_lo_done = sem("x_hi_done"), sem("x_lo_done")
        qk_psum, qk_hi, qk_lo = sem("qk_psum"), sem("qk_hi"), sem("qk_lo")
        r_flat, r_swap, r_cos, r_sin, r_sum = (sem(n) for n in ("r_flat", "r_swap", "r_cos", "r_sin", "r_sum"))
        p_read = qk_lo if bias is None else r_flat
        stacked = [sem(f"stacked{i}") for i in range(4)]
        vt_psum, vt_done, v_psum, v_done = sem("vt_psum"), sem("vt_done"), sem("v_psum"), sem("v_done")
        s_psum, max_done, row_max = sem("s_psum"), sem("max_done"), sem("row_max")
        mT_psum, mT_done, m_out, m_row = sem("mT_psum"), sem("mT_done"), sem("m_out"), sem("m_row")
        st_psum, exp_done, cut_done, pv_done = sem("st_psum"), sem("exp_done"), sem("cut_done"), sem("pv_done")
        inv_done, attn_done, y_psum = sem("inv_done"), sem("attn_done"), sem("y_psum")
        y_slots = [tail_buf[:, i, :] for i in (0, 1)]
        tail = Tail(nc, ctx, f"{L}_t", y_slots, y_slots, [tail_buf[:, i, :] for i in (2, 3)], [tail_buf[:, i, :] for i in (4, 5)],
                    [p_bank[1][:, :]], c, x_out, xT_out)

        x_rows = x_in.rearrange("(b t p) n -> b t p n", b=B, p=P)
        x_cols = xT_in.rearrange("(k p) (b s) -> b k p s", p=P, b=B)
        w_set = [[t[:, :, :, :].rearrange("p k i n -> p (k i n)") for t in s] for s in w]
        STACK_DMAS = 3 * 16

        def y_bank(g, tt):
            return s_bank[0] if g == G and tt % 2 else p_bank[0]

        def st_index(h, kt, j):
            return (4 * h + kt) * HG + j

        def cut_count(h, kt):
            return (kt + 1) * HG

        def s_index(j, qt, ch):
            return (qt // 4 + ch) * 4 * HG + j * 4 + qt % 4

        def each_step(eng, name, step):
            first_work = [e for e in attention_order(name, ORDERS[L], False, False, True)
                          if e[0] in ("proj", "flat", "hi", "lo", "s", "rows", "vt", "vb", "w")]
            step(0, -1, [("x", 0), ("w",)] + [("x", k) for k in range(1, KT)] + first_work)
            for first, last in ((True, False), (False, False), (False, True)):
                def batch(b):
                    for g in range(G):
                        step(b, g, attention_order(name, ORDERS[L], g == 0 and not first, g == G - 2 and not last, not (last and g == G - 1)))
                if first:
                    batch(0)
                elif last:
                    batch(B - 1)
                else:
                    with eng.Fori(1, B - 1) as b:
                        batch(b)
            step(B - 1, G, [e for n in range(TT + 2)
                            for e in (("y", n), ("yn", n - 1), ("xT", n - 2), ("store", n - 2)) if 0 <= e[1] < TT] + [("stored",)])

        block = ctx.enter_context(nc.Block())


        @block.sync
        def _(sp):
            def load_constants():
                if woT is not None:
                    sp.dma_start(wo[:, :, :], woT.rearrange("(k p) n -> p k n", p=P)).then_inc(const_in, 16)
                if bias is not None:
                    sp.dma_start(bias_sb[:, :], bias).then_inc(const_in, 16)
                    sp.dma_start(cosT[:, :], rope[0]).then_inc(const_in, 16)
                    sp.dma_start(sinT[:, :], rope[1]).then_inc(const_in, 16)

            loaded_w = [0]

            def step(b, g, order):
                m = b * G + g + 1
                for e in order:
                    if e[0] == "w":
                        nw = loaded_w[0] if g < 0 else m + 1
                        if g < 0:
                            loaded_w[0] += 1
                        if g < 0 and nw == 0:
                            pass
                        elif isinstance(b, int) and b == B - 1 and g >= G - 2:
                            continue
                        else:
                            sp.wait_ge(w_lo_done, nw)
                        sp.dma_start(w_raw[:, :], wqkv[(g + 2) % G if g >= 0 else nw].rearrange("p k i n -> p (k i n)")).then_inc(w_in, 16)
                    elif e[0] == "x":
                        k, q = e[1], b + 1 if g >= 0 else 0
                        if k >= 2:
                            sp.wait_ge(x_lo_done, q * KT + k - 1)
                        elif g >= 0:
                            sp.wait_ge(v_psum, (m + 1) * 2)
                        sp.dma_start(x_raw[:, k % 2, :], x_cols[q, k]).then_inc(x_raw_in[k % 2], 16)
                        if g < 0 and k == 3:
                            load_constants()
                    elif e[0] == "lo":
                        i, h = e[1:]
                        hi, lo = parts[i]
                        stack = (QS, KS)[i][(g + 1) % 2]
                        for part, done, rows in ((hi, qk_hi, ((0, 1), (0, 2))[i]), (lo, qk_lo, ((2,), (1,))[i])):
                            sp.wait_ge(done, m * 4 + 2 * h + i + 1)
                            for r in rows:
                                sp.dma_start(stack[HD * r:HD * (r + 1), :, h * HS:(h + 1) * HS].bitcast(F32),
                                             part[:, :].bitcast(F32)).then_inc(stacked[2 * h + i], 16)
                    elif e[0] == "rows":
                        sp.wait_ge(mT_done, m + 1)
                        sp.dma_start(m_scratch, nmax_T[:, :].bitcast(F32)).then_inc(m_out, 16)
                        sp.wait_ge(m_out, (m + 1) * 16)
                        sp.dma_start(QS[(g + 1) % 2][96:97, :, :].bitcast(F32),
                                     m_scratch.rearrange("(o j t) c -> o j (t c)", o=1, j=HG)).then_inc(m_row, 16)
                    elif e[0] == "y":
                        tail.load_res(sp, b - 1 + g // G, e[1], x_rows)
                    elif e[0] == "store":
                        tail.store(sp, b - 1 + g // G, e[1])
                    elif e[0] == "stored":
                        tail.wait_stored(sp, b - 1 + g // G)

            each_step(sp, "sp", step)

        @block.gpsimd
        def _(pool):
            for s in KS:
                pool.memset(s[96:97, :, :].bitcast(F32), 1.0).then_inc(const_done, 1)
            pool.wait_ge(const_done, 2)
            wn = [0]

            def step(b, g, order):
                n, m = b * G + g, b * G + g + 1
                for e in order:
                    if e[0] == "w":
                        nw, s = (wn[0], wn[0] % 2) if g < 0 else (m + 1, g % 2)
                        wn[0] += 1
                        if isinstance(b, int) and b == B - 1 and g >= G - 2:
                            continue
                        pool.wait_ge(w_hi_done, nw + 1)
                        pool.tensor_tensor(w_set[s][1], w_raw[:, :], w_set[s][0].bitcast(F32), ALU.subtract).then_inc(w_lo_done, 1)
                    elif e[0] == "flat" and bias is not None:
                        i, h = e[1:]
                        if g < 0:
                            pool.wait_ge(const_in, 3 * 16)
                        swapped = x_raw[:, i, HS:S]
                        pool.wait_ge(r_swap, m * 4 + 2 * h + i + 1)
                        pool.tensor_tensor(swapped, swapped, sinT[:, h * HS:(h + 1) * HS], ALU.mult).then_inc(r_sin, 1)
                    elif e[0] == "st" and e[2] >= 4 * e[1]:
                        u = st_index(*e[1:])
                        hold(pool, exp_done, n * (EXP * NS) + EXP * (u + 1), tail.passed[1])
                        diag = PT[:, u % 8, 0:P]
                        pool.affine_select(out=diag, in_=diag, compare_op=ALU.is_ge, fill=0.0, base=0,
                                           pattern=[[1, P]], channel_multiplier=-1).then_inc(cut_done, 1)
                    elif e[0] == "y":
                        tail.rsqrt(pool, b - 1 + g // G, e[1])

            each_step(pool, "pool", step)

        @block.scalar
        def _(act):
            wn = [0]

            def step(b, g, order):
                n, m = b * G + g, b * G + g + 1
                for e in order:
                    if e[0] == "w":
                        nw, s = (wn[0], wn[0] % 2) if g < 0 else (m + 1, g % 2)
                        wn[0] += 1
                        if isinstance(b, int) and b == B - 1 and g >= G - 2:
                            continue
                        act.wait_ge(w_in, (nw + 1) * 16)
                        act.activation(w_set[s][0], w_raw[:, :], ACT.Copy).then_inc(w_hi_done, 1)
                    elif e[0] == "x":
                        k, q = e[1], b + 1 if g >= 0 else 0
                        act.wait_ge(x_raw_in[k % 2], (q * (KT // 2) + k // 2 + 1) * 16)
                        act.activation(xs[0][:, k, :], x_raw[:, k % 2, :], ACT.Copy).then_inc(x_hi_done, 1)
                    elif e[0] == "flat" and bias is not None:
                        i, h = e[1:]
                        u = m * 4 + 2 * h + i
                        if g < 0:
                            act.wait_ge(const_in, 3 * 16)
                        act.wait_ge(qk_psum, u + 1)
                        if h:
                            act.wait_ge(qk_lo, u - 1)
                        act.activation(x_raw[:, i, 0:HS], p_bank[i][:, :], ACT.Identity,
                                       bias=bias_sb[:, i * G + (g + 1) % G:i * G + (g + 1) % G + 1]).then_inc(r_flat, 1)
                    elif e[0] == "hi":
                        i, h = e[1:]
                        u = m * 4 + 2 * h + i
                        if h:
                            act.wait_ge(stacked[i], (m + 1) * STACK_DMAS)
                        if bias is None:
                            act.wait_ge(qk_psum, u + 1)
                        else:
                            act.wait_ge(r_sum, u + 1)
                        src = p_bank[i][:, :] if bias is None else x_raw[:, i, 0:HS]
                        act.activation(parts[i][0][:, :], src, ACT.Copy, scale=SCALE if i == 0 else 1.0).then_inc(qk_hi, 1)
                    elif e[0] == "vt":
                        if bias is not None:
                            act.wait_ge(qk_lo, m * 4 + 3)
                        act.wait_ge(vt_psum, m * 2 + e[1] + 1)
                        gv = 2 * G + (g + 1) % G
                        if bias is None:
                            act.activation(VT[e[1]], p_bank[1 - e[1]][:, :], ACT.Copy).then_inc(vt_done, 1)
                        else:
                            act.activation(VT[e[1]], p_bank[1 - e[1]][:, :], ACT.Identity, bias=bias_sb[:, gv:gv + 1]).then_inc(vt_done, 1)
                    elif e[0] == "rows":
                        act.wait_ge(mT_psum, m + 1)
                        act.activation(nmax_T[:, :], p_bank[0][0:HG * TT, 0:P], ACT.Copy).then_inc(mT_done, 1)
                    elif e[0] == "st":
                        u = st_index(*e[1:])
                        act.wait_ge(st_psum, n * NS + u + 1)
                        if u >= 8 and e[3] == 0:
                            act.wait_ge(pv_done, n * NPV + u // HG - 1)
                        width = min(HS, (e[1] + 1) * HS - e[2] * P)
                        act.activation(PT[:, u % 8, 0:width], st_bank[u % 2][:, 0:width], ACT.Exp).then_inc(exp_done, EXP)
                    elif e[0] == "xT":
                        tail.copy_T(act, b - 1 + g // G, e[1])

            each_step(act, "act", step)

        @block.vector
        def _(dve):
            def step(b, g, order):
                n, m = b * G + g, b * G + g + 1
                for e in order:
                    if e[0] == "x":
                        k, q = e[1], b + 1 if g >= 0 else 0
                        dve.wait_ge(x_hi_done, q * KT + k + 1)
                        dve.tensor_tensor(xs[1][:, k, :], x_raw[:, k % 2, :], xs[0][:, k, :].bitcast(F32), ALU.subtract).then_inc(x_lo_done, 1)
                    elif e[0] == "flat" and bias is not None:
                        i, h = e[1:]
                        u = m * 4 + 2 * h + i
                        flat, swapped = x_raw[:, i, 0:HS], x_raw[:, i, HS:S]
                        if g < 0:
                            dve.wait_ge(const_in, 3 * 16)
                        hold(dve, r_flat, u + 1, tail.passed[2])
                        dve.stream_shuffle(swapped, flat, SWAP_HALVES).then_inc(r_swap, 1)
                        dve.wait_ge(r_swap, u + 1)
                        dve.tensor_tensor(flat, flat, cosT[:, h * HS:(h + 1) * HS], ALU.mult).then_inc(r_cos, 1)
                    elif e[0] == "hi" and bias is not None:
                        i, h = e[1:]
                        u = m * 4 + 2 * h + i
                        flat, swapped = x_raw[:, i, 0:HS], x_raw[:, i, HS:S]
                        dve.wait_ge(r_sin, u + 1)
                        dve.wait_ge(r_cos, u + 1)
                        dve.tensor_tensor(flat, flat, swapped, ALU.add).then_inc(r_sum, 1)
                    elif e[0] == "lo":
                        i, h = e[1:]
                        hi, lo = parts[i]
                        src = p_bank[i][:, :] if bias is None else x_raw[:, i, 0:HS]
                        dve.wait_ge(qk_hi, m * 4 + 2 * h + i + 1)
                        dve.scalar_tensor_tensor(out=lo[:, :], in0=src, scalar=SCALE if i == 0 else 1.0, in1=hi[:, :].bitcast(F32),
                                                 op0=ALU.mult, op1=ALU.subtract).then_inc(qk_lo, 1)
                    elif e[0] == "s":
                        _, j, qt, ch = e
                        u = s_index(j, qt, ch)
                        width = min(HS, (qt + 1) * P - ch * HS)
                        dst = nmax[:, j, qt:qt + 1] if ch == 0 else nmax_1[:, j, qt - 4:qt - 3]
                        dve.wait_ge(s_psum, m * NS + u + 1)
                        dve.tensor_reduce(dst, s_bank[u % 2][:, 0:width], AX.X, ALU.max, negate=True).then_inc(max_done, 1)
                    elif e[0] == "rows":
                        dve.wait_ge(max_done, (m + 1) * NS)
                        dve.tensor_tensor(nmax[:, :, 4:TT], nmax[:, :, 4:TT], nmax_1[:, :, :], ALU.min).then_inc(row_max, 1)
                    elif e[0] == "vb":
                        dve.wait_ge(v_psum, m * 2 + e[1] + 1)
                        dve.tensor_copy(V[(g + 1) % 2][:, 4 * e[1]:4 * e[1] + 4, :],
                                        p_bank[1 - e[1]][:, :].rearrange("p (t n) -> p t n", n=P)).then_inc(v_done, 1)
                    elif e[0] == "norm":
                        _, h, p = e
                        u = (n * 2 + h) * 4 + p
                        cols = slice(p * P, (p + 1) * P)
                        dve.wait_ge(pv_done, n * NPV + 4 + 8 * h)
                        if p:
                            dve.wait_ge(attn_done, u)
                        if ("y", 0) in order:
                            dve.wait_ge(y_psum, (b - 1) * TT + 4 * h + p + 1)
                        dve.reciprocal(inv[:, :], SUM[:, cols]).then_inc(inv_done, 1)
                        dve.wait_ge(inv_done, u + 1)
                        dve.tensor_tensor(attn[:, g, h * HS + p * P:h * HS + (p + 1) * P], O[:, cols], inv[:, :], ALU.mult).then_inc(attn_done, 1)
                    elif e[0] == "y":
                        dve.wait_ge(y_psum, (b - 1 + g // G) * TT + e[1] + 1)
                        tail.add_stats(dve, b - 1 + g // G, e[1], y_bank(g, e[1])[:, :])
                    elif e[0] == "yn":
                        tail.norm(dve, b - 1 + g // G, e[1])

            each_step(dve, "dve", step)

        @block.tensor
        def _(pe):
            pe.wait_ge(const_done, 2)

            def step(b, g, order):
                n, m = b * G + g, b * G + g + 1
                has_tail = ("y", 0) in order
                bt = b - 1 + g // G
                set_y, set_x = (g + 1) % 2, g % 2

                def project(out, i, h):
                    for t, (a, d) in enumerate(TERMS):
                        for k in range(KT):
                            last = pe.matmul(out[:, :], w[set_y][a][:, k, i, :], xs[d][:, k, h * HS:(h + 1) * HS],
                                             start=(t == 0 and k == 0), stop=(t == 2 and k == KT - 1))
                    return last

                for e in order:
                    if e[0] == "proj":
                        i, h = e[1:]
                        if h == 0 and i == 0:
                            pe.wait_ge(w_lo_done, m + 1)
                            pe.wait_ge(x_lo_done, (b + (g + 1) // G + 1) * KT)
                        if h:
                            pe.wait_ge(p_read, m * 4 + i + 1)
                        elif g >= 0 and i == 0:
                            pe.wait_ge(mT_done, m)
                        elif g >= 0:
                            pe.wait_ge(v_done, m * 2)
                            if g == 1 and not (isinstance(b, int) and b == 0):
                                pe.wait_ge(tail.xT_done, b * TT)
                        project(p_bank[i], i, h).then_inc(qk_psum, 1)
                    elif e[0] == "vt":
                        pe.wait_ge(p_read, m * 4 + 4 - e[1])
                        project(p_bank[1 - e[1]], 2, e[1]).then_inc(vt_psum, 1)
                    elif e[0] == "vb":
                        pe.wait_ge(vt_done, m * 2 + e[1] + 1)
                        for t in range(4):
                            last = pe.transpose(p_bank[1 - e[1]][:, t * P:(t + 1) * P], VT[e[1]][:, t * P:(t + 1) * P], c.ident[:, :])
                        last.then_inc(v_psum, 1)
                    elif e[0] == "s":
                        _, j, qt, ch = e
                        u = s_index(j, qt, ch)
                        width = min(HS, (qt + 1) * P - ch * HS)
                        if j == 0 and qt % 4 == 0:
                            for r in ((0, 1), (2,), (3,))[qt // 4 + ch]:
                                pe.wait_ge(stacked[r], (m + 1) * STACK_DMAS)
                        if u >= 2:
                            pe.wait_ge(max_done, m * NS + u - 1)
                        last = pe.matmul(s_bank[u % 2][:, 0:width], QS[set_y][0:96, j, qt * P:(qt + 1) * P],
                                         KS[set_y][0:96, j, ch * HS:ch * HS + width], start=True, stop=True)
                        if qt // 4 == ch:
                            last = pe.matmul(s_bank[u % 2][:, width - P:width], c.ident_b[:, :], c.tri[:, :], start=False, stop=True,
                                             skip_group_check=True)
                        last.then_inc(s_psum, 1)
                    elif e[0] == "rows":
                        pe.wait_ge(row_max, m + 1)
                        if has_tail:
                            pe.wait_ge(tail.y_sum, (bt + 1) * TT)
                        else:
                            pe.wait_ge(v_done, m * 2 + 2)
                        pe.transpose(p_bank[0][0:HG * TT, 0:P], nmax[:, :, :].rearrange("p j t -> p (j t)"), c.ident[:, :]).then_inc(mT_psum, 1)
                    elif e[0] == "st":
                        _, h, kt, j = e
                        u = st_index(h, kt, j)
                        if u == 0:
                            pe.wait_ge(m_row, (n + 1) * 16)
                        if u >= 2:
                            pe.wait_ge(exp_done, n * (EXP * NS) + EXP * (u - 1))
                        q0 = max(h * HS, kt * P)
                        pe.matmul(st_bank[u % 2][:, 0:(h + 1) * HS - q0], KS[set_x][0:97, j, kt * P:(kt + 1) * P],
                                  QS[set_x][0:97, j, q0:(h + 1) * HS], start=True, stop=True).then_inc(st_psum, 1)
                    elif e[0] == "pv":
                        _, h, kt = e
                        if kt == 0:
                            if h:
                                pe.wait_ge(attn_done, n * 8 + 4)
                            else:
                                pe.wait_ge(v_done, (n + 1) * 2)
                                if not (isinstance(b, int) and b * G + g == 0):
                                    pe.wait_ge(attn_done, n * 8)
                        if kt >= 4 * h:
                            pe.wait_ge(cut_done, n * NCUT + cut_count(h, kt))
                        else:
                            pe.wait_ge(exp_done, n * (EXP * NS) + EXP * (st_index(h, kt, HG - 1) + 1))
                        q0 = max(0, kt * P - h * HS)
                        for out in (O, SUM):
                            for j in range(HG):
                                stat = V[set_x][:, kt, HD * j:HD * (j + 1)] if out is O else c.ones[:, :]
                                last = pe.matmul(out[HD * j:HD * (j + 1), q0:HS], stat, PT[:, st_index(h, kt, j) % 8, 0:HS - q0],
                                                 start=(kt == 0), stop=(kt == 4 * h + 3), tile_position=(0, HD * j))
                        last.then_inc(pv_done, 1)
                    elif e[0] == "y":
                        tt = e[1]
                        if tt == 0:
                            if g < G:
                                pe.wait_ge(v_done, m * 2 + 2)
                            if woT is not None:
                                pe.wait_ge(const_in, 16)
                            pe.wait_ge(attn_done, (bt + 1) * G * 8)
                        elif g < G:
                            pe.wait_ge(tail.y_sum, bt * TT + tt)
                        elif tt >= 2:
                            pe.wait_ge(tail.y_sum, bt * TT + tt - 1)
                        dst = y_bank(g, tt)
                        for k in range(KT):
                            col = attn[:, k, tt * P:(tt + 1) * P]
                            if woT is not None:
                                last = pe.matmul(dst[:, :], col, wo[:, k, :], start=(k == 0), stop=(k == KT - 1))
                            else:
                                last = pe.transpose(dst[:, k * P:(k + 1) * P], col, c.ident[:, :])
                        last.then_inc(y_psum, 1)
                    elif e[0] == "xT":
                        if e[1] == 0 and g < G:
                            pe.wait_ge(v_done, m * 2 + 1)
                        tail.transpose(pe, bt, e[1])

            each_step(pe, "pe", step)


def ffn_phase(nc, c, xT_in, x_in, wg, wu, wd, x_out, xT_out):
    GT, NB = FFN // (4 * P), S // 512
    NU = GT * NB
    HALF = (slice(0, 256), slice(256, 512))
    NCMP = 3 + 2 * 3
    ctx = ExitStack()
    with ctx:
        def sb(n, shape, dt=F32):
            return ctx.enter_context(nc.sbuf_tensor(f"f_{n}", shape, dt))

        def sem(n):
            return c.semaphore(f"f_{n}")

        part_raw = sb("part_raw", [P, 2, KT * 512])
        xs = [[sb(f"x_{n}{i}", [P, KT, 512], F32R) for n in ("hi", "lo")] for i in range(NB)]
        gate = [[sb(f"gate_{n}{i}", [P, KT, 4, P], F32R) for n in ("hi", "lo")] for i in (0, 1)]
        up = [[sb(f"up_{n}{i}", [P, KT, 4, P], F32R) for n in ("hi", "lo")] for i in (0, 1)]
        down = [sb(f"down_{n}", [P, 4, H], F32R) for n in ("hi", "lo")]
        y = sb("y", [P, TT, H])
        sg = sb("silu_gate", [P, 4, 512])
        h = [sb(f"h{i}", [P, 4, 512]) for i in (0, 1)]
        h_parts = [sb(f"h_{n}", [P, 4, 512], F32R) for n in ("hi", "lo")]
        mag = sb("mag", [P, 4, 512])
        cmp = sb("cmp", [P, 6, 512], BF16)
        pair = sb("pair", [P, 4, 512], BF16)
        wins = pair
        xT_buf = sb("xT_buf", [P, 2, H])
        GU = [[ctx.enter_context(nc.psum_tensor(f"f_{n}{i}", [P, 512], F32)) for n in ("gate", "up")] for i in (0, 1)]
        D = [ctx.enter_context(nc.psum_tensor(f"f_D{i}", [P, H], F32)) for i in range(4)]

        part_in = [sem("part_in0"), sem("part_in1")]
        hi_done, lo_done = sem("hi_done"), sem("lo_done")
        y_in = [sem(f"y_in{i}") for i in range(NB)]
        gu_psum, silu_done, h_done, mag_done = sem("gu_psum"), sem("silu_done"), sem("h_done"), sem("mag_done")
        cmp_done, pair_done, wins_done, keep_done = sem("cmp_done"), sem("pair_done"), sem("wins_done"), sem("keep_done")
        h_hi_done, h_lo_done, d_psum, sum_done = sem("h_hi_done"), sem("h_lo_done"), sem("d_psum"), sem("sum_done")
        y_tiles = [y[:, t, :] for t in range(TT)]
        tail = Tail(nc, ctx, "f_t", None, y_tiles, y_tiles, [xT_buf[:, i, :] for i in (0, 1)],
                    [D[i][:, :] for i in range(4)], c, x_out, xT_out)

        x_rows = x_in.rearrange("(b i t p) n -> b i p t n", b=B, i=NB, p=P)
        x_cols = xT_in.rearrange("(k p) (b i s) -> b i p k s", p=P, b=B, i=NB)

        FIRST_PARTS = [(0, "x", 0), (0, "gate", 0), (0, "up", 0)]

        def parts(last):
            p = [(0, "x", 1), (0, "gate", 1), (0, "down", 0), (1, "up", 1)]
            for gt in range(1, GT):
                if gt + 1 < GT or not last:
                    p.append((2 * gt, "gate", (gt + 1) % GT))
                p.append((2 * gt, "down", gt))
                if gt + 1 < GT or not last:
                    p.append((2 * gt + 1, "up", (gt + 1) % GT))
            return p if last else p + [(NU - 1, "x", 0)]

        NP = len(parts(False))

        def part_number(b, q, last):
            return b * NP + len(FIRST_PARTS) + parts(last).index(q)

        def slot_of(i):
            return (len(FIRST_PARTS) + i) % 2

        def slot_count(b, i):
            return b * (NP // 2 * 16) + ((len(FIRST_PARTS) + i) // 2 + 1) * 16

        def split_to(q):
            _, kind, i = q
            if kind == "x":
                return [t[:, :, :].rearrange("p k s -> p (k s)") for t in xs[i]]
            if kind == "down":
                return [t[:, :, :].rearrange("p j n -> p (j n)") for t in down]
            return [t[:, :, :, :].rearrange("p k j m -> p (k j m)") for t in (gate if kind == "gate" else up)[i % 2]]

        def part_dram(b, q):
            _, kind, i = q
            if kind == "x":
                return x_cols[b if i else b + 1, i]
            return wd[i] if kind == "down" else (wg if kind == "gate" else wu)[i].rearrange("p k j m -> p k (j m)")

        def raw(slot):
            return part_raw[:, slot, :].rearrange("p (k n) -> p k n", k=KT)

        def count(b, u, per, more=0):
            return b * (NU * per) + (u * per + more)

        def each_step(eng, step):
            def batch(b, first, last):
                for u in range(NU):
                    step(b, u, True, not first or u > 0, first, last)

            batch(0, True, False)
            with eng.Fori(1, B - 1) as b:
                batch(b, False, False)
            batch(B - 1, False, True)
            step(B, 0, False, True, False, False)
            step(B, 1, False, False, False, False)

        def is_at(n, b, u, first):
            return not first or u >= n

        block = ctx.enter_context(nc.Block())


        @block.sync
        def _(sp):
            def load_first(i):
                _, kind, _ = FIRST_PARTS[i]
                if i >= 2:
                    sp.wait_ge(lo_done, i - 1)
                src = x_cols[0, 0] if kind == "x" else (wg if kind == "gate" else wu)[0].rearrange("p k j m -> p k (j m)")
                sp.dma_start(raw(i % 2), src).then_inc(part_in[i % 2], 16)

            def load(b, i, last):
                ps = parts(last)
                if i < len(ps):
                    sp.wait_ge(lo_done, b * NP + len(FIRST_PARTS) + i - 1)
                    sp.dma_start(raw(slot_of(i)), part_dram(b, ps[i])).then_inc(part_in[slot_of(i)], 16)

            def load_y(b, blk):
                sp.dma_start(y[:, 4 * blk:4 * blk + 4, :], x_rows[b, blk]).then_inc(y_in[blk], 16)

            for i in range(len(FIRST_PARTS)):
                load_first(i)
            load_y(0, 0)
            load_y(0, 1)
            load(0, 0, False)
            load(0, 1, False)

            def step(b, u, new, old, first, last):
                if u < NB and not first:
                    for tt in range(4 * u, 4 * u + 4):
                        tail.store(sp, b - 1, tt)
                    if new:
                        for s in (0, 1):
                            sp.wait_ge(tail.out_x[s], tail.loads(b - 1, 4 * u + 2))
                        load_y(b, u)
                    if u == NB - 1:
                        tail.wait_stored(sp, b - 1)
                if new:
                    for i, q in enumerate(parts(last)):
                        if q[0] == u:
                            if i + 2 < len(parts(last)):
                                load(b, i + 2, last)
                            elif not last:
                                load(b + 1, i + 2 - NP, False)

            each_step(sp, step)

        @block.gpsimd
        def _(pool):
            def split_lo(q, slot, n):
                pool.wait_ge(hi_done, n + 1)
                hi, lo = split_to(q)
                pool.tensor_tensor(lo, part_raw[:, slot, :], hi.bitcast(F32), ALU.subtract).then_inc(lo_done, 1)

            for n, q in enumerate(FIRST_PARTS):
                split_lo(q, n % 2, n)

            def step(b, u, new, old, first, last):
                mine = [(i, q) for i, q in enumerate(parts(last)) if q[0] == u] if new else []
                for i, q in mine:
                    if q[1] != "down":
                        split_lo(q, slot_of(i), part_number(b, q, last))
                if u == NU - 1:
                    for tt in range(4):
                        tail.rsqrt(pool, b, tt)
                if u == 0 and not first:
                    for tt in range(4, TT):
                        tail.rsqrt(pool, b - 1, tt)
                for i, q in mine:
                    if q[1] == "down":
                        split_lo(q, slot_of(i), part_number(b, q, last))

            each_step(pool, step)

        @block.scalar
        def _(act):
            for n, q in enumerate(FIRST_PARTS):
                act.wait_ge(part_in[n % 2], 16 * (n // 2 + 1))
                act.activation(split_to(q)[0], part_raw[:, n % 2, :], ACT.Copy).then_inc(hi_done, 1)

            def split_hi(b, u, kinds, first, last):
                for i, q in enumerate(parts(last)):
                    if q[0] == u and q[1] in kinds:
                        act.wait_ge(part_in[slot_of(i)], slot_count(b, i))
                        act.activation(split_to(q)[0], part_raw[:, slot_of(i), :], ACT.Copy).then_inc(hi_done, 1)

            def silu(b, u, j, first):
                act.wait_ge(gu_psum, count(b, u, 4, j + 1))
                if is_at(1, b, u, first):
                    act.wait_ge(h_done, count(b, u - 1, 4, j + 1))
                act.activation(sg[:, j, :], GU[j % 2][0][:, :], ACT.Silu).then_inc(silu_done, 1)

            def magnitude(b, u, j, first):
                act.wait_ge(h_done, count(b, u, 4, j + 1))
                if j == 0 and is_at(1, b, u, first):
                    act.wait_ge(cmp_done, count(b, u, NCMP))
                act.activation(mag[:, j, :], h[u % 2][:, j, :], ACT.Abs).then_inc(mag_done, 1)

            def split_h(b, u, half, first):
                at = HALF[half]
                act.wait_ge(keep_done, count(b, u - 1, 8, 4 * (half + 1)))
                if is_at(2, b, u, first):
                    act.wait_ge(d_psum, count(b, u - 1, 4))
                act.activation(h_parts[0][:, :, at], h[(u - 1) % 2][:, :, at], ACT.Copy).then_inc(h_hi_done, 1)

            def step(b, u, new, old, first, last):
                blk_done = u < NB and not first
                if u == 0 and new:
                    if not first:
                        act.wait_ge(gu_psum, count(b, 0, 4))
                    split_hi(b, u, ("x",), first, last)
                if new:
                    silu(b, u, 0, first)
                if old:
                    split_h(b, u, 0, first)
                for tt in range(4 * u, 4 * u + 2) if blk_done else ():
                    tail.copy_T(act, b - 1, tt)
                if new:
                    silu(b, u, 1, first)
                if old:
                    split_h(b, u, 1, first)
                for tt in range(4 * u + 2, 4 * u + 4) if blk_done else ():
                    tail.copy_T(act, b - 1, tt)
                if new:
                    magnitude(b, u, 0, first)
                    magnitude(b, u, 1, first)
                    if u:
                        act.wait_ge(gu_psum, count(b, u, 4))
                    split_hi(b, u, ("gate", "up") if u == 0 else ("gate", "up", "x"), first, last)
                    silu(b, u, 2, first)
                    magnitude(b, u, 2, first)
                    if u % NB == 0:
                        if old:
                            act.wait_ge(d_psum, count(b, u, 4))
                        split_hi(b, u, ("down",), first, last)
                    silu(b, u, 3, first)
                    magnitude(b, u, 3, first)

            each_step(act, step)

        @block.vector
        def _(dve):
            def mul(b, u, j, first):
                if j == 0 and is_at(2, b, u, first):
                    dve.wait_ge(h_lo_done, count(b, u - 1, 2))
                dve.wait_ge(silu_done, count(b, u, 4, j + 1))
                dve.tensor_tensor(h[u % 2][:, j, :], sg[:, j, :], GU[j % 2][1][:, :], ALU.mult).then_inc(h_done, 1)

            def add(b, u, first):
                blk = (u - 1) % NB
                for t in range(4):
                    tt = blk * 4 + t
                    if u == 1 or u == 2:
                        dve.wait_ge(y_in[blk], b * 16 + 16)
                    else:
                        dve.wait_ge(sum_done, count(b, u - 1 - NB, 4, t + 1))
                    dve.wait_ge(d_psum, count(b, u - 1, 4, t + 1))
                    dve.tensor_tensor(y[:, tt, :], D[t][:, :], y[:, tt, :], ALU.add).then_inc(sum_done, 1)
                    if u == NU - 1 or u == 0:
                        dve.wait_ge(sum_done, count(b, u - 1, 4, t + 1))
                        tail.stats_of(dve, b if u else b - 1, tt)

            def compare(b, u, i, j, at, slot):
                dve.wait_ge(mag_done, count(b, u, 4, j + 1))
                dve.tensor_tensor(cmp[:, slot, at], mag[:, i, at], mag[:, j, at], ALU.is_ge).then_inc(cmp_done, 1)

            def choose(b, u, half):
                at, hu = HALF[half], h[u % 2]
                compare(b, u, 0, 3, at, 4)
                compare(b, u, 1, 3, at, 3)
                compare(b, u, 2, 3, at, 1)
                dve.wait_ge(cmp_done, count(b, u, NCMP, 3 + 3 * (half + 1)))
                dve.tensor_tensor(pair[:, 0:2, at], cmp[:, 2:4, at], cmp[:, 4:6, at], ALU.add).then_inc(pair_done, 1)
                dve.tensor_tensor(pair[:, 2:4, at], cmp[:, 2:5:2, at], cmp[:, 5:2:-2, at], ALU.add).then_inc(pair_done, 1)
                dve.wait_ge(pair_done, count(b, u, 4, 2 * (half + 1)))
                dve.tensor_tensor(wins[:, 0, at], pair[:, 0, at], cmp[:, 0, at], ALU.add).then_inc(wins_done, 1)
                dve.tensor_tensor(wins[:, 1, at], pair[:, 1, at], cmp[:, 0, at], ALU.subtract).then_inc(wins_done, 1)
                dve.tensor_tensor(wins[:, 2, at], cmp[:, 1, at], pair[:, 2, at], ALU.subtract).then_inc(wins_done, 1)
                dve.tensor_tensor(wins[:, 3, at], cmp[:, 1, at], pair[:, 3, at], ALU.add).then_inc(wins_done, 1)
                dve.wait_ge(wins_done, count(b, u, 8, 4 * (half + 1)))
                for j, (op, bound) in enumerate(((ALU.is_ge, 2.0), (ALU.is_ge, 1.0), (ALU.is_ge, 0.0), (ALU.is_le, 1.0))):
                    dve.scalar_tensor_tensor(out=hu[:, j, at], in0=wins[:, j, at], scalar=bound, in1=hu[:, j, at],
                                             op0=op, op1=ALU.mult).then_inc(keep_done, 1)

            def split_lo(b, u, half):
                at, hu = HALF[half], h[u % 2]
                dve.wait_ge(h_hi_done, count(b, u, 2, half + 1))
                dve.tensor_tensor(h_parts[1][:, :, at], hu[:, :, at], h_parts[0][:, :, at].bitcast(F32),
                                  ALU.subtract).then_inc(h_lo_done, 1)

            def step(b, u, new, old, first, last):
                if old:
                    choose(b, u - 1, 0)
                if new:
                    mul(b, u, 0, first)
                if old:
                    choose(b, u - 1, 1)
                    split_lo(b, u - 1, 0)
                if new:
                    mul(b, u, 1, first)
                if old:
                    split_lo(b, u - 1, 1)
                if new:
                    mul(b, u, 2, first)
                    compare(b, u, 0, 1, slice(0, 512), 0)
                    compare(b, u, 0, 2, slice(0, 512), 2)
                    compare(b, u, 1, 2, slice(0, 512), 5)
                if old:
                    add(b, u, first)
                done = (b, range(4)) if u == NU - 1 else (b - 1, range(4, TT)) if u == 0 and not first else None
                for tt in done[1][:2] if done else ():
                    tail.norm(dve, done[0], tt)
                if new:
                    mul(b, u, 3, first)
                for tt in done[1][2:] if done else ():
                    tail.norm(dve, done[0], tt)

            each_step(dve, step)

        @block.tensor
        def _(pe):
            def gate_up_products(b, u, j, first, last):
                s, blk = (u // NB) % 2, u % NB
                if j >= 2:
                    pe.wait_ge(h_done, count(b, u, 4, j - 1))
                elif is_at(1, b, u, first):
                    pe.wait_ge(h_done, count(b, u - 1, 4, j + 3))
                for a, weights in enumerate((gate, up)):
                    if j == 0:
                        if first and u == 0:
                            pe.wait_ge(lo_done, 2 + a)
                        elif u == 0 and a == 0:
                            pe.wait_ge(lo_done, b * NP + len(FIRST_PARTS))
                        elif u == 1 and a == 0:
                            pe.wait_ge(lo_done, part_number(b, (0, "x", 1), last) + 1)
                        elif u % NB == 0 and u:
                            q = (u - 2 + a, ("gate", "up")[a], u // NB)
                            pe.wait_ge(lo_done, part_number(b, q, last) + 1)
                    for t, (i, d) in enumerate(TERMS):
                        for k in range(KT):
                            last_mm = pe.matmul(GU[j % 2][a][:, :], weights[s][i][:, k, j, :], xs[blk][d][:, k, :],
                                                start=(t == 0 and k == 0), stop=(t == 2 and k == KT - 1))
                last_mm.then_inc(gu_psum, 1)

            def down_products(b, u, first, last):
                if u % NB == 1:
                    pe.wait_ge(lo_done, part_number(b, (u - 1, "down", u // NB), last) + 1)
                for tt in range(4):
                    pe.wait_ge(h_lo_done, count(b, u - 1, 2, tt // 2 + 1))
                    if u < NB and not first:
                        pe.wait_ge(tail.xT_done, b * TT + (u * 4 - TT + tt + 1))
                    elif is_at(2, b, u, first):
                        pe.wait_ge(sum_done, count(b, u - 2, 4, tt + 1))
                    for t, (i, d) in enumerate(TERMS):
                        for j in range(4):
                            last_mm = pe.matmul(D[tt][:, :], h_parts[i][:, j, tt * P:(tt + 1) * P], down[d][:, j, :],
                                                start=(t == 0 and j == 0), stop=(t == 2 and j == 3))
                    last_mm.then_inc(d_psum, 1)

            def step(b, u, new, old, first, last):
                blk_done = u < NB and not first
                if new:
                    gate_up_products(b, u, 0, first, last)
                for tt in range(4 * u, 4 * u + 2) if blk_done else ():
                    tail.transpose(pe, b - 1, tt)
                if new:
                    gate_up_products(b, u, 1, first, last)
                for tt in range(4 * u + 2, 4 * u + 4) if blk_done else ():
                    tail.transpose(pe, b - 1, tt)
                if new:
                    gate_up_products(b, u, 2, first, last)
                if old:
                    down_products(b, u, first, last)
                if new:
                    gate_up_products(b, u, 3, first, last)

            each_step(pe, step)


def moe_phase(nc, c, xT_in, x_in, ew, rw, eb, rb, same_expert, earlier_chunk, chunk_of, out):
    NT, NC = T // P, P // NE
    R = NT // NC
    W = R * P
    EARLY = 3 * NT // 8
    EARLY_CHUNKS = EARLY // R + 1
    BITS = 30
    HALVES = [1 << n for n in range(W.bit_length() - 1)]
    ctx = ExitStack()
    with ctx:
        def sb(n, shape, dt=F32):
            return ctx.enter_context(nc.sbuf_tensor(f"m_{n}", shape, dt))

        def sem(n):
            return c.semaphore(f"m_{n}")

        raw = sb("raw", [P, NC, KT, W])
        z = sb("z", [P, NT, H])
        w, xs = [sb("w_hi", [P, KT, H], F32R), sb("w_lo", [P, KT, H], F32R)], [[sb(f"x_{n}{i}", [P, KT, W], F32R) for n in ("hi", "lo")] for i in (0, 1)]
        w_raw = z[:, NT - KT:NT, :]
        rw_sb, rb_sb, eb_sb = sb("rw", [P, KT, NE]), sb("rb", [P, NE]), sb("eb", [P, H])
        same_sb, earlier_sb, chunk_sb = sb("same", [P, P]), sb("earlier", [P, P]), sb("chunk", [P, NC])
        logits, e = sb("logits", [P, NT, NE]), sb("e", [P, NT, NE])
        row = sb("row", [P, 2, NT])
        probs = sb("probs", [P, R, NC, NE])
        ST = sb("ST", [P, W])
        junk, eq = sb("junk", [P, W]), sb("eq", [P, W])
        pre = [t[:, :, :].rearrange("p t e -> p (t e)") for t in (logits, e)]
        thr, cand, taken = sb("thr", [P, 1], I32), sb("cand", [P, 1], I32), sb("taken", [P, 1])
        bits = sb("bits", [P, BITS], I32)
        cnt, need = sb("cnt", [P, 3]), sb("need", [P, 2])
        gates = sb("gates", [P, NT])
        stats, mv = sb("stats", [P, NT, 6]), sb("mv", [P, NT, 2])
        vare, rstd = sb("vare", [P, NT]), sb("rstd", [P, NT])
        psL = [ctx.enter_context(nc.psum_tensor(f"m_psL{i}", [P, R, NE], F32)) for i in (0, 1)]
        psZ = [ctx.enter_context(nc.psum_tensor(f"m_psZ{i}", [P, H], F32)) for i in (0, 1)]
        psT = ctx.enter_context(nc.psum_tensor("m_psT", [P, W], F32))
        psC = ctx.enter_context(nc.psum_tensor("m_psC", [P, 4], F32))
        psG = ctx.enter_context(nc.psum_tensor("m_psG", [P, R, NC], F32))

        router_in, const_in, w_in, w_hi_done, w_lo_done = sem("router_in"), sem("const_in"), sem("w_in"), sem("w_hi_done"), sem("w_lo_done")
        raw_in = [sem(f"raw_in{i}") for i in range(NC)]
        l_psum, l_done = sem("l_psum"), sem("l_done")
        step = sem("softmax_step")
        exp_done, t_psum, st_done = sem("exp_done"), sem("t_psum"), sem("st_done")
        x_hi_done, z_psum = sem("x_hi_done"), sem("z_psum")
        x_lo_done = [sem("x_lo_dve"), sem("x_lo_pool")]
        z_done, z_copied, z_biased = sem("z_done"), sem("z_copied"), sem("z_biased")
        cand_done, cnt_done, cnt_psum, taken_done, thr_done = (sem(n) for n in ("cand_done", "cnt_done", "cnt_psum", "taken_done", "thr_done"))
        bits_done = sem("bits_done")
        tie_cnt, tie_psum, tie = sem("tie_cnt"), sem("tie_psum"), sem("tie_step")
        g_in, g_psum, g_done = sem("g_in"), sem("g_psum"), sem("g_done")
        y_sum_last = sem("y_sum_last")
        scaled, y_sum, y_stats, y_mv = sem("scaled"), sem("y_sum"), sem("y_stats"), sem("y_mv")
        y_vare, y_rstd, y_norm, stored = sem("y_vare"), sem("y_rstd"), sem("y_norm"), sem("stored")

        x_rows = x_in.rearrange("(c r p) n -> c p r n", c=NC, p=P)
        x_cols = xT_in.rearrange("(k p) (c s) -> c p k s", p=P, c=NC)
        out_rows = out.rearrange("(t p) n -> t p n", p=P)
        w_flat = [t[:, :, :].rearrange("p k n -> p (k n)") for t in w]
        w_raw_flat = w_raw.rearrange("p k n -> p (k n)")
        block = ctx.enter_context(nc.Block())

        def early_tiles(chunk):
            return range(chunk * EARLY // NC, (chunk + 1) * EARLY // NC)

        def lo_done(eng, chunk):
            if chunk < EARLY_CHUNKS:
                eng.wait_ge(x_lo_done[0], chunk + 1)
            else:
                eng.wait_ge(x_lo_done[1], chunk + 1 - EARLY_CHUNKS)

        def split_lo(eng, who, chunk):
            eng.wait_ge(x_hi_done, chunk + 1)
            hi, lo = xs[chunk % 2]
            eng.tensor_tensor(lo[:, :, :], raw[:, chunk, :, :], hi[:, :, :].bitcast(F32), ALU.subtract).then_inc(x_lo_done[who], 1)

        @block.sync
        def _(sp):
            def load_x(chunk):
                sp.dma_start(raw[:, chunk, :, :], x_cols[chunk]).then_inc(raw_in[chunk], 16)

            sp.dma_start(rw_sb[:, :, :], rw.rearrange("(k p) n -> p k n", p=P)).then_inc(router_in, 16)
            load_x(0)
            sp.dma_start(rb_sb[:, :], rb.partition_broadcast(P)).then_inc(router_in, 16)
            sp.dma_start(w_raw, ew.rearrange("(k p) n -> p k n", p=P)).then_inc(w_in, 16)
            sp.dma_start(eb_sb[:, :], eb.partition_broadcast(P)).then_inc(const_in, 16)
            for chunk in range(1, NC):
                load_x(chunk)
            sp.dma_start(same_sb[:, :], same_expert).then_inc(const_in, 16)
            sp.dma_start(earlier_sb[:, :], earlier_chunk).then_inc(const_in, 16)
            sp.dma_start(chunk_sb[:, :], chunk_of).then_inc(const_in, 16)
            sp.wait_ge(l_psum, NC)
            for chunk in range(NC):
                lo_done(sp, chunk)
                sp.dma_start(raw[:, chunk, :, :], x_rows[chunk]).then_inc(raw_in[chunk], 16)
            for t in range(NT):
                sp.wait_ge(y_norm, t + 1)
                sp.dma_start(out_rows[t], z[:, t, :]).then_inc(stored, 16)
            sp.wait_ge(stored, NT * 16)

        @block.gpsimd
        def _(pool):
            def bias(t):
                pool.wait_ge(z_copied, t + 1 - EARLY)
                pool.tensor_tensor(z[:, t, :], z[:, t, :], eb_sb[:, :], ALU.add).then_inc(z_biased, 1)

            pool.wait_ge(const_in, 4 * 16)
            split_lo(pool, 1, EARLY_CHUNKS)
            for t in range(EARLY, NT):
                bias(t)
                if t % R == R - 1 and t // R + 2 < NC:
                    split_lo(pool, 1, t // R + 2)
            for q in range(NC + 1):
                if q < NC:
                    for t in range(q * R, (q + 1) * R):
                        if t == q * R:
                            pool.wait_ge(raw_in[q], 2 * 16)
                        if t % R < R - 1:
                            pool.wait_ge(scaled, t + 1)
                            pool.tensor_tensor(z[:, t, :], z[:, t, :], raw[:, q, t % R, :], ALU.add).then_inc(y_sum, 1)
                        if q and t % R == 1:
                            at = slice((q - 1) * R, q * R)
                            pool.wait_ge(y_vare, q)
                            pool.tensor_tensor(rstd[:, at], vare[:, at], c.neg_half[:, :].to_broadcast([P, R]), ALU.pow).then_inc(y_rstd, 1)
                else:
                    at = slice((q - 1) * R, q * R)
                    pool.wait_ge(y_vare, q)
                    pool.tensor_tensor(rstd[:, at], vare[:, at], c.neg_half[:, :].to_broadcast([P, R]), ALU.pow).then_inc(y_rstd, 1)

        @block.scalar
        def _(act):
            def split_hi(chunk):
                act.wait_ge(raw_in[chunk], 16)
                if chunk >= 2:
                    act.wait_ge(z_psum, (chunk - 1) * R)
                act.activation(xs[chunk % 2][0][:, :, :], raw[:, chunk, :, :], ACT.Copy).then_inc(x_hi_done, 1)

            split_hi(0)
            act.wait_ge(w_in, 16)
            act.activation(w_flat[0], w_raw_flat, ACT.Copy).then_inc(w_hi_done, 1)
            for chunk in range(1, EARLY_CHUNKS):
                split_hi(chunk)
            act.wait_ge(step, 2)
            act.activation(e[:, :, :], logits[:, :, :], ACT.Exp).then_inc(exp_done, 1)
            act.wait_ge(t_psum, 1)
            act.activation(ST[:, :], psT[:, :], ACT.Copy).then_inc(st_done, 1)
            split_hi(EARLY_CHUNKS)
            for t in range(EARLY, NT):
                act.wait_ge(z_psum, t + 1)
                if t == NT - KT:
                    act.wait_ge(w_lo_done, 1)
                act.activation(z[:, t, :], psZ[t % 2][:, :], ACT.Copy).then_inc(z_copied, 1)
                if t % R == R - 1 and t // R + 2 < NC:
                    split_hi(t // R + 2)
            act.wait_ge(g_done, 1)
            for t in range(NT):
                if t < EARLY:
                    act.wait_ge(z_done, t + 1)
                else:
                    act.wait_ge(z_biased, t + 1 - EARLY)
                act.activation(z[:, t, :], z[:, t, :], ACT.Copy, scale=gates[:, t:t + 1]).then_inc(scaled, 1)

        @block.vector
        def _(dve):
            dve.memset(thr[:, :], 0).then_inc(thr_done, 1)
            for i in range(BITS):
                dve.memset(bits[:, i:i + 1], 1 << (BITS - 1 - i)).then_inc(bits_done, 1)
            dve.wait_ge(router_in, 2 * 16)
            for chunk in range(NC + 1):
                if chunk < NC:
                    dve.wait_ge(l_psum, chunk + 1)
                    dve.tensor_tensor(logits[:, chunk * R:(chunk + 1) * R, :], psL[chunk % 2][:, :, :],
                                      rb_sb[:, :].unsqueeze(1).to_broadcast([P, R, NE]), ALU.add).then_inc(l_done, 1)
                if chunk == 0:
                    split_lo(dve, 0, 0)
                    dve.wait_ge(w_hi_done, 1)
                    dve.tensor_tensor(w_flat[1], w_raw_flat, w_flat[0].bitcast(F32), ALU.subtract).then_inc(w_lo_done, 1)
                if chunk == NC:
                    dve.wait_ge(l_done, NC)
                    dve.tensor_reduce(row[:, 0, :], logits[:, :, :], AX.X, ALU.max).then_inc(step, 1)
                    dve.wait_ge(step, 1)
                    dve.tensor_tensor(logits[:, :, :], logits[:, :, :], row[:, 0, :].unsqueeze(2).to_broadcast([P, NT, NE]),
                                      ALU.subtract).then_inc(step, 1)
                for t in early_tiles(chunk - 1) if chunk else ():
                    dve.wait_ge(z_psum, t + 1)
                    if t == 0:
                        dve.wait_ge(const_in, 4 * 16)
                    dve.tensor_tensor(z[:, t, :], psZ[t % 2][:, :], eb_sb[:, :], ALU.add).then_inc(z_done, 1)
                for n in range(1, EARLY_CHUNKS):
                    if (n - 1) * R - 1 in early_tiles(chunk - 1) or (n == 1 and chunk == 0):
                        split_lo(dve, 0, n)
            dve.wait_ge(exp_done, 1)
            dve.tensor_reduce(row[:, 1, :], e[:, :, :], AX.X, ALU.add).then_inc(step, 1)
            dve.wait_ge(step, 3)
            dve.reciprocal(row[:, 0, :], row[:, 1, :]).then_inc(step, 1)
            dve.wait_ge(step, 4)
            dve.tensor_tensor(probs[:, :, :, :].rearrange("p r c e -> p c r e"),
                              e[:, :, :].rearrange("p (c r) e -> p c r e", c=NC),
                              row[:, 0, :].rearrange("p (c r) -> p c r", c=NC).unsqueeze(3).to_broadcast([P, NC, R, NE]),
                              ALU.mult).then_inc(step, 1)
            dve.wait_ge(st_done, 1)
            dve.wait_ge(bits_done, BITS)
            for n in range(BITS):
                dve.wait_ge(thr_done, n + 1)
                dve.tensor_tensor(cand[:, :], thr[:, :], bits[:, n:n + 1], ALU.bitwise_or).then_inc(cand_done, 1)
                dve.wait_ge(cand_done, n + 1)
                dve.tensor_scalar(junk[:, :], ST[:, :], cand[:, :].bitcast(F32), None, ALU.is_ge, ALU.add,
                                  accum_out=cnt[:, 0:1]).then_inc(cnt_done, 1)
                dve.wait_ge(cnt_psum, n + 1)
                dve.scalar_tensor_tensor(out=taken[:, :], in0=psC[:, 0:1], scalar=TOPK - 0.5, in1=cand[:, :].bitcast(F32),
                                         op0=ALU.is_ge, op1=ALU.mult).then_inc(taken_done, 1)
                dve.wait_ge(taken_done, n + 1)
                dve.tensor_tensor(thr[:, :].bitcast(F32), thr[:, :].bitcast(F32), taken[:, :], ALU.max).then_inc(thr_done, 1)
            dve.wait_ge(thr_done, BITS + 1)
            t = thr[:, :].bitcast(F32)
            dve.tensor_scalar(junk[:, :], ST[:, :], t, None, ALU.is_gt, ALU.add, accum_out=cnt[:, 1:2]).then_inc(tie_cnt, 1)
            dve.tensor_scalar(eq[:, :], ST[:, :], t, None, ALU.is_equal, ALU.add, accum_out=cnt[:, 2:3]).then_inc(tie_cnt, 1)
            dve.wait_ge(tie_cnt, 2)
            src = eq
            for s, d in enumerate(HALVES):
                dst = pre[s % 2]
                dve.tensor_tensor(dst[:, d:W], src[:, d:W], src[:, 0:W - d], ALU.add).then_inc(tie, 1)
                dve.tensor_copy(dst[:, 0:d], src[:, 0:d]).then_inc(tie, 1)
                dve.wait_ge(tie, 2 * (s + 1))
                src = dst
            n = 2 * len(HALVES)
            dve.wait_ge(tie_psum, 1)
            dve.tensor_copy(need[:, 1:2], psC[:, 2:3]).then_inc(tie, 1)
            dve.wait_ge(tie, n + 1)
            dve.scalar_tensor_tensor(out=need[:, 0:1], in0=psC[:, 1:2], scalar=-1.0, in1=need[:, 1:2],
                                     op0=ALU.mult, op1=ALU.subtract).then_inc(tie, 1)
            dve.wait_ge(tie, n + 2)
            dve.tensor_scalar(need[:, 1:2], need[:, 0:1], float(TOPK), None, ALU.add).then_inc(tie, 1)
            dve.wait_ge(tie, n + 3)
            dve.scalar_tensor_tensor(out=eq[:, :], in0=src[:, :], scalar=need[:, 1:2], in1=eq[:, :],
                                     op0=ALU.is_le, op1=ALU.mult).then_inc(tie, 1)
            dve.wait_ge(tie, n + 4)
            dve.scalar_tensor_tensor(out=eq[:, :], in0=ST[:, :], scalar=t, in1=eq[:, :],
                                     op0=ALU.is_gt, op1=ALU.add).then_inc(tie, 1)
            dve.wait_ge(tie, n + 5)
            dve.tensor_tensor(junk[:, :], eq[:, :], ST[:, :], ALU.mult).then_inc(g_in, 1)
            dve.wait_ge(g_psum, 1)
            dve.tensor_copy(gates[:, :].rearrange("p (c r) -> p r c", c=NC), psG[:, :, :]).then_inc(g_done, 1)
            for q in range(NC + 1):
                if q < NC:
                    for t in range(q * R, (q + 1) * R):
                        if t % R < R - 1:
                            dve.wait_ge(y_sum, q * (R - 1) + t % R + 1)
                        else:
                            dve.wait_ge(scaled, t + 1)
                            dve.wait_ge(raw_in[q], 2 * 16)
                            dve.tensor_tensor(z[:, t, :], z[:, t, :], raw[:, q, t % R, :], ALU.add).then_inc(y_sum_last, 1)
                            dve.wait_ge(y_sum_last, q + 1)
                        dve.bn_stats(stats[:, t, :], z[:, t, :]).then_inc(y_stats, 1)
                        dve.wait_ge(y_stats, t + 1)
                        dve.bn_aggr(mv[:, t, :], stats[:, t, :]).then_inc(y_mv, 1)
                    dve.wait_ge(y_mv, (q + 1) * R)
                    dve.tensor_scalar(vare[:, q * R:(q + 1) * R], mv[:, q * R:(q + 1) * R, 1], EPS, None, ALU.add).then_inc(y_vare, 1)
                if q:
                    dve.wait_ge(y_rstd, q)
                    for t in range((q - 1) * R, q * R):
                        dve.tensor_scalar(z[:, t, :], z[:, t, :], mv[:, t, 0:1], rstd[:, t:t + 1],
                                          ALU.subtract, ALU.mult).then_inc(y_norm, 1)

        @block.tensor
        def _(pe):
            def z_products(t):
                lo_done(pe, t // R)
                if t < 2:
                    pe.wait_ge(w_lo_done, 1)
                elif t - 2 < EARLY:
                    pe.wait_ge(z_done, t - 1)
                else:
                    pe.wait_ge(z_copied, t - 1 - EARLY)
                for a, (i, d) in enumerate(TERMS):
                    for k in range(KT):
                        last = pe.matmul(psZ[t % 2][:, :], xs[t // R % 2][i][:, k, t % R * P:(t % R + 1) * P], w[d][:, k, :],
                                         start=(a == 0 and k == 0), stop=(a == 2 and k == KT - 1))
                        if a == 2 and k == KT - 1:
                            last.then_inc(z_psum, 1)
                        yield

            pe.wait_ge(router_in, 2 * 16)
            for chunk in range(NC):
                if chunk >= 2:
                    pe.wait_ge(l_done, chunk - 1)
                pe.wait_ge(raw_in[chunk], 16)
                for r in range(R):
                    for k in range(KT):
                        last = pe.matmul(psL[chunk % 2][:, r, :], raw[:, chunk, k, r * P:(r + 1) * P], rw_sb[:, k, :],
                                         start=(k == 0), stop=(k == KT - 1))
                last.then_inc(l_psum, 1)
                for t in early_tiles(chunk):
                    for _ in z_products(t):
                        pass
            pe.wait_ge(step, 5)
            for r in range(R):
                last = pe.transpose(psT[:, r * P:(r + 1) * P], probs[:, r, :, :].rearrange("p c e -> p (c e)"), c.ident[:, :])
            last.then_inc(t_psum, 1)
            pe.wait_ge(const_in, 4 * 16)
            late = (m for t in range(EARLY, NT) for m in z_products(t))
            share = -(-(NT - EARLY) * len(TERMS) * KT // BITS)
            for n in range(BITS):
                for _ in range(share):
                    next(late, None)
                pe.wait_ge(cnt_done, n + 1)
                pe.matmul(psC[:, 0:1], same_sb[:, :], cnt[:, 0:1], start=True, stop=True).then_inc(cnt_psum, 1)
            pe.wait_ge(tie_cnt, 2)
            pe.matmul(psC[:, 1:2], same_sb[:, :], cnt[:, 1:2], start=True, stop=True)
            pe.matmul(psC[:, 2:3], earlier_sb[:, :], cnt[:, 2:3], start=True, stop=True).then_inc(tie_psum, 1)
            pe.wait_ge(g_in, 1)
            for r in range(R):
                last = pe.matmul(psG[:, r, :], junk[:, r * P:(r + 1) * P], chunk_sb[:, :], start=True, stop=True)
            last.then_inc(g_psum, 1)


def build(nc, xT, x, wqkv0, wo0T, wg, wu, wd, wqkv1, bqkv1, cosT, sinT, rw, rb, ew, eb,
          same_expert, earlier_chunk, chunk_of, out, stages=4):
    def scratch(name, shape):
        return nc.dram_tensor(name, shape, F32, kind="Internal").ap()

    x1, x1T, x2, x2T, x3, x3T = (scratch(f"s_{n}", s) for n, s in
                                 (("x1", [T, H]), ("x1T", [H, T]), ("x2", [T, H]), ("x2T", [H, T]), ("x3", [T, H]), ("x3T", [H, T])))
    m_scratch = scratch("s_m", [HG * TT, P])
    with ExitStack() as ctx:
        c = Consts(nc, ctx)
        if stages == 1:
            x1 = out
        attention_phase(nc, c, "a0", xT, x, wqkv0, wo0T, None, None, m_scratch, x1, x1T)
        c.end_phase()
        if stages == 1:
            return
        ffn_phase(nc, c, x1T, x1, wg, wu, wd, out if stages == 2 else x2, x2T)
        c.end_phase()
        if stages == 2:
            return
        attention_phase(nc, c, "a1", x2T, x2, wqkv1, None, bqkv1, (cosT, sinT), m_scratch, out if stages == 3 else x3, x3T)
        c.end_phase()
        if stages == 3:
            return
        moe_phase(nc, c, x3T, x3, ew, rw, eb, rb, same_expert, earlier_chunk, chunk_of, out)


def kernel(**inputs):
    import numpy as np
    import concourse.bacc as bacc
    from concourse.bass_utils import run_bass_kernel_spmd

    arrays, order = layout(inputs, np)
    nc = bacc.Bacc("TRN2", target_bir_lowering=False, num_devices=1)
    args = [nc.dram_tensor(f"in_{n}", arrays[n].shape, mybir.dt.from_np(arrays[n].dtype), kind="ExternalInput").ap() for n in order]
    out = nc.dram_tensor("out_y", (T, H), F32, kind="ExternalOutput").ap()
    build(nc, *args, out)
    r = run_bass_kernel_spmd(nc, [{f"in_{n}": arrays[n] for n in order}], core_ids=[0])
    return r.results[0]["out_y"].reshape(B, S, H)


def layout(inputs, np):
    a = {k: np.asarray(v) for k, v in inputs.items()}
    x = a["L0_attn_hidden_states"].reshape(T, H)
    inv_freq = (1.0 / np.float32(10000.0) ** (np.arange(0, HD, 2, dtype=np.float32) / np.float32(HD))).astype(np.float32)
    freqs = np.outer(np.arange(S, dtype=np.float32), inv_freq).astype(np.float32).T
    cos, sin = np.cos(freqs), np.sin(freqs)
    chunk, expert = np.arange(P) // NE, np.arange(P) % NE
    place = np.arange(P)
    within, head = place // HG, place % HG
    feature = within % 8 % 4 + within // 8 * 4 + within % 8 // 4 * (HD // 2)
    qk_order = head * HD + feature

    def qkv(w):
        w = w.T.reshape(KT, P, 3, G, P).transpose(3, 1, 0, 2, 4)
        return np.ascontiguousarray(np.stack([w[:, :, :, 0][..., qk_order], w[:, :, :, 1][..., qk_order], w[:, :, :, 2]], axis=3))

    b1 = a["L1_attn_Wqkv_b"].reshape(3, G, P)
    b1 = np.stack([b1[0][:, qk_order], b1[1][:, qk_order], b1[2]])
    arrays = {
        "xT": np.ascontiguousarray(x.T),
        "x": x,
        "wqkv0": qkv(a["L0_attn_w_qkv"]),
        "wo0T": np.ascontiguousarray(a["L0_attn_w_o"].T),
        "wg": np.ascontiguousarray(a["L0_ffn_w_gate"].reshape(KT, P, 4, P, 4).transpose(2, 1, 0, 4, 3)),
        "wu": np.ascontiguousarray(a["L0_ffn_w_up"].reshape(KT, P, 4, P, 4).transpose(2, 1, 0, 4, 3)),
        "wd": a["L0_ffn_w_down"].reshape(4, P, 4, H),
        "wqkv1": qkv(a["L1_attn_Wqkv_w"]),
        "bqkv1": np.ascontiguousarray(b1.reshape(3 * G, P).T),
        "cosT": np.ascontiguousarray(np.concatenate([cos, cos])[feature]),
        "sinT": np.ascontiguousarray(np.concatenate([-sin, sin])[feature]),
        "rw": a["L1_ffn_router_w"],
        "rb": a["L1_ffn_router_b"],
        "ew": a["L1_ffn_expert_w"],
        "eb": a["L1_ffn_expert_b"],
        "same_expert": (expert[:, None] == expert[None, :]).astype(np.float32),
        "earlier_chunk": ((expert[:, None] == expert[None, :]) & (chunk[:, None] < chunk[None, :])).astype(np.float32),
        "chunk_of": (chunk[:, None] == np.arange(P // NE)[None, :]).astype(np.float32),
    }
    return arrays, list(arrays)
```
